# Optimizing a Trainium2 kernel written in Bass

```python
import numpy as np
import jax
import jax.numpy as jnp

def _softmax(x, axis=-1):
    return jax.nn.softmax(x, axis=axis)

def _gelu(x):
    return jax.nn.gelu(x, approximate=True)

def _silu(x):
    return jax.nn.silu(x)

def _sigmoid(x):
    return jax.nn.sigmoid(x)

def _layernorm(x, axis=-1, eps=1e-05):
    m = jnp.mean(x, axis=axis, keepdims=True)
    v = jnp.var(x, axis=axis, keepdims=True)
    return (x - m) / jnp.sqrt(v + eps)

def _scatter_add(tgt, idx, src, axis=0):
    return tgt.at[idx].add(src)

def _segment_sum(src, seg, n):
    return jax.ops.segment_sum(src, seg, n)
kernel_name = 'mk_adj_ffn_d1_adj_r2_5b52dc'

def setup_inputs(seed: int=0):
    np.random.seed(seed)
    _w = jnp.asarray

    def _rec_inputs():
        import jax
        import jax.numpy as jnp
        _gk = jax.random.key(seed)
        x = -0.0002928 + 1 * jax.random.normal(jax.random.fold_in(_gk, 1), (64, 128, 128), jnp.float32)
        _a = jax.random.bernoulli(jax.random.fold_in(_gk, 2), 0.015625, (128, 128))
        _a = jnp.logical_or(_a, jnp.eye(128, dtype=bool))
        adj = _a.astype(jnp.int32)
        return (x, adj)
    x, adj = _rec_inputs()

    def _L0_gnn_setup():
        import jax, jax.numpy as jnp
        import numpy as np
        IN_F = 128
        OUT_F = 128
        N_HEADS = 4
        HEAD_DIM = OUT_F // N_HEADS
        B, N = (8, 1024)
        LN_EPS = 1e-05
        key = jax.random.key(seed)
        ks = jax.random.split(key, 12)
        x = jax.random.normal(ks[0], (B, N, IN_F), dtype=jnp.float32)
        adj = jax.random.randint(ks[1], (N, N), 0, 2, dtype=jnp.int32)
        adj = adj.at[jnp.arange(N), jnp.arange(N)].set(1)
        s = 0.02
        Wq = jax.random.normal(ks[2], (IN_F, OUT_F), jnp.float32) * s
        bq = jnp.zeros((OUT_F,), jnp.float32)
        Wk = jax.random.normal(ks[3], (IN_F, OUT_F), jnp.float32) * s
        bk = jnp.zeros((OUT_F,), jnp.float32)
        Wv = jax.random.normal(ks[4], (IN_F, OUT_F), jnp.float32) * s
        bv = jnp.zeros((OUT_F,), jnp.float32)
        Wo = jax.random.normal(ks[5], (OUT_F, OUT_F), jnp.float32) * s
        bo = jnp.zeros((OUT_F,), jnp.float32)
        gamma = jnp.ones((OUT_F,), jnp.float32)
        beta = jnp.zeros((OUT_F,), jnp.float32)
        return {'x': x, 'adj': adj, 'Wq': Wq, 'bq': bq, 'Wk': Wk, 'bk': bk, 'Wv': Wv, 'bv': bv, 'Wo': Wo, 'bo': bo, 'gamma': gamma, 'beta': beta}
    _L0_gnn_all = _L0_gnn_setup()
    _L0_gnn_in = {k: v for k, v in _L0_gnn_all.items() if k in ('Wq', 'bq', 'Wk', 'bk', 'Wv', 'bv', 'Wo', 'bo', 'gamma', 'beta')}
    del _L0_gnn_all

    def _L0_ffn_setup():
        import jax, jax.numpy as jnp
        import numpy as np
        B, S, D, F, E, K = (8, 1024, 128, 512, 8, 2)
        key = jax.random.key(seed)
        ks = jax.random.split(key, 10)
        s = 0.02
        return {'x': jax.random.normal(ks[0], (B, S, D), dtype=jnp.float32), 'Wr': jax.random.normal(ks[1], (D, E), dtype=jnp.float32) * s, 'W1s': jax.random.normal(ks[2], (D, F), dtype=jnp.float32) * s, 'b1s': jnp.zeros((F,), dtype=jnp.float32), 'W2s': jax.random.normal(ks[3], (F, D), dtype=jnp.float32) * s, 'b2s': jnp.zeros((D,), dtype=jnp.float32), 'W1p': jax.random.normal(ks[4], (E, D, F), dtype=jnp.float32) * s, 'b1p': jnp.zeros((E, F), dtype=jnp.float32), 'W2p': jax.random.normal(ks[5], (E, F, D), dtype=jnp.float32) * s, 'b2p': jnp.zeros((E, D), dtype=jnp.float32)}
    _L0_ffn_all = _L0_ffn_setup()
    _L0_ffn_in = {k: v for k, v in _L0_ffn_all.items() if k in ('Wr', 'W1s', 'b1s', 'W2s', 'b2s', 'W1p', 'b1p', 'W2p', 'b2p')}
    del _L0_ffn_all
    return {'x': x, 'adj': adj, 'L0_gnn_Wq': _L0_gnn_in['Wq'], 'L0_gnn_bq': _L0_gnn_in['bq'], 'L0_gnn_Wk': _L0_gnn_in['Wk'], 'L0_gnn_bk': _L0_gnn_in['bk'], 'L0_gnn_Wv': _L0_gnn_in['Wv'], 'L0_gnn_bv': _L0_gnn_in['bv'], 'L0_gnn_Wo': _L0_gnn_in['Wo'], 'L0_gnn_bo': _L0_gnn_in['bo'], 'L0_gnn_gamma': _L0_gnn_in['gamma'], 'L0_gnn_beta': _L0_gnn_in['beta'], 'L0_ffn_Wr': _L0_ffn_in['Wr'], 'L0_ffn_W1s': _L0_ffn_in['W1s'], 'L0_ffn_b1s': _L0_ffn_in['b1s'], 'L0_ffn_W2s': _L0_ffn_in['W2s'], 'L0_ffn_b2s': _L0_ffn_in['b2s'], 'L0_ffn_W1p': _L0_ffn_in['W1p'], 'L0_ffn_b1p': _L0_ffn_in['b1p'], 'L0_ffn_W2p': _L0_ffn_in['W2p'], 'L0_ffn_b2p': _L0_ffn_in['b2p']}

def reference(x, adj, L0_gnn_Wq, L0_gnn_bq, L0_gnn_Wk, L0_gnn_bk, L0_gnn_Wv, L0_gnn_bv, L0_gnn_Wo, L0_gnn_bo, L0_gnn_gamma, L0_gnn_beta, L0_ffn_Wr, L0_ffn_W1s, L0_ffn_b1s, L0_ffn_W2s, L0_ffn_b2s, L0_ffn_W1p, L0_ffn_b1p, L0_ffn_W2p, L0_ffn_b2p):
    import jax
    import jax.numpy as jnp

    def _L0_gnn_ref(x, adj, Wq, bq, Wk, bk, Wv, bv, Wo, bo, gamma, beta):
        import jax, jax.numpy as jnp
        import numpy as np
        IN_F = 128
        OUT_F = 128
        N_HEADS = 4
        HEAD_DIM = OUT_F // N_HEADS
        B, N = (8, 1024)
        LN_EPS = 1e-05
        b, n, _ = x.shape
        Q = (x @ Wq + bq).reshape(b, n, N_HEADS, HEAD_DIM)
        K = (x @ Wk + bk).reshape(b, n, N_HEADS, HEAD_DIM)
        V = (x @ Wv + bv).reshape(b, n, N_HEADS, HEAD_DIM)
        scale = 1.0 / np.sqrt(HEAD_DIM).astype(np.float32)
        scores = jnp.einsum('bnhd,bmhd->bhnm', Q, K) * scale
        mask = (adj == 0)[None, None, :, :]
        scores = jnp.where(mask, -jnp.inf, scores)
        attn = jax.nn.softmax(scores, axis=-1)
        out = jnp.einsum('bhnm,bmhd->bnhd', attn, V).reshape(b, n, OUT_F)
        out = out @ Wo + bo
        mu = jnp.mean(out, axis=-1, keepdims=True)
        var = jnp.mean(jnp.square(out - mu), axis=-1, keepdims=True)
        out = (out - mu) / jnp.sqrt(var + LN_EPS) * gamma + beta
        return out

    def _L0_ffn_ref(x, Wr, W1s, b1s, W2s, b2s, W1p, b1p, W2p, b2p):
        import jax, jax.numpy as jnp
        import numpy as np
        B, S, D, F, E, K = (8, 1024, 128, 512, 8, 2)
        gelu = lambda t: jax.nn.gelu(t, approximate=False)
        shared = gelu(x @ W1s + b1s) @ W2s + b2s
        rw = jax.nn.softmax(x @ Wr, axis=-1)
        topw, topi = jax.lax.top_k(rw, K)
        topw = topw / jnp.sum(topw, axis=-1, keepdims=True)
        mask = jnp.sum(jax.nn.one_hot(topi, E, dtype=topw.dtype) * topw[..., None], axis=-2)
        h = gelu(jnp.einsum('bsd,edf->bsef', x, W1p) + b1p)
        priv = jnp.einsum('bsef,efd->bsed', h, W2p) + b2p
        routed = jnp.einsum('bsed,bse->bsd', priv, mask)
        return shared + routed
    x = x + _L0_gnn_ref(_layernorm(x, axis=-1), adj, L0_gnn_Wq, L0_gnn_bq, L0_gnn_Wk, L0_gnn_bk, L0_gnn_Wv, L0_gnn_bv, L0_gnn_Wo, L0_gnn_bo, L0_gnn_gamma, L0_gnn_beta)
    x = x + _L0_ffn_ref(_layernorm(x, axis=-1), L0_ffn_Wr, L0_ffn_W1s, L0_ffn_b1s, L0_ffn_W2s, L0_ffn_b2s, L0_ffn_W1p, L0_ffn_b1p, L0_ffn_W2p, L0_ffn_b2p)
    return x

_drawn_inputs = setup_inputs


def setup_inputs(seed=0):
    import zlib

    import numpy as np

    out = dict(_drawn_inputs(seed))
    spreads = {'L0_gnn_bq': (0.0, 0.8),
     'L0_gnn_bk': (0.0, 0.8),
     'L0_gnn_bv': (0.0, 0.1),
     'L0_gnn_bo': (0.0, 0.1),
     'L0_gnn_gamma': (1.0, 0.2),
     'L0_gnn_beta': (0.0, 0.1),
     'L0_ffn_b1s': (0.0, 0.478),
     'L0_ffn_b2s': (0.0, 0.1),
     'L0_ffn_b1p': (0.0, 0.621),
     'L0_ffn_b2p': (0.0, 0.1)}
    factors = {'L0_gnn_Wq': 6.221, 'L0_gnn_Wk': 5.758}
    for name, (base, spread) in spreads.items():
        noise = np.random.default_rng([zlib.crc32(name.encode()), seed]).standard_normal(out[name].shape)
        drawn = base * np.exp(spread * noise) if base else spread * noise
        out[name] = jnp.asarray(drawn.astype(out[name].dtype))
    for name, factor in factors.items():
        out[name] = (out[name] * factor).astype(out[name].dtype)
    return out
```

```python
from contextlib import ExitStack

import concourse.bass as bass
from concourse import mybir

F32 = mybir.dt.float32
BF16 = mybir.dt.bfloat16
I32 = mybir.dt.int32
U32 = mybir.dt.uint32
ALU = mybir.AluOpType
ACT = mybir.ActivationFunctionType
AX_X = mybir.AxisListType.X

P = 128
EPS = 1e-5
MASKED = -1e30
NOWHERE = 1 << 20


def build_program(nc, x, adj, Wq, bq, Wk, bk, Wv, bv, Wo, bo, gamma, beta,
                  Wr, W1s, b1s, W2s, b2s, W1p, b1p, W2p, b2p, out):
    B = x.shape[0]
    HEADS = 4
    HD = P // HEADS
    E = Wr.shape[1]
    F = W1s.shape[1]
    FC = F // P
    TG = 4
    GROUPS = B // TG
    TOKENS = B * P
    W = TG * P
    ST = 2 * P
    REGION = TOKENS + ST
    TILES = 2 * TOKENS // ST + E
    IDLE_ROW = E * REGION
    SHARED_TILES = TOKENS // ST
    RW = 2 * P + 2
    SCALE = float(HD) ** -0.5
    assert GROUPS % 2 == 0 and TILES % 4 == 0

    slots = nc.dram_tensor("slots", [E * REGION + ST, RW], BF16).ap()
    pairs = nc.dram_tensor("pairs", [2 * TOKENS, P], F32).ap()

    with ExitStack() as ctx:
        def sb(name, shape, dt=F32):
            return ctx.enter_context(nc.sbuf_tensor(name, shape, dt))

        def sem(name):
            return ctx.enter_context(nc.semaphore(name))

        ident = sb("ident", [P, P])
        ident_h = sb("ident_h", [P, P], BF16)
        before = sb("before", [P, P], BF16)
        ones_h = sb("ones_h", [P, P], BF16)
        adj_i = sb("adj_i", [P, P], I32)
        mask_h = sb("mask_h", [P, P], BF16)
        w_q, w_k, w_v, w_o = sb("w_q", [P, P]), sb("w_k", [P, P]), sb("w_v", [P, P]), sb("w_o", [P, P])
        w_r = sb("w_r", [P, E])
        NB = (E + 1) * FC
        bias_rows = sb("bias_rows", [NB + 3, P])
        bias_cols = sb("bias_cols", [P, NB + 3])
        bq_scaled = sb("bq_scaled", [P, 1])
        bv_wide = sb("bv_wide", [P, P])
        bo_row, gamma_row, beta_row = sb("bo_row", [P, P]), sb("gamma_row", [P, P]), sb("beta_row", [P, P])
        b2s_row = sb("b2s_row", [P, P])
        b2_rows = sb("b2_rows", [P, E, P])
        c_row = sb("c_row", [P, P])
        minus_half = sb("minus_half", [P, TG])
        rank_i = sb("rank_i", [P, E], I32)
        rank = sb("rank", [P, E])
        base_i = sb("base_i", [P, E], I32)
        region_start = sb("region_start", [P, E])
        ids = sb("ids", [P, B], U32)
        pad_rows = sb("pad_rows", [P, 2, RW], BF16)

        x_all = sb("x_all", [P, B, P])
        xh_all = sb("xh_all", [P, TOKENS], BF16)
        xl_all = sb("xl_all", [P, TOKENS], BF16)
        w1 = sb("w1", [P, (E + 1) * FC * 2, P], BF16)
        w2 = sb("w2", [P, (E + 1) * FC * 2, P], BF16)
        delta = sb("delta", [P, B])
        weight1, weight2 = sb("weight1", [P, B]), sb("weight2", [P, B])
        base = sb("base", [P, 2, E])

        w_stage = sb("w_stage", [P, 2, F])
        stats = sb("stats", [P, 3, TG, 6])
        meanvar = sb("meanvar", [P, 3, TG, 2])
        var_eps = sb("var_eps", [P, 3, TG])
        rstd = sb("rstd", [P, 3, TG])
        xn = sb("xn", [P, W])
        xnT = sb("xnT", [P, W])
        qT = sb("qT", [P, 2, W])
        kT = sb("kT", [P, 2, W])
        k_wide = sb("k_wide", [P, 2, TG, HEADS, P])
        v1 = sb("v1", [P, 2, TG, HEADS, HD + 1])
        neg_max = sb("neg_max", [P, 2, HEADS])
        probs = sb("probs", [P, 2, HEADS, P])
        probsT = sb("probsT", [P, 2, HEADS * P])
        inv_sum = sb("inv_sum", [P, 2, HEADS])
        attn = sb("attn", [P, 2, TG, P])
        attnT = sb("attnT", [P, W])
        proj = sb("proj", [P, TG, P])
        scaled = sb("scaled", [P, TG, P])
        x2n = sb("x2n", [P, TG, P])
        x2T = sb("x2T", [P, W])
        rows = sb("rows", [P, 2, TG, RW], BF16)
        row_ids = rows[:, :, :, :].bitcast(U32)
        logits = sb("logits", [P, TG, E])
        top1, top2 = sb("top1", [P, TG]), sb("top2", [P, TG])
        first = sb("first", [P, 2, TG])
        hit = sb("hit", [P, 2, TG, E])
        hot1, hot2 = sb("hot1", [P, TG, E]), sb("hot2", [P, TG, E])
        rest = sb("rest", [P, TG, E])
        chosen = sb("chosen", [P, TG, E], BF16)
        place = sb("place", [P, TG, E])
        placed = sb("placed", [P, 2, TG, E])
        slot_f = sb("slot_f", [P, 2, TG])
        slot = sb("slot", [P, 2, 2, TG], U32)

        J = TILES
        count = sb("count", [P, E])
        ntile_i = sb("ntile_i", [P, E], I32)
        ntile = sb("ntile", [P, E])
        tri = sb("tri", [P, E, E])
        tmp88 = sb("tmp88", [P, E, E])
        upto = sb("upto", [P, E])
        jump = sb("jump", [P, E])
        j_i = sb("j_i", [P, J], I32)
        j_f = sb("j_f", [P, J])
        past = sb("past", [P, J, E])
        jumps = sb("jumps", [P, J, E])
        e_f, r_f, r_g = sb("e_f", [P, J]), sb("r_f", [P, J]), sb("r_g", [P, J])
        tile_expert = sb("tile_expert", [P, J], I32)
        tile_row = sb("tile_row", [P, J], I32)
        end_i = sb("end_i", [P, E], I32)

        xg = sb("xg", [P, 2, 2, RW], BF16)
        xg_ids = xg[:, :, :, :].bitcast(U32)
        home = sb("home", [P, 4, 2], U32)
        xgT = sb("xgT", [P, 2, 2, ST], BF16)
        over = k_wide[:, :, :, :, :].rearrange("p q t h m -> p (q t h m)")
        NH = 2 * FC * ST
        hid = over[:, 0:NH].rearrange("p (q c n) -> p q c n", q=2, c=FC)
        hid_h = over[:, NH:NH * 3 // 2].bitcast(BF16).rearrange("p (q c n) -> p q c n", q=2, c=FC)
        hid_l = over[:, NH * 3 // 2:2 * NH].bitcast(BF16).rearrange("p (q c n) -> p q c n", q=2, c=FC)
        y = sb("y", [P, 2, 2, P])
        x1b = sb("x1b", [P, 2, 2, P])
        yg = sb("yg", [P, 2, 2, 2 * P])
        acc = sb("acc", [P, 2, 2, P])
        acc2 = sb("acc2", [P, 2, 2, P])
        res = sb("res", [P, 2, 2, P])

        bank = [ctx.enter_context(nc.psum_tensor(f"bank{n}", [P, 512], F32)) for n in range(4)]
        wide = ctx.enter_context(nc.psum_tensor("wide", [P, 4, 512], F32))
        ps_s = wide[:, 0:2, :].rearrange("p q (h m) -> p q h m", h=HEADS)
        ps_av = wide[:, 2:4, 0:HEADS * (HD + 1)].rearrange("p q (h d) -> p q h d", h=HEADS)
        ps_pT, ps_o, ps_m, ps_n = bank
        ps_logit = ps_o[:, 0:TG * E].rearrange("p (t e) -> p t e", t=TG)
        ps_before = ps_o[:, 64:64 + TG * E].rearrange("p (t e) -> p t e", t=TG)
        ps_total = ps_o[:, 128:128 + E]
        ps_h = wide[:, :, :].rearrange("p b n -> p (b n)").rearrange("p (q c n) -> p q c n", q=2, c=FC)
        ps_y = [bank[0][:, 0:ST].rearrange("p (a d) -> p a d", a=2), bank[1][:, 0:ST].rearrange("p (a d) -> p a d", a=2)]
        ps_xT = [bank[2][:, 0:ST].bitcast(BF16).rearrange("p (h n) -> p h n", h=2),
                 bank[3][:, 0:ST].bitcast(BF16).rearrange("p (h n) -> p h n", h=2)]

        s_apart = sem("s_apart")
        s_c = sem("s_c")
        s_x = [sem("s_xin0"), sem("s_xin1")]
        s_kz = [sem("s_kz0"), sem("s_kz1")]
        s_w = sem("s_w")
        s_pool_c = sem("s_pool_c")
        s_cast_c = sem("s_cast_c")
        s_pe_c = sem("s_pe_c")
        s_act_c = sem("s_act_c")
        s_crow = sem("s_crow")
        s_ln = sem("s_ln")
        s_var = [sem(f"s_var{n}") for n in range(3)]
        s_pl = sem("s_pl")
        s_rstd = [sem(f"s_rstd{n}") for n in range(3)]
        s_xn = sem("s_xn")
        s_xT = sem("s_xT")
        s_xTc = sem("s_xTc")
        s_q, s_k, s_v = sem("s_q"), sem("s_k"), sem("s_v")
        s_qc, s_kc, s_vc = sem("s_qc"), sem("s_kc"), sem("s_vc")
        s_score, s_max, s_exp = sem("s_score"), sem("s_max"), sem("s_exp")
        s_pT, s_pTc, s_av, s_inv, s_attn = sem("s_pT"), sem("s_pTc"), sem("s_av"), sem("s_inv"), sem("s_attn")
        s_oT, s_oTc, s_proj, s_projc, s_scaled, s_x1 = (sem("s_oT"), sem("s_oTc"), sem("s_proj"), sem("s_projc"),
                                                        sem("s_scaled"), sem("s_x1"))
        s_xbeta = sem("s_xbeta")
        s_x2n, s_rowh, s_rowl = sem("s_x2n"), sem("s_rowh"), sem("s_rowl")
        s_x2T, s_x2Tc, s_xh, s_xl = sem("s_x2T"), sem("s_x2Tc"), sem("s_xh"), sem("s_xl")
        s_logit, s_route, s_chosen, s_before, s_place, s_slot = (sem("s_logit"), sem("s_route"), sem("s_chosen"),
                                                                 sem("s_before"), sem("s_place"), sem("s_slot"))
        s_id = sem("s_id")
        s_sent = [sem("s_sent0"), sem("s_sent1")]
        s_wh, s_wl = sem("s_wh"), sem("s_wl")
        s_list = sem("s_list")
        s_pad = sem("s_pad")
        s_soft, s_wt = sem("s_soft"), sem("s_wt")
        s_xg = [sem("s_xg0"), sem("s_xg1")]
        s_gT, s_gTc, s_h, s_hid, s_hh, s_hl, s_y, s_yc = (sem("s_gT"), sem("s_gTc"), sem("s_h"), sem("s_hid"),
                                                          sem("s_hh"), sem("s_hl"), sem("s_y"), sem("s_yc"))
        s_home = sem("s_home")
        s_back = [sem("s_back0"), sem("s_back1")]
        s_yg = [sem("s_yg0"), sem("s_yg1")]
        s_x1b, s_acc, s_res = sem("s_x1b"), sem("s_acc"), sem("s_res")
        s_out = [sem("s_out0"), sem("s_out1")]

        UNITS = 2 * (E + 1)
        STAGES = 5
        STEPS = GROUPS + STAGES - 1
        LOOP_FROM = 6
        LOOP_TO = GROUPS - 2

        def steps(eng, step):
            def plain(s):
                step(s, lambda k: (s + k) // 2, s % 2)

            for s in range(LOOP_FROM):
                plain(s)
            with eng.Fori(0, (LOOP_TO - LOOP_FROM) // 2) as i:
                for u in range(2):
                    s = LOOP_FROM + u
                    step(i * 2 + s, lambda k: i + (s + k) // 2, s % 2)
            for s in range(LOOP_TO, STEPS):
                plain(s)

        def active(s, stage):
            return not isinstance(s, int) or 0 <= s - stage < GROUPS

        def after_first(g):
            return not isinstance(g, int) or g > 0

        def apart(eng):
            eng.sem_inc(s_apart, 1)

        def later(g, n):
            return not isinstance(g, int) or g >= n

        def unit_source(u, half, par):
            if isinstance(u, int) and u < 2:
                return W1s if par == 0 else W2s.rearrange("(c p) d -> p c d", p=P)
            e = half(0) - 1
            if par == 0:
                return W1p[bass.ds(e, 1), :, :].rearrange("e d f -> d (e f)")
            return W2p[bass.ds(e, 1), :, :].rearrange("e (c p) d -> p (e c) d", p=P)

        def unit_block(u, half):
            return E * FC * 2 if isinstance(u, int) and u < 2 else (half(0) - 1) * (FC * 2)

        block = ctx.enter_context(nc.Block())

        @block.sync
        def _(sp):
            for dst, src in ((w_q, Wq), (w_k, Wk), (w_v, Wv), (w_o, Wo), (w_r, Wr), (adj_i, adj)):
                sp.dma_start(dst[:, :], src).then_inc(s_c, 16)
            for dst, src in ((bo_row, bo), (gamma_row, gamma), (beta_row, beta), (b2s_row, b2s)):
                sp.dma_start(dst[:, :], src.rearrange("(a d) -> a d", a=1).broadcast_to([P, P])).then_inc(s_c, 16)
            sp.dma_start(b2_rows[:, :, :].rearrange("p e d -> p (e d)"),
                         b2p.rearrange("(a e) d -> a (e d)", a=1).broadcast_to([P, E * P])).then_inc(s_c, 16)
            sp.dma_start(bias_rows[0:E * FC, :], b1p.rearrange("e (c p) -> (e c) p", p=P)).then_inc(s_c, 16)
            sp.dma_start(bias_rows[E * FC:NB, :], b1s.rearrange("(c p) -> c p", p=P)).then_inc(s_c, 16)
            sp.dma_start(bias_rows[NB:NB + 1, :], bq.rearrange("(a p) -> a p", a=1)).then_inc(s_c, 16)
            sp.dma_start(bias_rows[NB + 1:NB + 2, :], bk.rearrange("(a p) -> a p", a=1)).then_inc(s_c, 16)
            sp.dma_start(bias_rows[NB + 2:NB + 3, :], bv.rearrange("(a p) -> a p", a=1)).then_inc(s_c, 16)

            def load_x(g, par):
                sp.dma_start(x_all[:, bass.ds(g * TG, TG), :],
                             x[bass.ds(g * TG, TG), :, :].rearrange("t p d -> p t d")).then_inc(s_x[par], 16)

            load_x(0, 0)
            load_x(1, 1)

            def step(s, half, par):
                if active(s, -2):
                    sp.wait_ge(s_x[par], half(2) * 16)
                    load_x(s + 2, par)
                if not isinstance(s, int) or s < UNITS:
                    if after_first(s):
                        sp.wait_ge(s_w, s * 16)
                        apart(sp)
                    if later(s, 2):
                        sp.wait_ge(s_wl, s - 1)
                    apart(sp)
                    dst = w_stage[:, par, :]
                    if par:
                        dst = dst.rearrange("p (c d) -> p c d", c=FC)
                    sp.dma_start(dst, unit_source(s, half, par)).then_inc(s_w, 16)
                if active(s, 0):
                    sp.wait_ge(s_kc, s + 1)
                    if later(s, 2):
                        sp.wait_ge(s_score, s * TG - TG)
                    for h in range(HEADS):
                        on = slice(h * HD, (h + 1) * HD)
                        sp.dma_start(k_wide[on, par, :, h, :],
                                     kT[on, par, :].rearrange("p (t m) -> p t m", t=TG)).then_inc(s_kz[par], 16)

            steps(sp, step)
            sp.wait_ge(s_list, 1)
            for e in range(E):
                end = sp.value_load(end_i[0:1, e:e + 1], min_val=e * REGION, max_val=e * REGION + TOKENS)
                sp.dma_start(slots[bass.ds(end, ST), :].rearrange("(a p) w -> p a w", p=P),
                             pad_rows[:, :, :]).then_inc(s_pad, 16)
            sp.dma_start(slots[IDLE_ROW:IDLE_ROW + ST, :].rearrange("(a p) w -> p a w", p=P),
                         pad_rows[:, :, :]).then_inc(s_pad, 16)
            sp.wait_ge(s_pad, 16 * (E + 1))
            sp.wait_ge(s_sent[0], 16 * TG * GROUPS)
            sp.wait_ge(s_sent[1], 16 * TG * GROUPS)
            sp.wait_ge(s_list, 3)

            def load_slots(j, i, par, peeled):
                if not peeled:
                    sp.wait_ge(s_gT, j - 1)
                    sp.wait_ge(s_home, j - 1)
                row = sp.value_load(tile_row[0:1, bass.ds(j, 1)], min_val=0, max_val=IDLE_ROW)
                sp.dma_start(xg[:, par, :, :],
                             slots[bass.ds(row, ST), :].rearrange("(a p) w -> p a w", p=P)).then_inc(s_xg[par], 16)

            load_slots(0, 0, 0, True)
            load_slots(1, 0, 1, True)
            with sp.Fori(1, TILES // 2) as i:
                load_slots(i * 2, i, 0, False)
                load_slots(i * 2 + 1, i, 1, False)

            sp.wait_ge(s_back[0], 32 * (TILES // 2))
            sp.wait_ge(s_back[1], 32 * (TILES // 2))

            def load_pairs(j, par):
                sp.dma_start(yg[:, par, :, :], pairs[bass.ds(j * (2 * ST), 2 * ST), :].rearrange(
                    "(a p k) d -> p a (k d)", p=P, k=2)).then_inc(s_yg[par], 16)

            def store(j, par):
                sp.wait_ge(s_res, j + 1)
                sp.dma_start(out[bass.ds(j * 2, 2), :, :].rearrange("a p d -> p a d"),
                             res[:, par, :, :]).then_inc(s_out[par], 16)

            load_pairs(0, 0)
            load_pairs(1, 1)
            with sp.Fori(0, SHARED_TILES // 2 - 1) as i:
                for par in range(2):
                    store(i * 2 + par, par)
                    load_pairs(i * 2 + par + 2, par)
            for par in range(2):
                store(SHARED_TILES - 2 + par, par)
            for par in range(2):
                sp.wait_ge(s_out[par], 16 * (SHARED_TILES // 2))

        @block.gpsimd
        def _(gp):
            nc.gpsimd.memset(ident[:, :], 0.0).then_inc(s_pool_c, 1)
            nc.gpsimd.memset(ones_h[:, :], 1.0).then_inc(s_pool_c, 1)
            nc.gpsimd.memset(tri[:, :, :], 1.0).then_inc(s_pool_c, 1)
            nc.gpsimd.memset(minus_half[:, :], -0.5).then_inc(s_pool_c, 1)
            nc.gpsimd.memset(v1[:, :, :, :, :], 1.0).then_inc(s_pool_c, 1)
            nc.gpsimd.memset(pad_rows[:, :, :], 0.0).then_inc(s_pool_c, 1)
            nc.gpsimd.iota(rank_i[:, :], [[-1, E]], base=E, channel_multiplier=0).then_inc(s_pool_c, 1)
            nc.gpsimd.iota(j_i[:, :], [[1, J]], base=0, channel_multiplier=0).then_inc(s_pool_c, 1)
            nc.gpsimd.iota(base_i[:, :], [[REGION, E]], base=0, channel_multiplier=0).then_inc(s_pool_c, 1)
            nc.gpsimd.iota(ids[:, :], [[2 * P, B]], base=0, channel_multiplier=2).then_inc(s_pool_c, 1)
            gp.wait_ge(s_pool_c, 10)
            nc.gpsimd.affine_select(out=ident[:, :], in_=ident[:, :], compare_op=ALU.not_equal, fill=1.0,
                                    base=0, pattern=[[-1, P]], channel_multiplier=1).then_inc(s_pool_c, 1)
            nc.gpsimd.affine_select(out=before[:, :], in_=ones_h[:, :], compare_op=ALU.is_gt, fill=0.0,
                                    base=0, pattern=[[1, P]], channel_multiplier=-1).then_inc(s_pool_c, 1)
            nc.gpsimd.affine_select(out=tri[:, :, :], in_=tri[:, :, :], compare_op=ALU.is_ge, fill=0.0,
                                    base=0, pattern=[[1, E], [-1, E]], channel_multiplier=0).then_inc(s_pool_c, 1)
            nc.gpsimd.iota(pad_rows[:, :, :].bitcast(U32)[:, :, P:P + 1], [[0, 2], [0, 1]], base=NOWHERE,
                           channel_multiplier=0).then_inc(s_pool_c, 1)
            nc.gpsimd.memset(k_wide[:, :, :, :, :], 0.0).then_inc(s_pool_c, 1)

            def inv_std(n, g, own):
                gp.wait_ge(s_var[n], g + 1)
                apart(gp)
                nc.gpsimd.tensor_scalar(var_eps[:, n, :], meanvar[:, n, :, 1], EPS, None, ALU.add).then_inc(s_pl, 1)
                gp.wait_ge(s_pl, own)
                nc.gpsimd.tensor_tensor(rstd[:, n, :], var_eps[:, n, :], minus_half[:, :],
                                        ALU.pow).then_inc(s_rstd[n], 1)

            def own(s, n):
                if isinstance(s, int):
                    before_step = min(s + 1, GROUPS) + 2 * min(max(s - 2, 0), GROUPS)
                    here = [n_ for n_ in (1, 0, 2) if active(s, -1 if n_ == 0 else 2)]
                    return before_step + here.index(n) + 1
                return (s + 1) + (s - 2) * 2 + (1, 0, 2).index(n) + 1

            def step(s, half, par):
                g1, g2, g3 = s - 2, s - 3, s - 4
                has_unit = not isinstance(s, int) or s < UNITS
                if active(s, 0):
                    gp.wait_ge(s_xn, s + 1)
                    nc.gpsimd.tensor_tensor(x_all[:, bass.ds(s * TG, TG), :], x_all[:, bass.ds(s * TG, TG), :],
                                            beta_row[:, None, :].broadcast_to([P, TG, P]), ALU.add).then_inc(s_xbeta, 1)
                if has_unit:
                    blk = unit_block(s, half)
                    dst = (w2 if par else w1)[:, bass.ds(blk, FC * 2), :].rearrange("p (c h) d -> p c h d", h=2)
                    src = w_stage[:, par, :].rearrange("p (c d) -> p c d", c=FC)
                    gp.wait_ge(s_w, (s + 1) * 16)
                    apart(gp)
                    nc.gpsimd.tensor_copy(dst[:, :, 0, :], src).then_inc(s_wh, 1)
                if active(s, 4):
                    nc.gpsimd.tensor_copy(row_ids[:, par, :, P], ids[:, bass.ds(g3 * TG, TG)]).then_inc(s_id, 1)
                    gp.wait_ge(s_slot, g3 + 1)
                    gp.wait_ge(s_rowl, g3 + 1)
                    gp.wait_ge(s_id, g3 * 2 + 1)
                    apart(gp)
                    for t in range(TG):
                        nc.gpsimd.indirect_dma_start(
                            out=slots[:, :], out_offset=bass.IndirectOffsetOnAxis(ap=slot[:, par, 0, t:t + 1], axis=0),
                            in_=rows[:, par, t, :], in_offset=None).then_inc(s_sent[0], 16)
                if has_unit:
                    gp.wait_ge(s_wh, s + 1)
                    nc.gpsimd.tensor_tensor(dst[:, :, 1, :], src, dst[:, :, 0, :], ALU.subtract).then_inc(s_wl, 1)
                if active(s, 2):
                    inv_std(1, g1, own(s, 1))
                if active(s, -1):
                    inv_std(0, s + 1, own(s, 0))
                if active(s, 2):
                    inv_std(2, g1, own(s, 2))
                if active(s, 3):
                    gp.wait_ge(s_xh, g2 + 1)
                    nc.gpsimd.tensor_tensor(xl_all[:, bass.ds(g2 * W, W)], x2T[:, :], xh_all[:, bass.ds(g2 * W, W)],
                                            ALU.subtract).then_inc(s_xl, 1)
                if active(s, 4):
                    gp.wait_ge(s_sent[0], (g3 + 1) * (16 * TG))
                    apart(gp)
                    nc.gpsimd.tensor_scalar(row_ids[:, par, :, P], row_ids[:, par, :, P], 1, None,
                                            ALU.add).then_inc(s_id, 1)
                    gp.wait_ge(s_id, g3 * 2 + 2)
                    apart(gp)
                    for t in range(TG):
                        nc.gpsimd.indirect_dma_start(
                            out=slots[:, :], out_offset=bass.IndirectOffsetOnAxis(ap=slot[:, par, 1, t:t + 1], axis=0),
                            in_=rows[:, par, t, :], in_offset=None).then_inc(s_sent[1], 16)

            inv_std(0, 0, 1)
            steps(gp, step)

            def copy_home(j, i, q):
                gp.wait_ge(s_xg[q % 2], (i * 2 + q // 2 + 1) * 16)
                if later(j, 4):
                    gp.wait_ge(s_back[q % 2], (i * 2 + (q // 2 - 1)) * 32)
                apart(gp)
                nc.gpsimd.tensor_copy(home[:, q, :], xg_ids[:, q % 2, :, P]).then_inc(s_home, 1)

            def send_back(j, q):
                gp.wait_ge(s_yc, j + 1)
                gp.wait_ge(s_home, j + 1)
                apart(gp)
                for a in range(2):
                    nc.gpsimd.indirect_dma_start(
                        out=pairs[:, :], out_offset=bass.IndirectOffsetOnAxis(ap=home[:, q, a:a + 1], axis=0),
                        in_=y[:, q % 2, a, :], in_offset=None, bounds_check=2 * TOKENS - 1,
                        oob_is_err=False).then_inc(s_back[q % 2], 16)

            copy_home(0, 0, 0)
            for q in range(4):
                copy_home(q + 1, (q + 1) // 4, (q + 1) % 4)
                send_back(q, q)
            with gp.Fori(1, TILES // 4 - 1) as i:
                for q in range(4):
                    copy_home(i * 4 + q + 1, i + (q + 1) // 4, (q + 1) % 4)
                    send_back(i * 4 + q, q)
            for q in range(4):
                if q < 3:
                    copy_home(TILES - 4 + q + 1, TILES // 4 - 1, q + 1)
                send_back(TILES - 4 + q, q)

            def bias_x1(j, par):
                if later(j, 2):
                    gp.wait_ge(s_acc, j - 1)
                nc.gpsimd.tensor_tensor(x1b[:, par, :, :], x_all[:, bass.ds(j * 2, 2), :],
                                        b2s_row[:, None, :].broadcast_to([P, 2, P]), ALU.add).then_inc(s_x1b, 1)

            bias_x1(0, 0)
            bias_x1(1, 1)
            with gp.Fori(1, SHARED_TILES // 2) as i:
                bias_x1(i * 2, 0)
                bias_x1(i * 2 + 1, 1)

        @block.scalar
        def _(act):
            act.wait_ge(s_pe_c, 1)
            nc.scalar.activation(bias_cols[:, :], ps_m[:, 0:NB + 3], ACT.Identity).then_inc(s_act_c, 1)
            act.wait_ge(s_act_c, 1)
            nc.scalar.mul(bq_scaled[:, :], bias_cols[:, NB:NB + 1], SCALE).then_inc(s_act_c, 1)
            act.wait_ge(s_act_c, 2)

            def front_1(s):
                act.wait_ge(s_xT, s + 1)
                nc.scalar.activation(xnT[:, :], ps_m[:, :], ACT.Identity).then_inc(s_xTc, 1)

            def front_2(s, half, par):
                act.wait_ge(s_q, s + 1)
                nc.scalar.activation(qT[:, par, :], ps_n[:, :], ACT.Identity, bias=bq_scaled[:, 0:1],
                                     scale=SCALE).then_inc(s_qc, 1)
                act.wait_ge(s_k, s + 1)
                if later(s, 2):
                    act.wait_ge(s_kz[par], half(0) * 64)
                nc.scalar.activation(kT[:, par, :], ps_m[:, :], ACT.Identity,
                                     bias=bias_cols[:, NB + 1:NB + 2]).then_inc(s_kc, 1)

            def front_3(s, par):
                act.wait_ge(s_v, s + 1)
                nc.scalar.activation(v1[:, par, :, :, 0:HD], ps_n[:, :].rearrange("p (t h d) -> p t h d", t=TG, h=HEADS),
                                     ACT.Identity).then_inc(s_vc, 1)

            def exponentials(g, t):
                act.wait_ge(s_max, g * TG + t + 1)
                if t >= 2 or after_first(g):
                    act.wait_ge(s_pT, g * TG + t - 1)
                for h in range(HEADS):
                    last = nc.scalar.activation(probs[:, t % 2, h, :], ps_s[:, t % 2, h, :], ACT.Exp,
                                                bias=neg_max[:, t % 2, h:h + 1])
                last.then_inc(s_exp, 1)

            def copy_probsT(g, t):
                act.wait_ge(s_pT, g * TG + t + 1)
                nc.scalar.activation(probsT[:, t % 2, :], ps_pT[:, :], ACT.Identity).then_inc(s_pTc, 1)

            def copy_attnT(g):
                act.wait_ge(s_oT, g + 1)
                nc.scalar.activation(attnT[:, :], ps_m[:, :], ACT.Identity).then_inc(s_oTc, 1)

            def row_high(g, par):
                act.wait_ge(s_x2n, g + 1)
                if later(g, 2):
                    act.wait_ge(s_sent[1], (g - 1) * (16 * TG))
                nc.scalar.activation(rows[:, par, :, 0:P], x2n[:, :, :], ACT.Identity).then_inc(s_rowh, 1)

            def copy_x2T(g):
                act.wait_ge(s_x2T, g + 1)
                if after_first(g):
                    act.wait_ge(s_xl, g)
                nc.scalar.activation(x2T[:, :], ps_m[:, :], ACT.Identity).then_inc(s_x2Tc, 1)
                nc.scalar.activation(xh_all[:, bass.ds(g * W, W)], ps_m[:, :], ACT.Identity).then_inc(s_xh, 1)

            def step(s, half, par):
                m = s - 1
                if active(s, 0):
                    front_1(s)
                if active(s, 1):
                    exponentials(m, 0)
                if active(s, 0):
                    front_2(s, half, par)
                if active(s, 1):
                    exponentials(m, 1)
                    copy_probsT(m, 0)
                if active(s, 3):
                    row_high(s - 3, 1 - par)
                if active(s, 0):
                    front_3(s, par)
                if active(s, 1):
                    exponentials(m, 2)
                if active(s, 2):
                    copy_attnT(s - 2)
                if active(s, 1):
                    copy_probsT(m, 1)
                    exponentials(m, 3)
                    copy_probsT(m, 2)
                if active(s, 3):
                    copy_x2T(s - 3)
                if active(s, 1):
                    copy_probsT(m, 3)

            steps(act, step)
            act.wait_ge(s_list, 3)
            nc.scalar.activation(weight2[:, :], delta[:, :], ACT.Exp).then_inc(s_soft, 1)

            def hidden(j, par, n, b1):
                for c in range(FC):
                    if c % 2 == 0:
                        act.wait_ge(s_h, n * 2 + (c // 2 + 1))
                    if c == 0 and later(n, 2):
                        act.wait_ge(s_hl, n * 2 - 2)
                    nc.scalar.activation(hid[:, par, c, :], ps_h[:, par, c, :], ACT.Gelu,
                                         bias=b1(c)).then_inc(s_hid, 1)

            def slots_T(j, par):
                act.wait_ge(s_gT, j + 1)
                if not (isinstance(j, int) and j < 2):
                    act.wait_ge(s_h, j * 2 - 2)
                nc.scalar.activation(xgT[:, par, :, :], ps_xT[par], ACT.Identity).then_inc(s_gTc, 1)

            def expert(j, par):
                e = act.value_load(tile_expert[0:1, bass.ds(j, 1)], min_val=0, max_val=E - 1)
                hidden(j, par, j, lambda c: bias_cols[:, bass.ds(e * FC + c, 1)])

            act.wait_ge(s_list, 3)
            slots_T(0, 0)
            slots_T(1, 1)
            expert(0, 0)
            expert_last = TILES - 1
            slots_T(2, 0)
            expert(1, 1)
            with act.Fori(1, TILES // 2 - 1) as i:
                slots_T(i * 2 + 1, 1)
                expert(i * 2, 0)
                slots_T(i * 2 + 2, 0)
                expert(i * 2 + 1, 1)
            slots_T(expert_last, 1)
            expert(expert_last - 1, 0)
            expert(expert_last, 1)
            with act.Fori(0, SHARED_TILES // 2) as i:
                for par in range(2):
                    hidden(i * 2 + par, par, i * 2 + (TILES + par),
                           lambda c: bias_cols[:, E * FC + c:E * FC + c + 1])

        @block.vector
        def _(dve):
            dve.wait_ge(s_c, 16 * 16)
            dve.wait_ge(s_pool_c, 15)
            nc.vector.tensor_copy(ident_h[:, :], ident[:, :]).then_inc(s_cast_c, 1)
            nc.vector.tensor_scalar(mask_h[:, :], adj_i[:, :], 0, MASKED, ALU.is_equal, ALU.mult).then_inc(s_cast_c, 1)
            nc.vector.tensor_copy(rank[:, :], rank_i[:, :]).then_inc(s_cast_c, 1)
            nc.vector.tensor_copy(region_start[:, :], base_i[:, :]).then_inc(s_cast_c, 1)
            nc.vector.tensor_copy(base[:, 0, :], base_i[:, :]).then_inc(s_cast_c, 1)
            nc.vector.tensor_copy(j_f[:, :], j_i[:, :]).then_inc(s_cast_c, 1)
            dve.wait_ge(s_act_c, 1)
            nc.vector.tensor_copy(bv_wide[:, :], bias_cols[:, NB + 2:NB + 3].broadcast_to([P, P])).then_inc(s_cast_c, 1)
            dve.wait_ge(s_pe_c, 2)
            nc.vector.tensor_tensor(c_row[:, :], ps_n[:, 0:P], bo_row[:, :], ALU.add).then_inc(s_crow, 1)
            dve.wait_ge(s_crow, 1)

            def statistics(n, g, src, own):
                apart(dve)
                for t in range(TG):
                    nc.vector.bn_stats(stats[:, n, t, :], src(t)).then_inc(s_ln, 1)
                dve.wait_ge(s_ln, own + TG)
                apart(dve)
                for t in range(TG):
                    last = nc.vector.bn_aggr(meanvar[:, n, t, :], stats[:, n, t, :])
                last.then_inc(s_var[n], 1)

            def own_ln(s, n):
                if isinstance(s, int):
                    norms = min(s + 1, GROUPS) + 2 * min(max(s - 2, 0), GROUPS)
                    here = [k for k in (1, 0, 2) if active(s, -1 if k == 0 else 2)]
                    return 4 * (norms + here.index(n))
                return (s + 1 + (s - 2) * 2 + (1, 0, 2).index(n)) * 4

            def max_rows(g, t):
                dve.wait_ge(s_score, g * TG + t + 1)
                if t >= 2 or after_first(g):
                    dve.wait_ge(s_exp, g * TG + t - 1)
                nc.vector.tensor_reduce(neg_max[:, t % 2, :], ps_s[:, t % 2, :, :], AX_X, ALU.max,
                                        negate=True).then_inc(s_max, 1)

            def normalise(g, par, t):
                dve.wait_ge(s_av, g * TG + t + 1)
                nc.vector.reciprocal(inv_sum[:, t % 2, :], ps_av[:, t % 2, :, HD]).then_inc(s_inv, 1)
                dve.wait_ge(s_inv, g * TG + t + 1)
                nc.vector.tensor_tensor(attn[:, par, t, :].rearrange("p (h d) -> p h d", h=HEADS),
                                        ps_av[:, t % 2, :, 0:HD],
                                        inv_sum[:, t % 2, :].unsqueeze(2).broadcast_to([P, HEADS, HD]),
                                        ALU.mult).then_inc(s_attn, 1)

            def route_1(g):
                o = g * 11
                k = [0]

                def own(ins):
                    k[0] += 1
                    ins.then_inc(s_route, 1)
                    dve.wait_ge(s_route, o + k[0])

                rk = rank[:, None, :].broadcast_to([P, TG, E])
                dve.wait_ge(s_logit, g + 1)
                own(nc.vector.tensor_copy(logits[:, :, :], ps_logit))
                own(nc.vector.tensor_reduce(top1[:, :], logits[:, :, :], AX_X, ALU.max))
                own(nc.vector.tensor_tensor(hit[:, 0, :, :], logits[:, :, :],
                                            top1[:, :].unsqueeze(2).broadcast_to([P, TG, E]), ALU.is_equal))
                own(nc.vector.tensor_tensor(hit[:, 1, :, :], hit[:, 0, :, :], rk, ALU.mult))
                own(nc.vector.tensor_reduce(first[:, 0, :], hit[:, 1, :, :], AX_X, ALU.max))
                own(nc.vector.tensor_tensor(hot1[:, :, :], rk, first[:, 0, :].unsqueeze(2).broadcast_to([P, TG, E]),
                                            ALU.is_equal))
                own(nc.vector.scalar_tensor_tensor(rest[:, :, :], hot1[:, :, :], MASKED, logits[:, :, :],
                                                   ALU.mult, ALU.add))
                own(nc.vector.tensor_reduce(top2[:, :], rest[:, :, :], AX_X, ALU.max))
                nc.vector.tensor_tensor(delta[:, bass.ds(g * TG, TG)], top2[:, :], top1[:, :], ALU.subtract)
                own(nc.vector.tensor_tensor(hit[:, 0, :, :], rest[:, :, :],
                                            top2[:, :].unsqueeze(2).broadcast_to([P, TG, E]), ALU.is_equal))
                own(nc.vector.tensor_tensor(hit[:, 1, :, :], hit[:, 0, :, :], rk, ALU.mult))
                own(nc.vector.tensor_reduce(first[:, 1, :], hit[:, 1, :, :], AX_X, ALU.max))
                nc.vector.tensor_tensor(hot2[:, :, :], rk, first[:, 1, :].unsqueeze(2).broadcast_to([P, TG, E]),
                                        ALU.is_equal).then_inc(s_chosen, 1)
                dve.wait_ge(s_chosen, g * 2 + 1)
                nc.vector.tensor_tensor(chosen[:, :, :], hot1[:, :, :], hot2[:, :, :], ALU.add).then_inc(s_chosen, 1)

            def route_2(g, par):
                o = g * 5
                dve.wait_ge(s_before, g + 1)
                nc.vector.tensor_tensor(place[:, :, :], ps_before, base[:, par, None, :].broadcast_to([P, TG, E]),
                                        ALU.add).then_inc(s_place, 1)
                nc.vector.tensor_tensor(base[:, 1 - par, :], ps_total, base[:, par, :], ALU.add).then_inc(s_place, 1)
                dve.wait_ge(s_place, o + 2)
                nc.vector.tensor_tensor(placed[:, 0, :, :], place[:, :, :], hot1[:, :, :], ALU.mult).then_inc(s_place, 1)
                nc.vector.tensor_tensor(placed[:, 1, :, :], place[:, :, :], hot2[:, :, :], ALU.mult).then_inc(s_place, 1)
                dve.wait_ge(s_place, o + 4)
                nc.vector.tensor_reduce(slot_f[:, :, :], placed[:, :, :, :], AX_X, ALU.add).then_inc(s_place, 1)
                dve.wait_ge(s_place, o + 5)
                if later(g, 2):
                    dve.wait_ge(s_sent[1], (g - 1) * (16 * TG))
                nc.vector.tensor_copy(slot[:, par, :, :], slot_f[:, :, :]).then_inc(s_slot, 1)

            def tile_of(n):
                return x_all[:, bass.ds(n, 1), :].rearrange("p a d -> p (a d)")

            def x_statistics(g, half, par, own):
                dve.wait_ge(s_x[par], (half + 1) * 16)
                if after_first(g):
                    dve.wait_ge(s_rstd[0], g)
                statistics(0, g, lambda t: tile_of(g * TG + t), own)

            def x_normed(g):
                dve.wait_ge(s_rstd[0], g + 1)
                if after_first(g):
                    dve.wait_ge(s_xT, g)
                for t in range(TG):
                    last = nc.vector.tensor_scalar(xn[:, t * P:(t + 1) * P], tile_of(g * TG + t),
                                                   meanvar[:, 0, t, 0:1], rstd[:, 0, t:t + 1],
                                                   ALU.subtract, ALU.mult)
                last.then_inc(s_xn, 1)

            def projection(g, own):
                dve.wait_ge(s_proj, g + 1)
                if after_first(g):
                    dve.wait_ge(s_scaled, g)
                    dve.wait_ge(s_rstd[1], g)
                nc.vector.tensor_tensor(proj[:, :, :], ps_n[:, :].rearrange("p (t d) -> p t d", t=TG),
                                        c_row[:, None, :].broadcast_to([P, TG, P]), ALU.add).then_inc(s_projc, 1)
                dve.wait_ge(s_projc, g + 1)
                statistics(1, g, lambda t: proj[:, t, :], own)

            def residual(g, own):
                if after_first(g):
                    dve.wait_ge(s_x1, g)
                dve.wait_ge(s_var[1], g + 1)
                for t in range(TG):
                    last = nc.vector.scalar_tensor_tensor(scaled[:, t, :], proj[:, t, :], meanvar[:, 1, t, 0:1],
                                                          gamma_row[:, :], ALU.subtract, ALU.mult)
                last.then_inc(s_scaled, 1)
                dve.wait_ge(s_scaled, g + 1)
                dve.wait_ge(s_rstd[1], g + 1)
                dve.wait_ge(s_xbeta, g + 1)
                for t in range(TG):
                    last = nc.vector.scalar_tensor_tensor(tile_of(g * TG + t), scaled[:, t, :], rstd[:, 1, t:t + 1],
                                                          tile_of(g * TG + t), ALU.mult, ALU.add)
                last.then_inc(s_x1, 1)
                dve.wait_ge(s_x1, g + 1)
                if after_first(g):
                    dve.wait_ge(s_rstd[2], g)
                statistics(2, g, lambda t: tile_of(g * TG + t), own)

            def x1_normed(g):
                dve.wait_ge(s_rstd[2], g + 1)
                if after_first(g):
                    dve.wait_ge(s_x2T, g)
                    dve.wait_ge(s_rowh, g)
                for t in range(TG):
                    last = nc.vector.tensor_scalar(x2n[:, t, :], tile_of(g * TG + t), meanvar[:, 2, t, 0:1],
                                                   rstd[:, 2, t:t + 1], ALU.subtract, ALU.mult)
                last.then_inc(s_x2n, 1)

            def row_low(g, par):
                dve.wait_ge(s_rowh, g + 1)
                nc.vector.tensor_tensor(rows[:, par, :, P:2 * P], x2n[:, :, :], rows[:, par, :, 0:P],
                                        ALU.subtract).then_inc(s_rowl, 1)

            def step(s, half, par):
                m = s - 1
                if active(s, 1):
                    max_rows(m, 0)
                if active(s, 4):
                    route_1(s - 4)
                if active(s, 1):
                    max_rows(m, 1)
                if active(s, 3):
                    x1_normed(s - 3)
                if active(s, 1):
                    normalise(m, 1 - par, 0)
                    max_rows(m, 2)
                if active(s, 3):
                    row_low(s - 3, 1 - par)
                if active(s, 4):
                    route_2(s - 4, par)
                if active(s, 1):
                    normalise(m, 1 - par, 1)
                    max_rows(m, 3)
                if active(s, 2):
                    projection(s - 2, own_ln(s, 1))
                if active(s, 1):
                    normalise(m, 1 - par, 2)
                if active(s, -1):
                    x_statistics(s + 1, half(1), 1 - par, own_ln(s, 0))
                if active(s, 2):
                    residual(s - 2, own_ln(s, 2))
                if active(s, 1):
                    normalise(m, 1 - par, 3)
                if active(s, -1):
                    x_normed(s + 1)

            x_statistics(0, 0, 0, 0)
            x_normed(0)
            steps(dve, step)

            k = [0]

            def own(ins):
                k[0] += 1
                ins.then_inc(s_wt, 1)
                dve.wait_ge(s_wt, k[0])

            end = base[:, GROUPS % 2, :]
            nc.vector.tensor_copy(end_i[:, :], end).then_inc(s_list, 1)
            own(nc.vector.tensor_tensor(count[:, :], end, region_start[:, :], ALU.subtract))
            own(nc.vector.tensor_scalar(ntile_i[:, :], count[:, :], ST / 2 - 0.5, 1.0 / ST, ALU.add, ALU.mult))
            own(nc.vector.tensor_copy(ntile[:, :], ntile_i[:, :]))
            own(nc.vector.tensor_tensor(tmp88[:, :, :], tri[:, :, :], ntile[:, None, :].broadcast_to([P, E, E]),
                                        ALU.mult))
            own(nc.vector.tensor_reduce(upto[:, :], tmp88[:, :, :], AX_X, ALU.add))
            own(nc.vector.tensor_scalar(jump[:, :], ntile[:, :], -float(ST), float(REGION), ALU.mult, ALU.add))
            own(nc.vector.tensor_tensor(past[:, :, :], j_f[:, :].unsqueeze(2).broadcast_to([P, J, E]),
                                        upto[:, None, :].broadcast_to([P, J, E]), ALU.is_ge))
            own(nc.vector.tensor_tensor(jumps[:, :, :], past[:, :, :], jump[:, None, :].broadcast_to([P, J, E]),
                                        ALU.mult))
            own(nc.vector.tensor_reduce(e_f[:, :], past[:, :, :], AX_X, ALU.add))
            own(nc.vector.tensor_reduce(r_f[:, :], jumps[:, :, :], AX_X, ALU.add))
            own(nc.vector.scalar_tensor_tensor(r_g[:, :], j_f[:, :], float(ST), r_f[:, :], ALU.mult, ALU.add))
            nc.vector.tensor_scalar(tile_expert[:, :], e_f[:, :], float(E - 1), None, ALU.min).then_inc(s_list, 1)
            nc.vector.tensor_scalar(tile_row[:, :], r_g[:, :], float(IDLE_ROW), None, ALU.min).then_inc(s_list, 1)
            dve.wait_ge(s_soft, 1)
            own(nc.vector.tensor_scalar(weight1[:, :], weight2[:, :], 1.0, None, ALU.add))
            own(nc.vector.reciprocal(weight1[:, :], weight1[:, :]))
            own(nc.vector.tensor_tensor(weight2[:, :], weight2[:, :], weight1[:, :], ALU.mult))

            def split(n, par):
                for c in range(2):
                    dve.wait_ge(s_hid, n * FC + 2 * c + 2)
                    if c == 0 and not (isinstance(n, int) and n < 2):
                        dve.wait_ge(s_y, n - 1)
                    nc.vector.tensor_copy(hid_h[:, par, 2 * c:2 * c + 2, :],
                                          hid[:, par, 2 * c:2 * c + 2, :]).then_inc(s_hh, 1)
                    dve.wait_ge(s_hh, n * 2 + c + 1)
                    nc.vector.tensor_tensor(hid_l[:, par, 2 * c:2 * c + 2, :], hid[:, par, 2 * c:2 * c + 2, :],
                                            hid_h[:, par, 2 * c:2 * c + 2, :], ALU.subtract).then_inc(s_hl, 1)

            def collect(j, i, par):
                e = dve.value_load(tile_expert[0:1, bass.ds(j, 1)], min_val=0, max_val=E - 1)
                dve.wait_ge(s_y, j + 1)
                if not (isinstance(i, int) and i < 1):
                    dve.wait_ge(s_back[par], i * 32)
                nc.vector.tensor_tensor(y[:, par, :, :], ps_y[par],
                                        b2_rows[:, bass.ds(e, 1), :].broadcast_to([P, 2, P]), ALU.add).then_inc(s_yc, 1)

            split(0, 0)
            split(1, 1)
            collect(0, 0, 0)
            split(2, 0)
            collect(1, 0, 1)
            with dve.Fori(1, TILES // 2 - 1) as i:
                split(i * 2 + 1, 1)
                collect(i * 2, i, 0)
                split(i * 2 + 2, 0)
                collect(i * 2 + 1, i, 1)
            split(TILES - 1, 1)
            collect(TILES - 2, TILES // 2 - 1, 0)
            collect(TILES - 1, TILES // 2 - 1, 1)

            def finish(j, i, par):
                dve.wait_ge(s_y, j + (TILES + 1))
                dve.wait_ge(s_x1b, j + 1)
                nc.vector.tensor_tensor(acc[:, par, :, :], ps_y[par], x1b[:, par, :, :], ALU.add).then_inc(s_acc, 1)
                dve.wait_ge(s_yg[par], (i + 1) * 16)
                dve.wait_ge(s_acc, j + 1)
                for a in range(2):
                    col = j * 2 + a
                    last = nc.vector.scalar_tensor_tensor(acc2[:, par, a, :], yg[:, par, a, 0:P],
                                                          weight1[:, bass.ds(col, 1)], acc[:, par, a, :],
                                                          ALU.mult, ALU.add)
                last.then_inc(s_xn, 1)
                dve.wait_ge(s_xn, j + (GROUPS + 1))
                if not (isinstance(i, int) and i < 1):
                    dve.wait_ge(s_out[par], i * 16)
                for a in range(2):
                    col = j * 2 + a
                    last = nc.vector.scalar_tensor_tensor(res[:, par, a, :], yg[:, par, a, P:2 * P],
                                                          weight2[:, bass.ds(col, 1)], acc2[:, par, a, :],
                                                          ALU.mult, ALU.add)
                last.then_inc(s_res, 1)

            split(TILES, 0)
            split(TILES + 1, 1)
            finish(0, 0, 0)
            split(TILES + 2, 0)
            finish(1, 0, 1)
            with dve.Fori(1, SHARED_TILES // 2 - 1) as i:
                split(i * 2 + (TILES + 1), 1)
                finish(i * 2, i, 0)
                split(i * 2 + (TILES + 2), 0)
                finish(i * 2 + 1, i, 1)
            split(TILES + SHARED_TILES - 1, 1)
            finish(SHARED_TILES - 2, SHARED_TILES // 2 - 1, 0)
            finish(SHARED_TILES - 1, SHARED_TILES // 2 - 1, 1)

        @block.tensor
        def _(pe):
            pe.wait_ge(s_c, 16 * 16)
            pe.wait_ge(s_pool_c, 15)
            nc.tensor.transpose(ps_m[:, 0:NB + 3], bias_rows[:, :], ident[0:NB + 3, 0:NB + 3]).then_inc(s_pe_c, 1)
            pe.wait_ge(s_cast_c, 7)
            nc.tensor.matmul(ps_n[:, 0:P], bv_wide[:, :], w_o[:, :], start=True, stop=True).then_inc(s_pe_c, 1)
            pe.wait_ge(s_crow, 1)

            def transpose_x(s):
                pe.wait_ge(s_xn, s + 1)
                if later(s, 4):
                    pe.wait_ge(s_xh, s - 3)
                elif s == 3:
                    pe.wait_ge(s_oTc, 1)
                elif s:
                    pe.wait_ge(s_kc, s)
                for t in range(TG):
                    last = nc.tensor.transpose(ps_m[:, t * P:(t + 1) * P], xn[:, t * P:(t + 1) * P], ident[:, :])
                last.then_inc(s_xT, 1)

            def project_qk(s):
                if later(s, 3):
                    pe.wait_ge(s_projc, s - 2)
                elif s:
                    pe.wait_ge(s_vc, s)
                pe.wait_ge(s_xTc, s + 1)
                nc.tensor.matmul(ps_n[:, :], w_q[:, :], xnT[:, :], start=True, stop=True).then_inc(s_q, 1)
                nc.tensor.matmul(ps_m[:, :], w_k[:, :], xnT[:, :], start=True, stop=True).then_inc(s_k, 1)

            def project_v(s):
                pe.wait_ge(s_qc, s + 1)
                for t in range(TG):
                    last = nc.tensor.matmul(ps_n[:, t * P:(t + 1) * P], xnT[:, t * P:(t + 1) * P], w_v[:, :],
                                            start=True, stop=True)
                last.then_inc(s_v, 1)

            def scores(g, half, par, t):
                if t == 0:
                    pe.wait_ge(s_kz[par], (half + 1) * 64)
                if t >= 2 or after_first(g):
                    pe.wait_ge(s_exp, g * TG + t - 1)
                nc.tensor.matmul(ps_s[:, t % 2, :, :], ident_h[:, :], mask_h[:, None, :].broadcast_to([P, HEADS, P]),
                                 start=True, stop=False)
                nc.tensor.matmul(ps_s[:, t % 2, :, :], qT[:, par, t * P:(t + 1) * P], k_wide[:, par, t, :, :],
                                 start=False, stop=True).then_inc(s_score, 1)

            def transpose_probs(g, t):
                pe.wait_ge(s_exp, g * TG + t + 1)
                if t or after_first(g):
                    pe.wait_ge(s_pTc, g * TG + t)
                for h in range(HEADS):
                    last = nc.tensor.transpose(ps_pT[:, h * P:(h + 1) * P], probs[:, t % 2, h, :], ident[:, :])
                last.then_inc(s_pT, 1)

            def attend(g, par, t):
                pe.wait_ge(s_pTc, g * TG + t + 1)
                if t == 0:
                    pe.wait_ge(s_vc, g + 1)
                if t >= 2 or after_first(g):
                    pe.wait_ge(s_attn, g * TG + t - 1)
                for h in range(HEADS):
                    last = nc.tensor.matmul(ps_av[:, t % 2, h, :], probsT[:, t % 2, h * P:(h + 1) * P],
                                            v1[:, par, t, h, :], start=True, stop=True)
                last.then_inc(s_av, 1)

            def transpose_attn(g, par, free):
                pe.wait_ge(s_attn, (g + 1) * TG)
                pe.wait_ge(*free)
                for t in range(TG):
                    last = nc.tensor.transpose(ps_m[:, t * P:(t + 1) * P], attn[:, par, t, :], ident[:, :])
                last.then_inc(s_oT, 1)

            def project_out(g, free):
                pe.wait_ge(s_oTc, g + 1)
                pe.wait_ge(*free)
                for t in range(TG):
                    last = nc.tensor.matmul(ps_n[:, t * P:(t + 1) * P], attnT[:, t * P:(t + 1) * P], w_o[:, :],
                                            start=True, stop=True)
                last.then_inc(s_proj, 1)

            def count_before(g):
                pe.wait_ge(s_chosen, g * 2 + 2)
                for t in range(TG):
                    nc.tensor.matmul(ps_before[:, t, :], before[:, :], chosen[:, t, :], start=True, stop=t == 0)
                    for u in range(t):
                        nc.tensor.matmul(ps_before[:, t, :], ones_h[:, :], chosen[:, u, :], start=False,
                                         stop=u == t - 1)
                for t in range(TG):
                    last = nc.tensor.matmul(ps_total, ones_h[:, :], chosen[:, t, :], start=t == 0, stop=t == TG - 1)
                last.then_inc(s_before, 1)

            def transpose_x1(g, free):
                pe.wait_ge(s_x2n, g + 1)
                pe.wait_ge(*free)
                for t in range(TG):
                    last = nc.tensor.transpose(ps_m[:, t * P:(t + 1) * P], x2n[:, t, :], ident[:, :])
                last.then_inc(s_x2T, 1)

            def router(g):
                pe.wait_ge(s_x2Tc, g + 1)
                if after_first(g):
                    pe.wait_ge(s_place, g * 5)
                for t in range(TG):
                    last = nc.tensor.matmul(ps_logit[:, t, :], x2T[:, t * P:(t + 1) * P], w_r[:, :],
                                            start=True, stop=True)
                last.then_inc(s_logit, 1)

            def step(s, half, par):
                m = s - 1
                q = 1 - par
                if active(s, 0):
                    transpose_x(s)
                if active(s, 1):
                    scores(m, half(-1), q, 0)
                if active(s, 0):
                    project_qk(s)
                if active(s, 1):
                    scores(m, half(-1), q, 1)
                    transpose_probs(m, 0)
                if active(s, 0):
                    project_v(s)
                if active(s, 1):
                    attend(m, q, 0)
                    scores(m, half(-1), q, 2)
                if active(s, 2):
                    transpose_attn(s - 2, par, (s_kc, s + 1) if active(s, 0) else (s_xh, s - 3))
                if active(s, 1):
                    transpose_probs(m, 1)
                if active(s, 4):
                    count_before(s - 4)
                if active(s, 1):
                    attend(m, q, 1)
                    scores(m, half(-1), q, 3)
                if active(s, 2):
                    project_out(s - 2, (s_vc, s + 1) if active(s, 0) else (s_projc, s - 2))
                if active(s, 1):
                    transpose_probs(m, 2)
                if active(s, 3):
                    transpose_x1(s - 3, (s_oTc, s - 1) if active(s, 2) else (s_xh, s - 3))
                if active(s, 1):
                    attend(m, q, 2)
                    transpose_probs(m, 3)
                if active(s, 3):
                    router(s - 3)
                if active(s, 1):
                    attend(m, q, 3)

            steps(pe, step)

            def slots_T(j, i, par):
                pe.wait_ge(s_xg[par], (i + 1) * 16)
                if not (isinstance(j, int) and j < 2):
                    pe.wait_ge(s_gTc, j - 1)
                for hl in range(2):
                    for a in range(2):
                        last = nc.tensor.transpose(ps_xT[par][:, hl, a * P:(a + 1) * P],
                                                   xg[:, par, a, hl * P:(hl + 1) * P], ident_h[:, :])
                last.then_inc(s_gT, 1)

            def first_layer(n, par, w_at, hi, lo):
                for c in range(FC):
                    if c % 2 == 0 and later(n, 2):
                        pe.wait_ge(s_hid, n * FC + (c + 2 - 2 * FC))
                    dst = ps_h[:, par, c, :]
                    nc.tensor.matmul(dst, w_at(w1, 2 * c), hi, start=True, stop=False)
                    nc.tensor.matmul(dst, w_at(w1, 2 * c), lo, start=False, stop=False)
                    last = nc.tensor.matmul(dst, w_at(w1, 2 * c + 1), hi, start=False, stop=True)
                    if c % 2:
                        last.then_inc(s_h, 1)

            def second_layer(n, par, w_at):
                for a in range(2):
                    dst = ps_y[par][:, a, :]
                    for c in range(FC):
                        if a == 0 and c % 2 == 0:
                            pe.wait_ge(s_hl, n * 2 + c // 2 + 1)
                        cols = slice(a * P, (a + 1) * P)
                        nc.tensor.matmul(dst, hid_h[:, par, c, cols], w_at(w2, 2 * c), start=c == 0, stop=False)
                        nc.tensor.matmul(dst, hid_h[:, par, c, cols], w_at(w2, 2 * c + 1), start=False, stop=False)
                        last = nc.tensor.matmul(dst, hid_l[:, par, c, cols], w_at(w2, 2 * c), start=False,
                                                stop=c == FC - 1)
                last.then_inc(s_y, 1)

            def expert_weights(j):
                e = pe.value_load(tile_expert[0:1, bass.ds(j, 1)], min_val=0, max_val=E - 1)

                def w_at(w, k):
                    return w[:, bass.ds(e * (2 * FC) + k, 1), :].rearrange("p a d -> p (a d)")
                return w_at

            def expert_1(j, par):
                pe.wait_ge(s_gTc, j + 1)
                first_layer(j, par, expert_weights(j), xgT[:, par, 0, :], xgT[:, par, 1, :])

            def expert_2(j, par):
                if not (isinstance(j, int) and j < 2):
                    pe.wait_ge(s_yc, j - 1)
                apart(pe)
                second_layer(j, par, expert_weights(j))

            pe.wait_ge(s_list, 3)
            pe.wait_ge(s_wl, UNITS)
            pe.wait_ge(s_place, GROUPS * 5)
            pe.wait_ge(s_exp, GROUPS * TG)
            slots_T(0, 0, 0)
            slots_T(1, 0, 1)
            expert_1(0, 0)
            slots_T(2, 1, 0)
            expert_1(1, 1)
            expert_2(0, 0)
            slots_T(3, 1, 1)
            with pe.Fori(1, TILES // 2 - 1) as i:
                expert_1(i * 2, 0)
                expert_2(i * 2 - 1, 1)
                slots_T(i * 2 + 2, i + 1, 0)
                expert_1(i * 2 + 1, 1)
                expert_2(i * 2, 0)
                slots_T(i * 2 + 3, i + 1, 1)
            expert_1(TILES - 2, 0)
            expert_2(TILES - 3, 1)
            expert_1(TILES - 1, 1)
            expert_2(TILES - 2, 0)
            expert_2(TILES - 1, 1)

            def shared_w(w, k):
                return w[:, E * FC * 2 + k, :]

            def shared_1(j, par):
                first_layer(j + TILES, par, shared_w, xh_all[:, bass.ds(j * ST, ST)], xl_all[:, bass.ds(j * ST, ST)])

            def shared_2(j, par):
                if isinstance(j, int) and j < 2:
                    pe.wait_ge(s_yc, TILES - 1 + j)
                else:
                    pe.wait_ge(s_acc, j - 1)
                second_layer(j + TILES, par, shared_w)

            pe.wait_ge(s_xl, GROUPS)
            shared_1(0, 0)
            shared_1(1, 1)
            shared_2(0, 0)
            shared_1(2, 0)
            shared_2(1, 1)
            with pe.Fori(1, SHARED_TILES // 2 - 1) as i:
                shared_1(i * 2 + 1, 1)
                shared_2(i * 2, 0)
                shared_1(i * 2 + 2, 0)
                shared_2(i * 2 + 1, 1)
            shared_1(SHARED_TILES - 1, 1)
            shared_2(SHARED_TILES - 2, 0)
            shared_2(SHARED_TILES - 1, 1)


NAMES = ["x", "adj", "L0_gnn_Wq", "L0_gnn_bq", "L0_gnn_Wk", "L0_gnn_bk", "L0_gnn_Wv", "L0_gnn_bv", "L0_gnn_Wo",
         "L0_gnn_bo", "L0_gnn_gamma", "L0_gnn_beta", "L0_ffn_Wr", "L0_ffn_W1s", "L0_ffn_b1s", "L0_ffn_W2s",
         "L0_ffn_b2s", "L0_ffn_W1p", "L0_ffn_b1p", "L0_ffn_W2p", "L0_ffn_b2p"]


def kernel(**inputs):
    import numpy as np
    import concourse.bacc as bacc
    from concourse.bass_utils import run_bass_kernel_spmd

    nc = bacc.Bacc("TRN2", target_bir_lowering=False, num_devices=1)
    arrays, args = {}, []
    for name in NAMES:
        a = np.ascontiguousarray(inputs[name])
        arrays["in_" + name] = a
        args.append(nc.dram_tensor("in_" + name, a.shape, mybir.dt.from_np(a.dtype), kind="ExternalInput").ap())
    result = nc.dram_tensor("result", arrays["in_x"].shape, F32, kind="ExternalOutput").ap()
    build_program(nc, *args, result)
    return run_bass_kernel_spmd(nc, [arrays], core_ids=[0]).results[0]["result"]
```

```python
from contextlib import ExitStack

import concourse.bass as bass
from concourse import mybir

F32 = mybir.dt.float32
BF16 = mybir.dt.bfloat16
I32 = mybir.dt.int32
U32 = mybir.dt.uint32
ALU = mybir.AluOpType
ACT = mybir.ActivationFunctionType
AX_X = mybir.AxisListType.X

P = 128
EPS = 1e-5
MASKED = -1e30
NOWHERE = 1 << 20


def build_program(nc, x, adj, Wq, bq, Wk, bk, Wv, bv, Wo, bo, gamma, beta,
                  Wr, W1s, b1s, W2s, b2s, W1p, b1p, W2p, b2p, out):
    B = x.shape[0]
    HEADS = 4
    HD = P // HEADS
    E = Wr.shape[1]
    F = W1s.shape[1]
    FC = F // P
    TG = 4
    GROUPS = B // TG
    TOKENS = B * P
    W = TG * P
    ST = 2 * P
    REGION = TOKENS + ST
    TILES = 2 * TOKENS // ST + E
    IDLE_ROW = E * REGION
    SHARED_TILES = TOKENS // ST
    RW = 2 * P + 2
    SCALE = float(HD) ** -0.5
    assert GROUPS % 2 == 0 and TILES % 4 == 0

    slots = nc.dram_tensor("slots", [E * REGION + ST, RW], BF16).ap()
    pairs = nc.dram_tensor("pairs", [2 * TOKENS, P], F32).ap()

    with ExitStack() as ctx:
        def sb(name, shape, dt=F32):
            return ctx.enter_context(nc.sbuf_tensor(name, shape, dt))

        def sem(name):
            return ctx.enter_context(nc.semaphore(name))

        ident = sb("ident", [P, P])
        ident_h = sb("ident_h", [P, P], BF16)
        before = sb("before", [P, P], BF16)
        ones_h = sb("ones_h", [P, P], BF16)
        adj_i = sb("adj_i", [P, P], I32)
        mask_h = sb("mask_h", [P, P], BF16)
        w_q, w_k, w_v, w_o = sb("w_q", [P, P]), sb("w_k", [P, P]), sb("w_v", [P, P]), sb("w_o", [P, P])
        w_r = sb("w_r", [P, E])
        NB = (E + 1) * FC
        bias_rows = sb("bias_rows", [NB + 3, P])
        bias_cols = sb("bias_cols", [P, NB + 3])
        bq_scaled = sb("bq_scaled", [P, 1])
        bv_wide = sb("bv_wide", [P, P])
        bo_row, gamma_row, beta_row = sb("bo_row", [P, P]), sb("gamma_row", [P, P]), sb("beta_row", [P, P])
        b2s_row = sb("b2s_row", [P, P])
        b2_rows = sb("b2_rows", [P, E, P])
        c_row = sb("c_row", [P, P])
        minus_half = sb("minus_half", [P, TG])
        rank_i = sb("rank_i", [P, E], I32)
        rank = sb("rank", [P, E])
        base_i = sb("base_i", [P, E], I32)
        region_start = sb("region_start", [P, E])
        ids = sb("ids", [P, B], U32)
        pad_rows = sb("pad_rows", [P, 2, RW], BF16)

        x_all = sb("x_all", [P, B, P])
        xh_all = sb("xh_all", [P, TOKENS], BF16)
        xl_all = sb("xl_all", [P, TOKENS], BF16)
        w1 = sb("w1", [P, (E + 1) * FC * 2, P], BF16)
        w2 = sb("w2", [P, (E + 1) * FC * 2, P], BF16)
        delta = sb("delta", [P, B])
        weight1, weight2 = sb("weight1", [P, B]), sb("weight2", [P, B])
        base = sb("base", [P, 2, E])

        w_stage = sb("w_stage", [P, 2, F])
        stats = sb("stats", [P, 3, TG, 6])
        meanvar = sb("meanvar", [P, 3, TG, 2])
        var_eps = sb("var_eps", [P, 3, TG])
        rstd = sb("rstd", [P, 3, TG])
        shift = sb("shift", [P, 3, TG])
        xn = sb("xn", [P, W])
        xnT = sb("xnT", [P, W])
        qk = sb("qk", [P, 4, W])
        qT, kT = qk[:, 0:2, :], qk[:, 2:4, :]
        k_wide = sb("k_wide", [P, 2, TG, HEADS, P])
        v1 = sb("v1", [P, 2, TG, HEADS, HD + 1])
        neg_max = sb("neg_max", [P, 2, HEADS])
        probs = sb("probs", [P, 2, HEADS, P])
        probsT = sb("probsT", [P, 2, HEADS * P])
        inv_sum = sb("inv_sum", [P, 2, HEADS])
        attn = sb("attn", [P, 2, TG, P])
        attnT = sb("attnT", [P, W])
        proj = sb("proj", [P, TG, P])
        scaled = sb("scaled", [P, TG, P])
        x2n = sb("x2n", [P, 2, TG, P])
        x2T = sb("x2T", [P, W])
        rows = sb("rows", [P, 2, TG, RW], BF16)
        row_ids = rows[:, :, :, :].bitcast(U32)
        logits = sb("logits", [P, TG, E])
        top1, top2 = sb("top1", [P, TG]), sb("top2", [P, TG])
        first = sb("first", [P, 2, TG])
        hit = sb("hit", [P, 2, TG, E])
        hot1, hot2 = sb("hot1", [P, TG, E]), sb("hot2", [P, TG, E])
        rest = sb("rest", [P, TG, E])
        chosen = sb("chosen", [P, TG, E], BF16)
        place = sb("place", [P, TG, E])
        placed = sb("placed", [P, 2, TG, E])
        slot_f = sb("slot_f", [P, 2, TG])
        slot = sb("slot", [P, 2, 2, TG], U32)

        J = TILES
        count = sb("count", [P, E])
        ntile_i = sb("ntile_i", [P, E], I32)
        ntile = sb("ntile", [P, E])
        tri = sb("tri", [P, E, E])
        tmp88 = sb("tmp88", [P, E, E])
        upto = sb("upto", [P, E])
        jump = sb("jump", [P, E])
        j_i = sb("j_i", [P, J], I32)
        j_f = sb("j_f", [P, J])
        past = sb("past", [P, J, E])
        jumps = sb("jumps", [P, J, E])
        e_f, r_f, r_g = sb("e_f", [P, J]), sb("r_f", [P, J]), sb("r_g", [P, J])
        tile_expert = sb("tile_expert", [P, J], I32)
        tile_row = sb("tile_row", [P, J], I32)
        end_i = sb("end_i", [P, E], I32)

        xg = sb("xg", [P, 8, 2, RW], BF16)
        xg_ids = xg[:, :, :, :].bitcast(U32)
        xgT = sb("xgT", [P, 2, 2, ST], BF16)
        over = k_wide[:, :, :, :, :].rearrange("p q t h m -> p (q t h m)")
        NH = 2 * FC * ST
        hid = over[:, 0:NH].rearrange("p (q c n) -> p q c n", q=2, c=FC)
        hid_h = over[:, NH:2 * NH].bitcast(BF16).rearrange("p (q c n) -> p q c n", q=4, c=FC)
        hid_l = qk[:, :, :].rearrange("p a n -> p (a n)").bitcast(BF16).rearrange("p (q c n) -> p q c n", q=4, c=FC)
        y = w_stage[:, :, :].rearrange("p q (a b d) -> p (q a) b d", a=2, b=2)
        yg = sb("yg", [P, 3, 2, 2 * P])
        part = v1[:, :, :, :, :].rearrange("p q t h d -> p (q t h d)")[:, 0:3 * ST].rearrange(
            "p (q a d) -> p q a d", q=3, a=2)
        res = sb("res", [P, 3, 2, P])

        bank = [ctx.enter_context(nc.psum_tensor(f"bank{n}", [P, 512], F32)) for n in range(4)]
        wide = ctx.enter_context(nc.psum_tensor("wide", [P, 4, 512], F32))
        ps_s = wide[:, 0:2, :].rearrange("p q (h m) -> p q h m", h=HEADS)
        ps_av = wide[:, 2:4, 0:HEADS * (HD + 1)].rearrange("p q (h d) -> p q h d", h=HEADS)
        ps_pT, ps_o, ps_m, ps_n = bank
        ps_logit = ps_o[:, 0:TG * E].rearrange("p (t e) -> p t e", t=TG)
        ps_before = ps_o[:, 64:64 + TG * E].rearrange("p (t e) -> p t e", t=TG)
        ps_total = ps_o[:, 128:128 + E]
        ps_h = wide[:, :, :].rearrange("p b n -> p (b n)").rearrange("p (q c n) -> p q c n", q=2, c=FC)
        ps_y = bank[0][:, 0:ST].rearrange("p (a d) -> p a d", a=2)
        ps_xT = [bank[2][:, 0:ST].bitcast(BF16).rearrange("p (h n) -> p h n", h=2),
                 bank[3][:, 0:ST].bitcast(BF16).rearrange("p (h n) -> p h n", h=2)]

        s_apart = sem("s_apart")
        s_c = sem("s_c")
        s_x = sem("s_x")
        s_kz = [sem("s_kz0"), sem("s_kz1")]
        s_w = [sem("s_w0"), sem("s_w1")]
        s_pool_c = sem("s_pool_c")
        s_cast_c = sem("s_cast_c")
        s_pe_c = sem("s_pe_c")
        s_act_c = sem("s_act_c")
        s_crow = sem("s_crow")
        s_ln = sem("s_ln")
        s_var = [sem(f"s_var{n}") for n in range(3)]
        s_pl = sem("s_pl")
        s_rstd = [sem(f"s_rstd{n}") for n in range(3)]
        s_shift = {0: sem("s_shift0"), 2: sem("s_shift2")}
        s_xn = sem("s_xn")
        s_xT, s_xTc = sem("s_xT"), sem("s_xTc")
        s_q, s_k, s_v = sem("s_q"), sem("s_k"), sem("s_v")
        s_qc, s_kc, s_vc = sem("s_qc"), sem("s_kc"), sem("s_vc")
        s_score, s_max, s_exp = sem("s_score"), sem("s_max"), sem("s_exp")
        s_pT, s_pTc = sem("s_pT"), sem("s_pTc")
        s_av, s_inv, s_attn = sem("s_av"), sem("s_inv"), sem("s_attn")
        s_oT, s_oTc = sem("s_oT"), sem("s_oTc")
        s_proj, s_projc = sem("s_proj"), sem("s_projc")
        s_scaled, s_x1res = sem("s_scaled"), sem("s_x1res")
        s_xbeta = sem("s_xbeta")
        s_x2n, s_rowh, s_rowl = sem("s_x2n"), sem("s_rowh"), sem("s_rowl")
        s_x2T, s_x2Tc, s_xh, s_xl = sem("s_x2T"), sem("s_x2Tc"), sem("s_xh"), sem("s_xl")
        s_logit, s_route, s_chosen = sem("s_logit"), sem("s_route"), sem("s_chosen")
        s_before, s_place, s_slot = sem("s_before"), sem("s_place"), sem("s_slot")
        s_id = sem("s_id")
        s_sent = [sem("s_sent0"), sem("s_sent1")]
        s_wh, s_wl = sem("s_wh"), sem("s_wl")
        s_list = sem("s_list")
        s_pad = sem("s_pad")
        s_soft, s_wt = sem("s_soft"), sem("s_wt")
        s_xg = [sem(f"s_xg{n}") for n in range(8)]
        s_gT, s_gTc = sem("s_gT"), sem("s_gTc")
        s_h, s_hid = sem("s_h"), sem("s_hid")
        s_hh = sem("s_hh")
        s_hs = sem("s_hs")
        s_hl = [sem("s_hl0"), sem("s_hl1")]
        s_y, s_yc = sem("s_y"), sem("s_yc")
        s_back = [sem(f"s_back{n}") for n in range(4)]
        s_yg = [sem(f"s_yg{n}") for n in range(3)]
        s_part, s_res = sem("s_part"), sem("s_res")
        s_out = [sem(f"s_out{n}") for n in range(3)]

        UNITS = 2 * (E + 1)
        UNITS_PER_STEP = 3
        STEPS = GROUPS + 5
        LOOP_FROM = 6
        LOOP_TO = GROUPS - 2
        X_PIECES = [0, 1, 2, 4, 8, 12, GROUPS]
        EARLY = 8
        X_FROM, L_FROM, T_END = EARLY, EARLY + TILES, TILES + SHARED_TILES
        L_TILES = SHARED_TILES - EARLY
        BEGIN_AFTER = {STEPS - 4: [0, 1], STEPS - 3: [2, 3], STEPS - 2: [4, 5], STEPS - 1: [6, 7]}
        assert EARLY == 8 and L_FROM % 8 == 0 and L_TILES == 24

        def norms_before(s, order, n):
            lag = {0: -2, 1: 2, 2: 3}
            if isinstance(s, int):
                total = sum(min(max(s - lag[k], 0), GROUPS) for k in range(3))
                return total + [k for k in order if active(s, lag[k])].index(n)
            return (s + 2) + (s - 2) + (s - 3) + order.index(n)

        def apart(eng):
            eng.sem_inc(s_apart, 1)

        def steps(eng, step, tile_step=None):
            def plain(s):
                step(s, lambda k: (s + k) // 2, s % 2)
                for n in BEGIN_AFTER.get(s, ()):
                    if tile_step:
                        tile_step(n, n // 8, n % 8)

            for s in range(-2, LOOP_FROM):
                plain(s)
            with eng.Fori(0, (LOOP_TO - LOOP_FROM) // 2) as i:
                for u in range(2):
                    s = LOOP_FROM + u
                    step(i * 2 + s, lambda k: i + (s + k) // 2, s % 2)
            for s in range(LOOP_TO, STEPS):
                plain(s)

        def tiles(eng, tile_step):
            def plain(lo, hi):
                for n in range(lo, hi):
                    tile_step(n, n // 8, n % 8)

            def loop(lo, hi, unit, kind):
                with eng.Fori(lo // unit, hi // unit) as i:
                    for q in range(unit):
                        tile_step(i * unit + q, i, q, kind)

            plain(X_FROM, X_FROM + 8)
            loop(X_FROM + 8, L_FROM - 8, 8, "expert")
            plain(L_FROM - 8, L_FROM + 4)
            loop(L_FROM + 4, T_END - 4, 4, "shared")
            plain(T_END - 4, T_END + 2)

        def kind_of(n, kind):
            if not isinstance(n, int):
                return kind
            if n < 0 or n >= T_END:
                return None
            return "early" if n < X_FROM else "expert" if n < L_FROM else "shared"

        def active(s, stage):
            return not isinstance(s, int) or 0 <= s - stage < GROUPS

        def later(g, n):
            return not isinstance(g, int) or g >= n

        def graph(s, t, ahead=0):
            k = s * TG + (t + ahead - TG)
            return k if not isinstance(k, int) or 0 <= k < B else None

        block = ctx.enter_context(nc.Block())

        @block.sync
        def _(sp):
            def load_x(piece):
                lo, hi = X_PIECES[piece] * TG, X_PIECES[piece + 1] * TG
                if piece:
                    sp.wait_ge(s_x, piece * 16)
                sp.dma_start(x_all[:, lo:hi, :], x[lo:hi, :, :].rearrange("t p d -> p t d")).then_inc(s_x, 16)

            def load_unit(u):
                e, q = u // 2 - 1, u % 2
                if u >= 2:
                    sp.wait_ge(s_wl, u - 1)
                dst = w_stage[:, q, :]
                if q:
                    dst = dst.rearrange("p (c d) -> p c d", c=FC)
                    src = (W2s if e < 0 else W2p[e, :, :]).rearrange("(c p) d -> p c d", p=P)
                else:
                    src = W1s if e < 0 else W1p[e, :, :]
                sp.dma_start(dst, src).then_inc(s_w[q], 16)

            load_x(0)
            for dst, src in ((w_q, Wq), (w_k, Wk), (w_v, Wv), (w_o, Wo), (w_r, Wr), (adj_i, adj)):
                sp.dma_start(dst[:, :], src).then_inc(s_c, 16)
            for n, src in enumerate((bq, bk, bv)):
                sp.dma_start(bias_rows[NB + n:NB + n + 1, :], src.rearrange("(a p) -> a p", a=1)).then_inc(s_c, 16)
            sp.dma_start(bias_rows[0:E * FC, :], b1p.rearrange("e (c p) -> (e c) p", p=P)).then_inc(s_c, 16)
            sp.dma_start(bias_rows[E * FC:NB, :], b1s.rearrange("(c p) -> c p", p=P)).then_inc(s_c, 16)
            for dst, src in ((bo_row, bo), (gamma_row, gamma), (beta_row, beta), (b2s_row, b2s)):
                sp.dma_start(dst[:, :], src.rearrange("(a d) -> a d", a=1).broadcast_to([P, P])).then_inc(s_c, 16)
            sp.dma_start(b2_rows[:, :, :].rearrange("p e d -> p (e d)"),
                         b2p.rearrange("(a e) d -> a (e d)", a=1).broadcast_to([P, E * P])).then_inc(s_c, 16)
            load_x(1)
            load_x(2)
            load_unit(0)
            load_unit(1)
            for piece in range(3, len(X_PIECES) - 1):
                load_x(piece)

            def step(s, half, par):
                if active(s, 0):
                    sp.wait_ge(s_kc, s + 1)
                    if later(s, 2):
                        sp.wait_ge(s_score, s * TG - TG)
                    for h in range(HEADS):
                        on = slice(h * HD, (h + 1) * HD)
                        sp.dma_start(k_wide[on, par, :, h, :],
                                     kT[on, par, :].rearrange("p (t m) -> p t m", t=TG)).then_inc(s_kz[par], 16)
                if isinstance(s, int) and 0 <= s:
                    for u in range(UNITS_PER_STEP * s, UNITS_PER_STEP * (s + 1)):
                        if u + 2 < UNITS:
                            load_unit(u + 2)

            steps(sp, step)
            sp.wait_ge(s_list, 1)
            for e in range(E):
                end = sp.value_load(end_i[0:1, e:e + 1], min_val=e * REGION, max_val=e * REGION + TOKENS)
                sp.dma_start(slots[bass.ds(end, ST), :].rearrange("(a p) w -> p a w", p=P),
                             pad_rows[:, :, :]).then_inc(s_pad, 16)
            sp.dma_start(slots[IDLE_ROW:IDLE_ROW + ST, :].rearrange("(a p) w -> p a w", p=P),
                         pad_rows[:, :, :]).then_inc(s_pad, 16)
            sp.wait_ge(s_pad, 16 * (E + 1))
            sp.wait_ge(s_sent[0], 16 * TG * GROUPS)
            sp.wait_ge(s_sent[1], 16 * TG * GROUPS)
            sp.wait_ge(s_list, 3)

            def load_slots(j, i, q):
                if later(j, 8):
                    sp.wait_ge(s_gT, j - 7)
                    sp.wait_ge(s_back[q % 4], i * 64 + (q // 4 - 1) * 32)
                row = sp.value_load(tile_row[0:1, bass.ds(j, 1)], min_val=0, max_val=IDLE_ROW)
                sp.dma_start(xg[:, q, :, :],
                             slots[bass.ds(row, ST), :].rearrange("(a p) w -> p a w", p=P)).then_inc(s_xg[q], 16)

            for q in range(8):
                load_slots(q, 0, q)
            with sp.Fori(1, TILES // 8) as i:
                for q in range(8):
                    load_slots(i * 8 + q, i, q)

            for q in range(4):
                sp.wait_ge(s_back[q], 32 * (TILES // 4))

            def load_pairs(j, q):
                sp.dma_start(yg[:, q, :, :], pairs[bass.ds(j * (2 * ST), 2 * ST), :].rearrange(
                    "(a p k) d -> p a (k d)", p=P, k=2)).then_inc(s_yg[q], 16)

            def store(j, q):
                sp.wait_ge(s_res, j + 1)
                sp.dma_start(out[bass.ds(j * 2, 2), :, :].rearrange("a p d -> p a d"),
                             res[:, q, :, :]).then_inc(s_out[q], 16)

            LAST = SHARED_TILES - 5
            for q in range(3):
                load_pairs(q, q)
            with sp.Fori(0, LAST // 3) as i:
                for q in range(3):
                    store(i * 3 + q, q)
                    load_pairs(i * 3 + (q + 3), q)
            for j in range(LAST // 3 * 3, SHARED_TILES):
                store(j, j % 3)
                if j + 3 < SHARED_TILES:
                    load_pairs(j + 3, j % 3)
            for q in range(3):
                sp.wait_ge(s_out[q], 16 * len(range(q, SHARED_TILES, 3)))

        @block.gpsimd
        def _(gp):
            nc.gpsimd.memset(ident[:, :], 0.0).then_inc(s_pool_c, 1)
            nc.gpsimd.memset(ones_h[:, :], 1.0).then_inc(s_pool_c, 1)
            nc.gpsimd.memset(tri[:, :, :], 1.0).then_inc(s_pool_c, 1)
            nc.gpsimd.memset(minus_half[:, :], -0.5).then_inc(s_pool_c, 1)
            nc.gpsimd.memset(v1[:, :, :, :, :], 1.0).then_inc(s_pool_c, 1)
            nc.gpsimd.memset(pad_rows[:, :, :], 0.0).then_inc(s_pool_c, 1)
            nc.gpsimd.iota(rank_i[:, :], [[-1, E]], base=E, channel_multiplier=0).then_inc(s_pool_c, 1)
            nc.gpsimd.iota(j_i[:, :], [[1, J]], base=0, channel_multiplier=0).then_inc(s_pool_c, 1)
            nc.gpsimd.iota(base_i[:, :], [[REGION, E]], base=0, channel_multiplier=0).then_inc(s_pool_c, 1)
            nc.gpsimd.iota(ids[:, :], [[2 * P, B]], base=0, channel_multiplier=2).then_inc(s_pool_c, 1)
            gp.wait_ge(s_pool_c, 10)
            nc.gpsimd.affine_select(out=ident[:, :], in_=ident[:, :], compare_op=ALU.not_equal, fill=1.0,
                                    base=0, pattern=[[-1, P]], channel_multiplier=1).then_inc(s_pool_c, 1)
            nc.gpsimd.affine_select(out=before[:, :], in_=ones_h[:, :], compare_op=ALU.is_gt, fill=0.0,
                                    base=0, pattern=[[1, P]], channel_multiplier=-1).then_inc(s_pool_c, 1)
            nc.gpsimd.affine_select(out=tri[:, :, :], in_=tri[:, :, :], compare_op=ALU.is_ge, fill=0.0,
                                    base=0, pattern=[[1, E], [-1, E]], channel_multiplier=0).then_inc(s_pool_c, 1)
            nc.gpsimd.iota(pad_rows[:, :, :].bitcast(U32)[:, :, P:P + 1], [[0, 2], [0, 1]], base=NOWHERE,
                           channel_multiplier=0).then_inc(s_pool_c, 1)
            nc.gpsimd.memset(k_wide[:, :, :, :, :], 0.0).then_inc(s_pool_c, 1)

            ORDER = (2, 1, 0)

            def inv_std(n, s, g):
                gp.wait_ge(s_var[n], g + 1)
                apart(gp)
                nc.gpsimd.tensor_scalar(var_eps[:, n, :], meanvar[:, n, :, 1], EPS, None, ALU.add).then_inc(s_pl, 1)
                if later(g, 1):
                    gp.wait_ge((s_xn, s_x1res, s_x2n)[n], g)
                gp.wait_ge(s_pl, norms_before(s, ORDER, n) + 1)
                nc.gpsimd.tensor_tensor(rstd[:, n, :], var_eps[:, n, :], minus_half[:, :],
                                        ALU.pow).then_inc(s_rstd[n], 1)

            def add_beta(g):
                gp.wait_ge(s_xn, g + 1)
                nc.gpsimd.tensor_tensor(x_all[:, bass.ds(g * TG, TG), :], x_all[:, bass.ds(g * TG, TG), :],
                                        beta_row[:, None, :].broadcast_to([P, TG, P]), ALU.add).then_inc(s_xbeta, 1)

            def split_unit(u):
                block_ = (E if u < 2 else u // 2 - 1) * FC * 2
                dst = (w2 if u % 2 else w1)[:, block_:block_ + FC * 2, :].rearrange("p (c h) d -> p c h d", h=2)
                src = w_stage[:, u % 2, :].rearrange("p (c d) -> p c d", c=FC)
                gp.wait_ge(s_w[u % 2], (u // 2 + 1) * 16)
                nc.gpsimd.tensor_copy(dst[:, :, 0, :], src).then_inc(s_wh, 1)
                gp.wait_ge(s_wh, u + 1)
                nc.gpsimd.tensor_tensor(dst[:, :, 1, :], src, dst[:, :, 0, :], ALU.subtract).then_inc(s_wl, 1)

            def send(par, choice, lo, hi):
                for t in range(lo, hi):
                    nc.gpsimd.indirect_dma_start(
                        out=slots[:, :], out_offset=bass.IndirectOffsetOnAxis(ap=slot[:, par, choice, t:t + 1], axis=0),
                        in_=rows[:, par, t, :], in_offset=None).then_inc(s_sent[choice], 16)

            def low_part(g):
                gp.wait_ge(s_xh, g + 1)
                nc.gpsimd.tensor_tensor(xl_all[:, bass.ds(g * W, W)], x2T[:, :], xh_all[:, bass.ds(g * W, W)],
                                        ALU.subtract).then_inc(s_xl, 1)

            def step(s, half, par):
                g, q = s - 5, 1 - par
                if active(s, 5):
                    nc.gpsimd.tensor_copy(row_ids[:, q, :, P], ids[:, bass.ds(g * TG, TG)]).then_inc(s_id, 1)
                    gp.wait_ge(s_slot, g + 1)
                    gp.wait_ge(s_rowl, g + 1)
                    gp.wait_ge(s_id, g * 2 + 1)
                    apart(gp)
                    send(q, 0, 0, 3)
                if active(s, 3):
                    inv_std(2, s, s - 3)
                if active(s, 5):
                    send(q, 0, 3, 4)
                if active(s, 4):
                    low_part(s - 4)
                if active(s, -1):
                    add_beta(s + 1)
                if isinstance(s, int) and 0 <= s:
                    for u in range(UNITS_PER_STEP * s, UNITS_PER_STEP * (s + 1)):
                        if u < UNITS:
                            split_unit(u)
                if active(s, 5):
                    gp.wait_ge(s_sent[0], (g + 1) * (16 * TG))
                    apart(gp)
                    nc.gpsimd.tensor_scalar(row_ids[:, q, :, P], row_ids[:, q, :, P], 1, None,
                                            ALU.add).then_inc(s_id, 1)
                    gp.wait_ge(s_id, g * 2 + 2)
                    apart(gp)
                    send(q, 1, 0, TG)
                if active(s, 2):
                    inv_std(1, s, s - 2)
                if active(s, -2):
                    inv_std(0, s, s + 2)

            steps(gp, step)

            def tile_step(n, i, q, kind=None):
                kind2 = kind_of(n - 2, kind)
                if kind2 == "expert":
                    gp.wait_ge(s_yc, n - 1)
                    apart(gp)
                    for a in range(2):
                        nc.gpsimd.indirect_dma_start(
                            out=pairs[:, :],
                            out_offset=bass.IndirectOffsetOnAxis(ap=xg_ids[:, (q - 2) % 8, a, P:P + 1], axis=0),
                            in_=y[:, (q - 2) % 4, a, :], in_offset=None, bounds_check=2 * TOKENS - 1,
                            oob_is_err=False).then_inc(s_back[(q - 2) % 4], 16)
                if kind_of(n, kind) == "shared":
                    gp.wait_ge(s_hs, n * 2 + (2 - 2 * L_FROM))
                    if isinstance(n, int) and n == L_FROM:
                        gp.wait_ge(s_hl[1], n)
                    if later(n, 4):
                        gp.wait_ge(s_y, n - 3)
                    nc.gpsimd.tensor_tensor(hid_l[:, q % 4, 2:4, :], hid[:, q % 2, 2:4, :], hid_h[:, q % 4, 2:4, :],
                                            ALU.subtract).then_inc(s_hl[1], 1)

            tiles(gp, tile_step)

        @block.scalar
        def _(act):
            def copy(out, in_, **kw):
                return nc.scalar.activation(out, in_, ACT.Identity, **kw)

            act.wait_ge(s_pe_c, 1)
            copy(bias_cols[:, :], ps_m[:, 0:NB + 3]).then_inc(s_act_c, 1)
            act.wait_ge(s_act_c, 1)
            nc.scalar.mul(bq_scaled[:, :], bias_cols[:, NB:NB + 1], SCALE).then_inc(s_act_c, 1)
            act.wait_ge(s_act_c, 2)

            def tile_of(n):
                return x_all[:, bass.ds(n, 1), :].rearrange("p a d -> p (a d)")

            def x_normed(g):
                act.wait_ge(s_shift[0], g + 1)
                if later(g, 1):
                    act.wait_ge(s_xT, g)
                for t in range(TG):
                    last = copy(xn[:, t * P:(t + 1) * P], tile_of(g * TG + t), bias=shift[:, 0, t:t + 1],
                                scale=rstd[:, 0, t:t + 1])
                last.then_inc(s_xn, 1)

            def x1_normed(g, par):
                act.wait_ge(s_shift[2], g + 1)
                if later(g, 2):
                    act.wait_ge(s_rowl, g - 1)
                for t in range(TG):
                    last = copy(x2n[:, par, t, :], tile_of(g * TG + t), bias=shift[:, 2, t:t + 1],
                                scale=rstd[:, 2, t:t + 1])
                last.then_inc(s_x2n, 1)

            def copy_xT(g):
                act.wait_ge(s_xT, g + 1)
                copy(xnT[:, :], ps_m[:, :]).then_inc(s_xTc, 1)

            def copy_qk(g, half, par):
                act.wait_ge(s_q, g + 1)
                copy(qT[:, par, :], ps_n[:, :], bias=bq_scaled[:, 0:1], scale=SCALE).then_inc(s_qc, 1)
                act.wait_ge(s_k, g + 1)
                if later(g, 2):
                    act.wait_ge(s_kz[par], half * 64)
                copy(kT[:, par, :], ps_m[:, :], bias=bias_cols[:, NB + 1:NB + 2]).then_inc(s_kc, 1)

            def copy_v(g, par):
                act.wait_ge(s_v, g + 1)
                copy(v1[:, par, :, :, 0:HD],
                     ps_n[:, :].rearrange("p (t h d) -> p t h d", t=TG, h=HEADS)).then_inc(s_vc, 1)

            def exponentials(k, q):
                act.wait_ge(s_max, k + 1)
                for h in range(HEADS):
                    last = nc.scalar.activation(probs[:, q, h, :], ps_s[:, q, h, :], ACT.Exp,
                                                bias=neg_max[:, q, h:h + 1])
                last.then_inc(s_exp, 1)

            def copy_probsT(k, q):
                act.wait_ge(s_pT, k + 1)
                copy(probsT[:, q, :], ps_pT[:, :]).then_inc(s_pTc, 1)

            def copy_attnT(g):
                act.wait_ge(s_oT, g + 1)
                copy(attnT[:, :], ps_m[:, :]).then_inc(s_oTc, 1)

            def row_high(g, par):
                if later(g, 2):
                    act.wait_ge(s_sent[1], (g - 1) * (16 * TG))
                copy(rows[:, par, :, 0:P], x2n[:, par, :, :]).then_inc(s_rowh, 1)

            def copy_x2T(g):
                act.wait_ge(s_x2T, g + 1)
                if later(g, 1):
                    act.wait_ge(s_xl, g)
                    act.wait_ge(s_logit, g)
                copy(x2T[:, :], ps_m[:, :]).then_inc(s_x2Tc, 1)
                copy(xh_all[:, bass.ds(g * W, W)], ps_m[:, :]).then_inc(s_xh, 1)

            def step(s, half, par):
                for t in range(TG):
                    if graph(s, t) is not None:
                        copy_probsT(graph(s, t), t % 2)
                    if t == 0 and active(s, 0):
                        copy_qk(s, half(0), par)
                    if graph(s, t, 2) is not None:
                        exponentials(graph(s, t, 2), t % 2)
                    if t == 0 and active(s, -1):
                        x_normed(s + 1)
                    if t == 1:
                        if active(s, 0):
                            copy_v(s, par)
                        if active(s, 4):
                            row_high(s - 4, par)
                        if active(s, 2):
                            copy_attnT(s - 2)
                    if t == 2:
                        if active(s, 3):
                            x1_normed(s - 3, 1 - par)
                        if active(s, -1):
                            copy_xT(s + 1)
                    if t == 3 and active(s, 3):
                        copy_x2T(s - 3)

            def tile_step(n, i, q, kind=None):
                kind0, kind1 = kind_of(n, kind), kind_of(n + 1, kind)
                par = q % 2
                if isinstance(n, int) and n == X_FROM:
                    act.wait_ge(s_gT, 1)
                    copy(xgT[:, 0, :, :], ps_xT[0]).then_inc(s_gTc, 1)
                if kind1 == "expert" and later(n, X_FROM):
                    j = n - (X_FROM - 1)
                    act.wait_ge(s_gT, j + 1)
                    if later(j, 2):
                        act.wait_ge(s_h, n * 2 - 2)
                    copy(xgT[:, 1 - par, :, :], ps_xT[1 - par]).then_inc(s_gTc, 1)
                if kind0 is None:
                    return
                if kind0 == "expert":
                    e = act.value_load(tile_expert[0:1, bass.ds(n - X_FROM, 1)], min_val=0, max_val=E - 1)
                for c in range(FC):
                    if c % 2 == 0:
                        act.wait_ge(s_h, n * 2 + (c // 2 + 1))
                        if later(n, 2):
                            act.wait_ge(s_hl[c // 2], n - 1)
                    col = bass.ds(e * FC + c, 1) if kind0 == "expert" else slice(E * FC + c, E * FC + c + 1)
                    nc.scalar.activation(hid[:, par, c, :], ps_h[:, par, c, :], ACT.Gelu,
                                         bias=bias_cols[:, col]).then_inc(s_hid, 1)
                if kind0 == "shared":
                    for b in range(2):
                        act.wait_ge(s_hid, n * 4 + (2 * b + 2))
                        if b == 0:
                            act.wait_ge(s_y, n - 3)
                        copy(hid_h[:, q % 4, 2 * b:2 * b + 2, :], hid[:, par, 2 * b:2 * b + 2, :]).then_inc(s_hs, 1)

            steps(act, step, tile_step)
            act.wait_ge(s_list, 3)
            nc.scalar.activation(weight2[:, :], delta[:, :], ACT.Exp).then_inc(s_soft, 1)
            tiles(act, tile_step)

        @block.vector
        def _(dve):
            dve.wait_ge(s_c, 16 * 16)
            dve.wait_ge(s_pool_c, 15)
            nc.vector.tensor_copy(ident_h[:, :], ident[:, :]).then_inc(s_cast_c, 1)
            nc.vector.tensor_scalar(mask_h[:, :], adj_i[:, :], 0, MASKED, ALU.is_equal, ALU.mult).then_inc(s_cast_c, 1)
            nc.vector.tensor_copy(rank[:, :], rank_i[:, :]).then_inc(s_cast_c, 1)
            nc.vector.tensor_copy(region_start[:, :], base_i[:, :]).then_inc(s_cast_c, 1)
            nc.vector.tensor_copy(base[:, 0, :], base_i[:, :]).then_inc(s_cast_c, 1)
            nc.vector.tensor_copy(j_f[:, :], j_i[:, :]).then_inc(s_cast_c, 1)
            nc.vector.tensor_tensor(b2_rows[:, :, :], b2_rows[:, :, :], b2s_row[:, None, :].broadcast_to([P, E, P]),
                                    ALU.add).then_inc(s_cast_c, 1)
            dve.wait_ge(s_act_c, 1)
            nc.vector.tensor_copy(bv_wide[:, :], bias_cols[:, NB + 2:NB + 3].broadcast_to([P, P])).then_inc(s_cast_c, 1)
            dve.wait_ge(s_pe_c, 2)
            nc.vector.tensor_tensor(c_row[:, :], ps_n[:, 0:P], bo_row[:, :], ALU.add).then_inc(s_crow, 1)
            dve.wait_ge(s_crow, 1)

            ORDER = (2, 0, 1)

            def statistics(n, s, g, src):
                if later(g, 1):
                    dve.wait_ge(s_rstd[n], g)
                apart(dve)
                for t in range(TG):
                    nc.vector.bn_stats(stats[:, n, t, :], src(t)).then_inc(s_ln, 1)
                dve.wait_ge(s_ln, (norms_before(s, ORDER, n) + 1) * TG)
                apart(dve)
                for t in range(TG):
                    last = nc.vector.bn_aggr(meanvar[:, n, t, :], stats[:, n, t, :])
                last.then_inc(s_var[n], 1)

            def make_shift(n, g):
                dve.wait_ge(s_rstd[n], g + 1)
                nc.vector.scalar_tensor_tensor(shift[:, n, :], meanvar[:, n, :, 0], -1.0, rstd[:, n, :],
                                               ALU.mult, ALU.mult).then_inc(s_shift[n], 1)

            def max_rows(k, q):
                dve.wait_ge(s_score, k + 1)
                if later(k, 2):
                    dve.wait_ge(s_exp, k - 1)
                nc.vector.tensor_reduce(neg_max[:, q, :], ps_s[:, q, :, :], AX_X, ALU.max,
                                        negate=True).then_inc(s_max, 1)

            def normalise(k, par, t):
                dve.wait_ge(s_av, k + 1)
                nc.vector.reciprocal(inv_sum[:, t % 2, :], ps_av[:, t % 2, :, HD]).then_inc(s_inv, 1)
                dve.wait_ge(s_inv, k + 1)
                nc.vector.tensor_tensor(attn[:, par, t, :].rearrange("p (h d) -> p h d", h=HEADS),
                                        ps_av[:, t % 2, :, 0:HD],
                                        inv_sum[:, t % 2, :].unsqueeze(2).broadcast_to([P, HEADS, HD]),
                                        ALU.mult).then_inc(s_attn, 1)

            def route_1(g):
                o = g * 11
                k = [0]

                def own(ins):
                    k[0] += 1
                    ins.then_inc(s_route, 1)
                    dve.wait_ge(s_route, o + k[0])

                rk = rank[:, None, :].broadcast_to([P, TG, E])
                dve.wait_ge(s_logit, g + 1)
                own(nc.vector.tensor_copy(logits[:, :, :], ps_logit))
                own(nc.vector.tensor_reduce(top1[:, :], logits[:, :, :], AX_X, ALU.max))
                own(nc.vector.tensor_tensor(hit[:, 0, :, :], logits[:, :, :],
                                            top1[:, :].unsqueeze(2).broadcast_to([P, TG, E]), ALU.is_equal))
                own(nc.vector.tensor_tensor(hit[:, 1, :, :], hit[:, 0, :, :], rk, ALU.mult))
                own(nc.vector.tensor_reduce(first[:, 0, :], hit[:, 1, :, :], AX_X, ALU.max))
                own(nc.vector.tensor_tensor(hot1[:, :, :], rk, first[:, 0, :].unsqueeze(2).broadcast_to([P, TG, E]),
                                            ALU.is_equal))
                own(nc.vector.scalar_tensor_tensor(rest[:, :, :], hot1[:, :, :], MASKED, logits[:, :, :],
                                                   ALU.mult, ALU.add))
                own(nc.vector.tensor_reduce(top2[:, :], rest[:, :, :], AX_X, ALU.max))
                nc.vector.tensor_tensor(delta[:, bass.ds(g * TG, TG)], top2[:, :], top1[:, :], ALU.subtract)
                own(nc.vector.tensor_tensor(hit[:, 0, :, :], rest[:, :, :],
                                            top2[:, :].unsqueeze(2).broadcast_to([P, TG, E]), ALU.is_equal))
                own(nc.vector.tensor_tensor(hit[:, 1, :, :], hit[:, 0, :, :], rk, ALU.mult))
                own(nc.vector.tensor_reduce(first[:, 1, :], hit[:, 1, :, :], AX_X, ALU.max))
                nc.vector.tensor_tensor(hot2[:, :, :], rk, first[:, 1, :].unsqueeze(2).broadcast_to([P, TG, E]),
                                        ALU.is_equal).then_inc(s_chosen, 1)
                dve.wait_ge(s_chosen, g * 2 + 1)
                nc.vector.tensor_tensor(chosen[:, :, :], hot1[:, :, :], hot2[:, :, :], ALU.add).then_inc(s_chosen, 1)

            def route_2(g, par):
                o = g * 5
                dve.wait_ge(s_before, g + 1)
                nc.vector.tensor_tensor(place[:, :, :], ps_before, base[:, par, None, :].broadcast_to([P, TG, E]),
                                        ALU.add).then_inc(s_place, 1)
                nc.vector.tensor_tensor(base[:, 1 - par, :], ps_total, base[:, par, :], ALU.add).then_inc(s_place, 1)
                dve.wait_ge(s_place, o + 2)
                nc.vector.tensor_tensor(placed[:, 0, :, :], place[:, :, :], hot1[:, :, :], ALU.mult).then_inc(s_place, 1)
                nc.vector.tensor_tensor(placed[:, 1, :, :], place[:, :, :], hot2[:, :, :], ALU.mult).then_inc(s_place, 1)
                dve.wait_ge(s_place, o + 4)
                nc.vector.tensor_reduce(slot_f[:, :, :], placed[:, :, :, :], AX_X, ALU.add).then_inc(s_place, 1)
                dve.wait_ge(s_place, o + 5)
                if later(g, 2):
                    dve.wait_ge(s_sent[1], (g - 1) * (16 * TG))
                nc.vector.tensor_copy(slot[:, par, :, :], slot_f[:, :, :]).then_inc(s_slot, 1)

            def tile_of(n):
                return x_all[:, bass.ds(n, 1), :].rearrange("p a d -> p (a d)")

            def x_statistics(s, g):
                piece = max(n for n in range(len(X_PIECES) - 1) if not isinstance(g, int) or X_PIECES[n] <= g)
                dve.wait_ge(s_x, 16 * (piece + 1))
                statistics(0, s, g, lambda t: tile_of(g * TG + t))

            def projection(s, g):
                dve.wait_ge(s_proj, g + 1)
                if later(g, 1):
                    dve.wait_ge(s_scaled, g)
                nc.vector.tensor_tensor(proj[:, :, :], ps_n[:, :].rearrange("p (t d) -> p t d", t=TG),
                                        c_row[:, None, :].broadcast_to([P, TG, P]), ALU.add).then_inc(s_projc, 1)
                dve.wait_ge(s_projc, g + 1)
                statistics(1, s, g, lambda t: proj[:, t, :])

            def residual(s, g):
                dve.wait_ge(s_var[1], g + 1)
                if later(g, 1):
                    dve.wait_ge(s_x1res, g)
                for t in range(TG):
                    last = nc.vector.scalar_tensor_tensor(scaled[:, t, :], proj[:, t, :], meanvar[:, 1, t, 0:1],
                                                          gamma_row[:, :], ALU.subtract, ALU.mult)
                last.then_inc(s_scaled, 1)
                dve.wait_ge(s_scaled, g + 1)
                dve.wait_ge(s_rstd[1], g + 1)
                dve.wait_ge(s_xbeta, g + 1)
                for t in range(TG):
                    last = nc.vector.scalar_tensor_tensor(tile_of(g * TG + t), scaled[:, t, :], rstd[:, 1, t:t + 1],
                                                          tile_of(g * TG + t), ALU.mult, ALU.add)
                last.then_inc(s_x1res, 1)
                dve.wait_ge(s_x1res, g + 1)
                statistics(2, s, g, lambda t: tile_of(g * TG + t))

            def row_low(g, par):
                dve.wait_ge(s_rowh, g + 1)
                nc.vector.tensor_tensor(rows[:, par, :, P:2 * P], x2n[:, par, :, :], rows[:, par, :, 0:P],
                                        ALU.subtract).then_inc(s_rowl, 1)

            def step(s, half, par):
                for t in range(TG):
                    if graph(s, t, -1) is not None:
                        normalise(graph(s, t, -1), par if t == 0 else 1 - par, (t - 1) % TG)
                    if graph(s, t, 2) is not None:
                        max_rows(graph(s, t, 2), t % 2)
                    if t == 0:
                        if active(s, -1):
                            make_shift(0, s + 1)
                        if active(s, 3):
                            residual(s, s - 3)
                    if t == 1 and active(s, 4):
                        route_1(s - 4)
                    if t == 2:
                        if active(s, 3):
                            make_shift(2, s - 3)
                        if active(s, 4):
                            row_low(s - 4, par)
                        if active(s, -2):
                            x_statistics(s, s + 2)
                    if t == 3:
                        if active(s, 4):
                            route_2(s - 4, par)
                        if active(s, 2):
                            projection(s, s - 2)

            def tile_step(n, i, q, kind=None):
                kind0, kind2 = kind_of(n, kind), kind_of(n - 2, kind)
                par = q % 2
                for b in range(2):
                    half_ = slice(2 * b, 2 * b + 2)
                    if kind0 in ("early", "expert"):
                        dve.wait_ge(s_hid, n * 4 + (2 * b + 2))
                        if b == 0 and later(n, 4):
                            dve.wait_ge(s_y, n - 3)
                        nc.vector.tensor_copy(hid_h[:, q % 4, half_, :], hid[:, par, half_, :]).then_inc(s_hh, 1)
                    if kind0 in ("early", "expert") or (kind0 == "shared" and b == 0):
                        if kind0 == "shared":
                            dve.wait_ge(s_hs, n * 2 + (b + 1 - 2 * L_FROM))
                        else:
                            dve.wait_ge(s_hh, n * 2 + (b + 1))
                        nc.vector.tensor_tensor(hid_l[:, q % 4, half_, :], hid[:, par, half_, :],
                                                hid_h[:, q % 4, half_, :],
                                                ALU.subtract).then_inc(s_hl[b], 1)
                if kind2 == "expert":
                    j = n - (2 + X_FROM)
                    e = dve.value_load(tile_expert[0:1, bass.ds(j, 1)], min_val=0, max_val=E - 1)
                    dve.wait_ge(s_y, n - 1)
                    if later(j, 4):
                        dve.wait_ge(s_back[(q - 2) % 4], i * 64 + ((q - 2 - X_FROM) // 4) * 32)
                    nc.vector.tensor_tensor(y[:, (q - 2) % 4, :, :], ps_y,
                                            b2_rows[:, bass.ds(e, 1), :].broadcast_to([P, 2, P]),
                                            ALU.add).then_inc(s_yc, 1)
                elif kind2:
                    tile = n - 2 if kind2 == "early" else n - (2 + TILES)
                    dve.wait_ge(s_y, n - 1)
                    nc.vector.tensor_tensor(x_all[:, bass.ds(tile * 2, 2), :], ps_y,
                                            x_all[:, bass.ds(tile * 2, 2), :], ALU.add).then_inc(s_yc, 1)
                if isinstance(n, int):
                    ready = {T_END - 4: (24, 25), T_END - 3: (26,), T_END - 2: (27, 28), T_END - 1: (29,),
                             T_END: (30,), T_END + 1: (31,)}
                    for j in ready.get(n, ()):
                        finish(j, j // 3, j % 3)
                elif kind == "shared":
                    first_i = (L_FROM + 4) // 4
                    for u in ((0, 1), (2,), (3, 4), (5,))[q]:
                        finish(i * 6 + (u - 6 * first_i), i * 2 + (u // 3 - 2 * first_i), u % 3)

            def finish(j, third, q):
                dve.wait_ge(s_yg[q], third * 16 + 16)
                dve.wait_ge(s_yc, j + 1 if isinstance(j, int) and j < EARLY else j + (TILES + 1))
                for a in range(2):
                    last = nc.vector.scalar_tensor_tensor(part[:, q, a, :], yg[:, q, a, 0:P],
                                                          weight1[:, bass.ds(j * 2 + a, 1)], tile_of(j * 2 + a),
                                                          ALU.mult, ALU.add)
                last.then_inc(s_part, 1)
                dve.wait_ge(s_part, j + 1)
                if later(third, 1):
                    dve.wait_ge(s_out[q], third * 16)
                for a in range(2):
                    last = nc.vector.scalar_tensor_tensor(res[:, q, a, :], yg[:, q, a, P:2 * P],
                                                          weight2[:, bass.ds(j * 2 + a, 1)], part[:, q, a, :],
                                                          ALU.mult, ALU.add)
                last.then_inc(s_res, 1)

            steps(dve, step, tile_step)

            k = [0]

            def own(ins):
                k[0] += 1
                ins.then_inc(s_wt, 1)
                dve.wait_ge(s_wt, k[0])

            end = base[:, GROUPS % 2, :]
            nc.vector.tensor_copy(end_i[:, :], end).then_inc(s_list, 1)
            own(nc.vector.tensor_tensor(count[:, :], end, region_start[:, :], ALU.subtract))
            own(nc.vector.tensor_scalar(ntile_i[:, :], count[:, :], ST / 2 - 0.5, 1.0 / ST, ALU.add, ALU.mult))
            own(nc.vector.tensor_copy(ntile[:, :], ntile_i[:, :]))
            own(nc.vector.tensor_tensor(tmp88[:, :, :], tri[:, :, :], ntile[:, None, :].broadcast_to([P, E, E]),
                                        ALU.mult))
            own(nc.vector.tensor_reduce(upto[:, :], tmp88[:, :, :], AX_X, ALU.add))
            own(nc.vector.tensor_scalar(jump[:, :], ntile[:, :], -float(ST), float(REGION), ALU.mult, ALU.add))
            own(nc.vector.tensor_tensor(past[:, :, :], j_f[:, :].unsqueeze(2).broadcast_to([P, J, E]),
                                        upto[:, None, :].broadcast_to([P, J, E]), ALU.is_ge))
            own(nc.vector.tensor_tensor(jumps[:, :, :], past[:, :, :], jump[:, None, :].broadcast_to([P, J, E]),
                                        ALU.mult))
            own(nc.vector.tensor_reduce(e_f[:, :], past[:, :, :], AX_X, ALU.add))
            own(nc.vector.tensor_reduce(r_f[:, :], jumps[:, :, :], AX_X, ALU.add))
            own(nc.vector.scalar_tensor_tensor(r_g[:, :], j_f[:, :], float(ST), r_f[:, :], ALU.mult, ALU.add))
            nc.vector.tensor_scalar(tile_expert[:, :], e_f[:, :], float(E - 1), None, ALU.min).then_inc(s_list, 1)
            nc.vector.tensor_scalar(tile_row[:, :], r_g[:, :], float(IDLE_ROW), None, ALU.min).then_inc(s_list, 1)
            dve.wait_ge(s_soft, 1)
            own(nc.vector.tensor_scalar(weight1[:, :], weight2[:, :], 1.0, None, ALU.add))
            own(nc.vector.reciprocal(weight1[:, :], weight1[:, :]))
            own(nc.vector.tensor_tensor(weight2[:, :], weight2[:, :], weight1[:, :], ALU.mult))
            dve.wait_ge(s_list, 3)
            tiles(dve, tile_step)

        @block.tensor
        def _(pe):
            pe.wait_ge(s_c, 16 * 16)
            pe.wait_ge(s_pool_c, 15)
            nc.tensor.transpose(ps_m[:, 0:NB + 3], bias_rows[:, :], ident[0:NB + 3, 0:NB + 3]).then_inc(s_pe_c, 1)
            pe.wait_ge(s_cast_c, 8)
            nc.tensor.matmul(ps_n[:, 0:P], bv_wide[:, :], w_o[:, :], start=True, stop=True).then_inc(s_pe_c, 1)
            pe.wait_ge(s_crow, 1)

            M_USERS = [(s_kc, 0), (s_oTc, 2), (s_xTc, -1), (s_xh, 3)]
            N_USERS = [(s_qc, 0), (s_vc, 0), (s_projc, 2)]

            def wait_free(users, s, at):
                for back in range(len(users)):
                    at -= 1
                    earlier = 1 if at < 0 else 0
                    sem_, lag = users[at]
                    if not isinstance(s, int):
                        pe.wait_ge(sem_, s - (lag + earlier - 1))
                        return
                    if active(s - earlier, lag):
                        pe.wait_ge(sem_, s - (lag + earlier - 1))
                        return

            def transpose_x(s):
                g = s + 1
                pe.wait_ge(s_xn, g + 1)
                wait_free(M_USERS, s, 2)
                for t in range(TG):
                    last = nc.tensor.transpose(ps_m[:, t * P:(t + 1) * P], xn[:, t * P:(t + 1) * P], ident[:, :])
                last.then_inc(s_xT, 1)

            def project_qk(s):
                pe.wait_ge(s_xTc, s + 1)
                wait_free(N_USERS, s, 0)
                nc.tensor.matmul(ps_n[:, :], w_q[:, :], xnT[:, :], start=True, stop=True).then_inc(s_q, 1)
                wait_free(M_USERS, s, 0)
                nc.tensor.matmul(ps_m[:, :], w_k[:, :], xnT[:, :], start=True, stop=True).then_inc(s_k, 1)

            def project_v(s):
                wait_free(N_USERS, s, 1)
                for t in range(TG):
                    last = nc.tensor.matmul(ps_n[:, t * P:(t + 1) * P], xnT[:, t * P:(t + 1) * P], w_v[:, :],
                                            start=True, stop=True)
                last.then_inc(s_v, 1)

            def scores(k, half, par, t, q):
                if t == 0:
                    pe.wait_ge(s_kz[par], half * 64 + 64)
                if later(k, 2):
                    pe.wait_ge(s_exp, k - 1)
                nc.tensor.matmul(ps_s[:, q, :, :], ident_h[:, :], mask_h[:, None, :].broadcast_to([P, HEADS, P]),
                                 start=True, stop=False)
                nc.tensor.matmul(ps_s[:, q, :, :], qT[:, par, t * P:(t + 1) * P], k_wide[:, par, t, :, :],
                                 start=False, stop=True).then_inc(s_score, 1)

            def transpose_probs(k, q):
                pe.wait_ge(s_exp, k + 1)
                if later(k, 1):
                    pe.wait_ge(s_pTc, k)
                for h in range(HEADS):
                    last = nc.tensor.transpose(ps_pT[:, h * P:(h + 1) * P], probs[:, q, h, :], ident[:, :])
                last.then_inc(s_pT, 1)

            def attend(k, g, par, t):
                pe.wait_ge(s_pTc, k + 1)
                if t == 0:
                    pe.wait_ge(s_vc, g + 1)
                if later(k, 2):
                    pe.wait_ge(s_attn, k - 1)
                for h in range(HEADS):
                    last = nc.tensor.matmul(ps_av[:, t % 2, h, :], probsT[:, t % 2, h * P:(h + 1) * P],
                                            v1[:, par, t, h, :], start=True, stop=True)
                last.then_inc(s_av, 1)

            def transpose_attn(s, par):
                pe.wait_ge(s_attn, s * TG - TG)
                wait_free(M_USERS, s, 1)
                for t in range(TG):
                    last = nc.tensor.transpose(ps_m[:, t * P:(t + 1) * P], attn[:, par, t, :], ident[:, :])
                last.then_inc(s_oT, 1)

            def project_out(s):
                pe.wait_ge(s_oTc, s - 1)
                wait_free(N_USERS, s, 2)
                for t in range(TG):
                    last = nc.tensor.matmul(ps_n[:, t * P:(t + 1) * P], attnT[:, t * P:(t + 1) * P], w_o[:, :],
                                            start=True, stop=True)
                last.then_inc(s_proj, 1)

            def count_before(g):
                pe.wait_ge(s_chosen, g * 2 + 2)
                for t in range(TG):
                    nc.tensor.matmul(ps_before[:, t, :], before[:, :], chosen[:, t, :], start=True, stop=t == 0)
                    for u in range(t):
                        nc.tensor.matmul(ps_before[:, t, :], ones_h[:, :], chosen[:, u, :], start=False,
                                         stop=u == t - 1)
                for t in range(TG):
                    last = nc.tensor.matmul(ps_total, ones_h[:, :], chosen[:, t, :], start=t == 0, stop=t == TG - 1)
                last.then_inc(s_before, 1)

            def transpose_x1(s, par):
                pe.wait_ge(s_x2n, s - 2)
                wait_free(M_USERS, s, 3)
                for t in range(TG):
                    last = nc.tensor.transpose(ps_m[:, t * P:(t + 1) * P], x2n[:, par, t, :], ident[:, :])
                last.then_inc(s_x2T, 1)

            def router(g):
                pe.wait_ge(s_x2Tc, g + 1)
                if later(g, 1):
                    pe.wait_ge(s_place, g * 5)
                for t in range(TG):
                    last = nc.tensor.matmul(ps_logit[:, t, :], x2T[:, t * P:(t + 1) * P], w_r[:, :],
                                            start=True, stop=True)
                last.then_inc(s_logit, 1)

            def step(s, half, par):
                for t in range(TG):
                    k = graph(s, t)
                    if k is not None:
                        transpose_probs(k, t % 2)
                    if graph(s, t, 2) is not None:
                        if t < 2:
                            scores(graph(s, t, 2), None, 1 - par, t + 2, t % 2)
                        else:
                            scores(graph(s, t, 2), half(0), par, t - 2, t % 2)
                    if t == 0:
                        if active(s, 4):
                            router(s - 4)
                        if active(s, 0):
                            project_qk(s)
                    if t == 1:
                        if active(s, 0):
                            project_v(s)
                        if active(s, 2):
                            transpose_attn(s, par)
                    if t == 2:
                        if active(s, 2):
                            project_out(s)
                        if active(s, -1):
                            transpose_x(s)
                        if active(s, 4):
                            count_before(s - 4)
                    if t == 3 and active(s, 3):
                        transpose_x1(s, 1 - par)
                    if k is not None:
                        attend(k, s - 1, 1 - par, t)

            def slots_T(j, landed, q):
                pe.wait_ge(s_xg[q], landed)
                if later(j, 2):
                    pe.wait_ge(s_gTc, j - 1)
                for hl in range(2):
                    for a in range(2):
                        last = nc.tensor.transpose(ps_xT[q % 2][:, hl, a * P:(a + 1) * P],
                                                   xg[:, q, a, hl * P:(hl + 1) * P], ident_h[:, :])
                last.then_inc(s_gT, 1)

            def shared_w(w, k):
                return w[:, E * FC * 2 + k, :]

            def expert_weights(j):
                e = pe.value_load(tile_expert[0:1, bass.ds(j, 1)], min_val=0, max_val=E - 1)

                def w_at(w, k):
                    return w[:, bass.ds(e * (2 * FC) + k, 1), :].rearrange("p a d -> p (a d)")
                return w_at

            def first_layer(n, par, w_at, hi, lo):
                for c in range(FC):
                    if c % 2 == 0 and later(n, 2):
                        pe.wait_ge(s_hid, n * FC + (c + 2 - 2 * FC))
                    dst = ps_h[:, par, c, :]
                    nc.tensor.matmul(dst, w_at(w1, 2 * c), hi, start=True, stop=False)
                    nc.tensor.matmul(dst, w_at(w1, 2 * c), lo, start=False, stop=False)
                    last = nc.tensor.matmul(dst, w_at(w1, 2 * c + 1), hi, start=False, stop=True)
                    if c % 2:
                        last.then_inc(s_h, 1)

            def second_layer(m, q, w_at):
                if later(m, 1):
                    pe.wait_ge(s_yc, m)
                for a in range(2):
                    dst = ps_y[:, a, :]
                    for c in range(FC):
                        if a == 0 and c % 2 == 0:
                            pe.wait_ge(s_hl[c // 2], m + 1)
                        cols = slice(a * P, (a + 1) * P)
                        nc.tensor.matmul(dst, hid_h[:, q, c, cols], w_at(w2, 2 * c), start=c == 0, stop=False)
                        nc.tensor.matmul(dst, hid_h[:, q, c, cols], w_at(w2, 2 * c + 1), start=False, stop=False)
                        last = nc.tensor.matmul(dst, hid_l[:, q, c, cols], w_at(w2, 2 * c), start=False,
                                                stop=c == FC - 1)
                last.then_inc(s_y, 1)

            def tile_step(n, i, q, kind=None):
                kind0, kind1, kind2 = kind_of(n, kind), kind_of(n + 1, kind), kind_of(n - 2, kind)
                if isinstance(n, int) and n == 0:
                    pe.wait_ge(s_exp, B)
                    pe.wait_ge(s_pTc, B)
                    pe.wait_ge(s_attn, B)
                    pe.wait_ge(s_wl, UNITS)
                    pe.wait_ge(s_xl, EARLY // 2)
                if isinstance(n, int) and n == X_FROM:
                    pe.wait_ge(s_list, 3)
                    pe.wait_ge(s_xh, GROUPS)
                    pe.wait_ge(s_projc, GROUPS)
                    slots_T(0, 16, 0)
                if kind1 == "expert" and later(n, X_FROM):
                    slots_T(n - (X_FROM - 1), i * 16 + ((q + 1) // 8) * 16, (q + 1) % 8)
                if kind0 == "expert":
                    w_at = expert_weights(n - X_FROM)
                    pe.wait_ge(s_gTc, n - (X_FROM - 1))
                    first_layer(n, q % 2, w_at, xgT[:, q % 2, 0, :], xgT[:, q % 2, 1, :])
                elif kind0:
                    if isinstance(n, int) and n == L_FROM:
                        pe.wait_ge(s_xl, GROUPS)
                    tile = n if kind0 == "early" else n - TILES
                    cols = bass.ds(tile * ST, ST)
                    first_layer(n, q % 2, shared_w, xh_all[:, cols], xl_all[:, cols])
                if kind2 == "expert":
                    w_at = expert_weights(n - (X_FROM + 2))
                    second_layer(n - 2, (q - 2) % 4, w_at)
                elif kind2:
                    second_layer(n - 2, (q - 2) % 4, shared_w)

            steps(pe, step, tile_step)
            tiles(pe, tile_step)


NAMES = ["x", "adj", "L0_gnn_Wq", "L0_gnn_bq", "L0_gnn_Wk", "L0_gnn_bk", "L0_gnn_Wv", "L0_gnn_bv", "L0_gnn_Wo",
         "L0_gnn_bo", "L0_gnn_gamma", "L0_gnn_beta", "L0_ffn_Wr", "L0_ffn_W1s", "L0_ffn_b1s", "L0_ffn_W2s",
         "L0_ffn_b2s", "L0_ffn_W1p", "L0_ffn_b1p", "L0_ffn_W2p", "L0_ffn_b2p"]


def kernel(**inputs):
    import numpy as np
    import concourse.bacc as bacc
    from concourse.bass_utils import run_bass_kernel_spmd

    nc = bacc.Bacc("TRN2", target_bir_lowering=False, num_devices=1)
    arrays, args = {}, []
    for name in NAMES:
        a = np.ascontiguousarray(inputs[name])
        arrays["in_" + name] = a
        args.append(nc.dram_tensor("in_" + name, a.shape, mybir.dt.from_np(a.dtype), kind="ExternalInput").ap())
    result = nc.dram_tensor("result", arrays["in_x"].shape, F32, kind="ExternalOutput").ap()
    build_program(nc, *args, result)
    return run_bass_kernel_spmd(nc, [arrays], core_ids=[0]).results[0]["result"]
```

```python
from contextlib import ExitStack

import concourse.bass as bass
from concourse import mybir

F32 = mybir.dt.float32
BF16 = mybir.dt.bfloat16
I32 = mybir.dt.int32
U32 = mybir.dt.uint32
ALU = mybir.AluOpType
ACT = mybir.ActivationFunctionType
AX_X = mybir.AxisListType.X

P = 128
EPS = 1e-5
MASKED = -1e30
NOWHERE = 1 << 20


def build_program(nc, x, adj, Wq, bq, Wk, bk, Wv, bv, Wo, bo, gamma, beta,
                  Wr, W1s, b1s, W2s, b2s, W1p, b1p, W2p, b2p, out):
    B = x.shape[0]
    HEADS = 4
    HD = P // HEADS
    E = Wr.shape[1]
    F = W1s.shape[1]
    FC = F // P
    TG = 4
    GROUPS = B // TG
    TOKENS = B * P
    W = TG * P
    ST = 2 * P
    REGION = TOKENS + ST
    TILES = 2 * TOKENS // ST + E
    IDLE_ROW = E * REGION
    SHARED_TILES = TOKENS // ST
    RW = 2 * P + 2
    SCALE = float(HD) ** -0.5
    assert GROUPS % 2 == 0 and TILES % 4 == 0

    slots = nc.dram_tensor("slots", [E * REGION + ST, RW], BF16).ap()
    pairs = nc.dram_tensor("pairs", [2 * TOKENS, P], F32).ap()

    with ExitStack() as ctx:
        def sb(name, shape, dt=F32):
            return ctx.enter_context(nc.sbuf_tensor(name, shape, dt))

        def sem(name):
            return ctx.enter_context(nc.semaphore(name))

        ident = sb("ident", [P, P])
        ident_h = sb("ident_h", [P, P], BF16)
        before = sb("before", [P, P], BF16)
        ones_h = sb("ones_h", [P, P], BF16)
        adj_i = sb("adj_i", [P, P], I32)
        mask_h = sb("mask_h", [P, P], BF16)
        w_q, w_k, w_v, w_o = sb("w_q", [P, P]), sb("w_k", [P, P]), sb("w_v", [P, P]), sb("w_o", [P, P])
        w_r = sb("w_r", [P, E])
        NB = (E + 1) * FC
        bias_rows = sb("bias_rows", [NB + 3, P])
        bias_cols = sb("bias_cols", [P, NB + 3])
        bq_scaled = sb("bq_scaled", [P, 1])
        bv_wide = sb("bv_wide", [P, P])
        bo_row, gamma_row, beta_row = sb("bo_row", [P, P]), sb("gamma_row", [P, P]), sb("beta_row", [P, P])
        b2s_row = sb("b2s_row", [P, P])
        b2_rows = sb("b2_rows", [P, E, P])
        c_row = sb("c_row", [P, P])
        minus_half = sb("minus_half", [P, TG])
        rank_i = sb("rank_i", [P, E], I32)
        rank = sb("rank", [P, E])
        base_i = sb("base_i", [P, E], I32)
        region_start = sb("region_start", [P, E])
        ids = sb("ids", [P, B], U32)
        pad_rows = sb("pad_rows", [P, 2, RW], BF16)

        x_all = sb("x_all", [P, B, P])
        xh_all = sb("xh_all", [P, TOKENS], BF16)
        xl_all = sb("xl_all", [P, TOKENS], BF16)
        w1 = sb("w1", [P, (E + 1) * FC * 2, P], BF16)
        w2 = sb("w2", [P, (E + 1) * FC * 2, P], BF16)
        delta = sb("delta", [P, B])
        weight1, weight2 = sb("weight1", [P, B]), sb("weight2", [P, B])
        base = sb("base", [P, 2, E])

        w_stage = sb("w_stage", [P, 4, F])
        stats = sb("stats", [P, 3, TG, 6])
        meanvar = sb("meanvar", [P, 3, TG, 2])
        var_eps = sb("var_eps", [P, 3, TG])
        rstd = sb("rstd", [P, 4, TG])
        shift = sb("shift", [P, 3, TG])
        xn = sb("xn", [P, W])
        xnT = sb("xnT", [P, W])
        qk = sb("qk", [P, 4, W])
        qT, kT = qk[:, 0:2, :], qk[:, 2:4, :]
        k_wide = sb("k_wide", [P, 2, TG, HEADS, P])
        v1 = sb("v1", [P, 2, TG, HEADS, HD + 1])
        neg_max = sb("neg_max", [P, 2, HEADS])
        probs = sb("probs", [P, 2, HEADS, P])
        probsT = sb("probsT", [P, 2, HEADS * P])
        inv_sum = sb("inv_sum", [P, 2, HEADS])
        attn = sb("attn", [P, 2, TG, P])
        attnT = sb("attnT", [P, W])
        proj = sb("proj", [P, TG, P])
        scaled = sb("scaled", [P, TG, P])
        x2n = sb("x2n", [P, 2, TG, P])
        x2T = sb("x2T", [P, W])
        rows = sb("rows", [P, 2, TG, RW], BF16)
        row_ids = rows[:, :, :, :].bitcast(U32)
        logits = sb("logits", [P, TG, E])
        top1, top2 = sb("top1", [P, TG]), sb("top2", [P, TG])
        first = sb("first", [P, 2, TG])
        hit = sb("hit", [P, 2, TG, E])
        hot1, hot2 = sb("hot1", [P, TG, E]), sb("hot2", [P, TG, E])
        rest = sb("rest", [P, TG, E])
        chosen = sb("chosen", [P, TG, E], BF16)
        place = sb("place", [P, TG, E])
        placed = sb("placed", [P, 2, TG, E])
        slot_f = sb("slot_f", [P, 2, TG])
        slot = sb("slot", [P, 2, 2, TG], U32)

        J = TILES
        count = sb("count", [P, E])
        ntile_i = sb("ntile_i", [P, E], I32)
        ntile = sb("ntile", [P, E])
        tri = sb("tri", [P, E, E])
        tmp88 = sb("tmp88", [P, E, E])
        upto = sb("upto", [P, E])
        jump = sb("jump", [P, E])
        j_i = sb("j_i", [P, J], I32)
        j_f = sb("j_f", [P, J])
        past = sb("past", [P, J, E])
        jumps = sb("jumps", [P, J, E])
        e_f, r_f, r_g = sb("e_f", [P, J]), sb("r_f", [P, J]), sb("r_g", [P, J])
        e_c, e_sum = sb("e_c", [P, J]), sb("e_sum", [P, J // 8])
        powers = sb("powers", [P, 8])
        experts = sb("experts", [P, J // 8], I32)
        tile_row = sb("tile_row", [P, J], I32)
        end_i = sb("end_i", [P, E], I32)

        YG = 4
        xg_yg = sb("xg_yg", [P, max(8 * RW, YG * 4 * P)])
        xg = xg_yg[:, 0:8 * RW].bitcast(BF16).rearrange("p (q a w) -> p q a w", q=8, a=2)
        xg_ids = xg_yg[:, 0:8 * RW].bitcast(U32).rearrange("p (q a w) -> p q a w", q=8, a=2)
        xgT = sb("xgT", [P, 2, 2, ST], BF16)
        over = k_wide[:, :, :, :, :].rearrange("p q t h m -> p (q t h m)")
        NH = 2 * FC * ST
        hid = over[:, 0:NH].rearrange("p (q c n) -> p q c n", q=2, c=FC)
        hid_h = over[:, NH:2 * NH].bitcast(BF16).rearrange("p (q c n) -> p q c n", q=4, c=FC)
        hid_l = qk[:, :, :].rearrange("p a n -> p (a n)").bitcast(BF16).rearrange("p (q c n) -> p q c n", q=4, c=FC)
        y = w_stage[:, 0:2, :].rearrange("p q (a b d) -> p (q a) b d", a=2, b=2)
        res = w_stage[:, 2:4, :].rearrange("p q (a b d) -> p (q a) b d", a=2, b=2)
        yg = xg_yg[:, 0:YG * 4 * P].rearrange("p (q a w) -> p q a w", q=YG, a=2)
        part = v1[:, :, :, :, :].rearrange("p q t h d -> p (q t h d)")[:, 0:4 * ST].rearrange(
            "p (q a d) -> p q a d", q=4, a=2)

        pair = ctx.enter_context(nc.psum_tensor("pair", [P, 2, 512], F32))
        bank = [pair[:, 0, :], pair[:, 1, :]]
        bank += [ctx.enter_context(nc.psum_tensor(f"bank{n}", [P, 512], F32)) for n in (2, 3)]
        wide = ctx.enter_context(nc.psum_tensor("wide", [P, 4, 512], F32))
        ps_s = wide[:, 0:2, :].rearrange("p q (h m) -> p q h m", h=HEADS)
        ps_av = wide[:, 2:4, 0:HEADS * (HD + 1)].rearrange("p q (h d) -> p q h d", h=HEADS)
        ps_pT, ps_o, ps_m, ps_n = bank
        ps_logit = ps_o[:, 0:TG * E].rearrange("p (t e) -> p t e", t=TG)
        ps_before = ps_o[:, 64:64 + TG * E].rearrange("p (t e) -> p t e", t=TG)
        ps_total = ps_o[:, 128:128 + E]
        ps_h = wide[:, :, :].rearrange("p b n -> p (b n)").rearrange("p (q c n) -> p q c n", q=2, c=FC)
        ps_y = pair[:, :, 0:ST].rearrange("p q (a d) -> p q a d", a=2)
        ps_xT = [bank[2][:, 0:ST].bitcast(BF16).rearrange("p (h n) -> p h n", h=2),
                 bank[3][:, 0:ST].bitcast(BF16).rearrange("p (h n) -> p h n", h=2)]

        s_apart = sem("s_apart")
        s_c1 = sem("s_c1")
        s_c2 = sem("s_c2")
        s_x = sem("s_x")
        s_kz = [sem("s_kz0"), sem("s_kz1")]
        s_w = [sem(f"s_w{n}") for n in range(4)]
        s_pool_c = sem("s_pool_c")
        s_cast_c = sem("s_cast_c")
        s_pe_c = sem("s_pe_c")
        s_act_c = sem("s_act_c")
        s_crow = sem("s_crow")
        s_ln = sem("s_ln")
        s_var = [sem(f"s_var{n}") for n in range(3)]
        s_pl = sem("s_pl")
        s_rstd = [sem(f"s_rstd{n}") for n in range(3)]
        s_shift = {0: sem("s_shift0"), 2: sem("s_shift2")}
        s_xn = sem("s_xn")
        s_xT, s_xTc = sem("s_xT"), sem("s_xTc")
        s_q, s_k, s_v = sem("s_q"), sem("s_k"), sem("s_v")
        s_qc, s_kc, s_vc = sem("s_qc"), sem("s_kc"), sem("s_vc")
        s_score, s_max, s_exp = sem("s_score"), sem("s_max"), sem("s_exp")
        s_pT, s_pTc = sem("s_pT"), sem("s_pTc")
        s_av, s_inv, s_attn = sem("s_av"), sem("s_inv"), sem("s_attn")
        s_oT, s_oTc = sem("s_oT"), sem("s_oTc")
        s_proj, s_projc = sem("s_proj"), sem("s_projc")
        s_scaled, s_x1res = sem("s_scaled"), sem("s_x1res")
        s_xbeta = sem("s_xbeta")
        s_x2n, s_rowh, s_rowl = sem("s_x2n"), sem("s_rowh"), sem("s_rowl")
        s_x2T, s_x2Tc, s_xh, s_xl = sem("s_x2T"), sem("s_x2Tc"), sem("s_xh"), sem("s_xl")
        s_logit, s_route, s_chosen = sem("s_logit"), sem("s_route"), sem("s_chosen")
        s_before, s_place, s_slot = sem("s_before"), sem("s_place"), sem("s_slot")
        s_id = sem("s_id")
        s_sent = [sem("s_sent0"), sem("s_sent1")]
        s_wh, s_wl = sem("s_wh"), sem("s_wl")
        s_list = sem("s_list")
        s_pad = sem("s_pad")
        s_soft, s_wt = sem("s_soft"), sem("s_wt")
        s_xg = [sem(f"s_xg{n}") for n in range(8)]
        s_gT, s_gTc = sem("s_gT"), sem("s_gTc")
        s_h, s_hid = sem("s_h"), sem("s_hid")
        s_hh = sem("s_hh")
        s_hs = sem("s_hs")
        s_hl = [sem("s_hl0"), sem("s_hl1")]
        s_y, s_yc = sem("s_y"), sem("s_yc")
        s_back = [sem(f"s_back{n}") for n in range(4)]
        s_yg = [sem(f"s_yg{n}") for n in range(YG)]
        s_part, s_res = sem("s_part"), sem("s_res")
        s_out = [sem(f"s_out{n}") for n in range(4)]

        UNITS = 2 * (E + 1)
        UNITS_PER_STEP = 3
        STEPS = GROUPS + 6
        LOOP_FROM = 6
        LOOP_TO = GROUPS - 2
        X_PIECES = [0, 1, 2, 4, 8, 12, GROUPS]
        EARLY = 16
        TILE_BEHIND = [(STEPS - 5, 1), (STEPS - 5, 3), (STEPS - 4, 1), (STEPS - 4, 3), (STEPS - 3, 1),
                       (STEPS - 3, 2), (STEPS - 3, 3), (STEPS - 2, 0), (STEPS - 2, 1), (STEPS - 2, 2)]
        IN_STEPS = len(TILE_BEHIND)
        AHEAD_OF_LIST = 2
        X_FROM, L_FROM, T_END = EARLY, EARLY + TILES, TILES + SHARED_TILES
        assert EARLY == 16 and L_FROM % 8 == 0 and T_END - L_FROM == 16

        def norms_before(s, order, n):
            at = [k for k, lag in order if active(s, lag)].index(n)
            if isinstance(s, int):
                return at + sum(min(max(s - lag, 0), GROUPS) for _, lag in order)
            return s * 3 + (at - sum(lag for _, lag in order))

        def apart(eng):
            eng.sem_inc(s_apart, 1)

        def tiles_in(s, t):
            if not isinstance(s, int):
                return ()
            if (s, t) == (STEPS - 2, TG - 1):
                return range(IN_STEPS, EARLY)
            return [TILE_BEHIND.index((s, t))] if (s, t) in TILE_BEHIND else ()

        def steps(eng, step):
            def plain(s):
                step(s, lambda k: (s + k) // 2, s % 2)

            for s in range(-2, LOOP_FROM):
                plain(s)
            with eng.Fori(0, (LOOP_TO - LOOP_FROM) // 2) as i:
                for u in range(2):
                    s = LOOP_FROM + u
                    step(i * 2 + s, lambda k: i + (s + k) // 2, s % 2)
            for s in range(LOOP_TO, STEPS):
                plain(s)

        def tiles(eng, tile_step, before_loop=None):
            def plain(lo, hi):
                for n in range(lo, hi):
                    tile_step(n, n // 8, n % 8)

            def loop(lo, hi, unit, kind):
                with eng.Fori(lo // unit, hi // unit) as i:
                    for q in range(unit):
                        tile_step(i * unit + q, i, q, kind)

            plain(X_FROM, X_FROM + 8)
            if before_loop:
                before_loop(X_FROM // 8 + 1)
            loop(X_FROM + 8, L_FROM - 8, 8, "expert")
            plain(L_FROM - 8, L_FROM + 4)
            loop(L_FROM + 4, T_END - 4, 4, "shared")
            plain(T_END - 4, T_END + 2)

        class ExpertsOfRounds:
            def __init__(self, eng):
                self.eng, self.packed, self.held = eng, {}, {}

            def read(self, r, name):
                self.packed[name] = self.eng.value_load(experts[0:1, bass.ds(r, 1)], min_val=0, max_val=8 ** 8 - 1)

            def hold(self, name, r):
                self.held[name] = self.eng.alloc_register("experts_" + name)
                self.read_into(name, r)

            def read_into(self, name, r):
                self.eng.reg_load(self.held[name], experts[0:1, bass.ds(r, 1)])
                self.packed[name] = bass.RuntimeValue.of_register_unchecked(self.held[name], min_val=0,
                                                                            max_val=8 ** 8 - 1)

            def expert(self, name, k):
                return self.eng.snap((self.packed[name] >> (3 * k)) & 7, min_val=0, max_val=E - 1)

        def kind_of(n, kind):
            if not isinstance(n, int):
                return kind
            if n < 0 or n >= T_END:
                return None
            return "early" if n < X_FROM else "expert" if n < L_FROM else "shared"

        def active(s, stage):
            return not isinstance(s, int) or 0 <= s - stage < GROUPS

        def later(g, n):
            return not isinstance(g, int) or g >= n

        def unit_parts(u):
            first = (E if u < 2 else u // 2 - 1) * FC * 2
            dst = (w2 if u % 2 else w1)[:, first:first + FC * 2, :].rearrange("p (c h) d -> p c h d", h=2)
            return w_stage[:, u % 4, :].rearrange("p (c d) -> p c d", c=FC), dst[:, :, 0, :], dst[:, :, 1, :]

        def graph(s, t, ahead=0):
            k = s * TG + (t + ahead - TG)
            return k if not isinstance(k, int) or 0 <= k < B else None

        block = ctx.enter_context(nc.Block())

        @block.sync
        def _(sp):
            def load_x(piece):
                lo, hi = X_PIECES[piece] * TG, X_PIECES[piece + 1] * TG
                if piece:
                    sp.wait_ge(s_x, piece * 16)
                sp.dma_start(x_all[:, lo:hi, :], x[lo:hi, :, :].rearrange("t p d -> p t d")).then_inc(s_x, 16)

            def load_unit(u):
                e = u // 2 - 1
                if u >= 4:
                    sp.wait_ge(s_wl, u - 3)
                dst = w_stage[:, u % 4, :]
                if u % 2:
                    dst = dst.rearrange("p (c d) -> p c d", c=FC)
                    src = (W2s if e < 0 else W2p[e, :, :]).rearrange("(c p) d -> p c d", p=P)
                else:
                    src = W1s if e < 0 else W1p[e, :, :]
                sp.dma_start(dst, src).then_inc(s_w[u % 4], 16)

            load_x(0)
            for n, src in enumerate((bq, bk, bv)):
                sp.dma_start(bias_rows[NB + n:NB + n + 1, :], src.rearrange("(a p) -> a p", a=1)).then_inc(s_c1, 16)
            sp.dma_start(bias_rows[0:E * FC, :], b1p.rearrange("e (c p) -> (e c) p", p=P)).then_inc(s_c1, 16)
            sp.dma_start(bias_rows[E * FC:NB, :], b1s.rearrange("(c p) -> c p", p=P)).then_inc(s_c1, 16)
            for dst, src in ((w_k, Wk), (w_q, Wq), (w_v, Wv), (adj_i, adj)):
                sp.dma_start(dst[:, :], src).then_inc(s_c1, 16)
            load_x(1)
            for dst, src in ((w_o, Wo), (w_r, Wr)):
                sp.dma_start(dst[:, :], src).then_inc(s_c2, 16)
            for dst, src in ((bo_row, bo), (gamma_row, gamma), (beta_row, beta), (b2s_row, b2s)):
                sp.dma_start(dst[:, :], src.rearrange("(a d) -> a d", a=1).broadcast_to([P, P])).then_inc(s_c2, 16)
            sp.dma_start(b2_rows[:, :, :].rearrange("p e d -> p (e d)"),
                         b2p.rearrange("(a e) d -> a (e d)", a=1).broadcast_to([P, E * P])).then_inc(s_c2, 16)
            load_x(2)
            for u in range(4):
                load_unit(u)

            def step(s, half, par):
                if active(s, 0):
                    sp.wait_ge(s_kc, s + 1)
                    if isinstance(s, int) and s == 0:
                        sp.wait_ge(s_pool_c, 23)
                    if later(s, 2):
                        sp.wait_ge(s_score, s * TG - TG)
                    for h in range(HEADS):
                        on = slice(h * HD, (h + 1) * HD)
                        sp.dma_start(k_wide[on, par, :, h, :],
                                     kT[on, par, :].rearrange("p (t m) -> p t m", t=TG)).then_inc(s_kz[par], 16)
                if isinstance(s, int) and 0 <= s:
                    if s + 3 < len(X_PIECES) - 1:
                        load_x(s + 3)
                    for u in range(UNITS_PER_STEP * s - UNITS_PER_STEP, UNITS_PER_STEP * s):
                        if 0 <= u and u + 4 < UNITS:
                            load_unit(u + 4)

            steps(sp, step)
            sp.wait_ge(s_list, 1)
            for e in range(E):
                end = sp.value_load(end_i[0:1, e:e + 1], min_val=e * REGION, max_val=e * REGION + TOKENS)
                sp.dma_start(slots[bass.ds(end, ST), :].rearrange("(a p) w -> p a w", p=P),
                             pad_rows[:, :, :]).then_inc(s_pad, 16)
            sp.dma_start(slots[IDLE_ROW:IDLE_ROW + ST, :].rearrange("(a p) w -> p a w", p=P),
                         pad_rows[:, :, :]).then_inc(s_pad, 16)
            sp.wait_ge(s_pad, 16 * (E + 1))
            sp.wait_ge(s_sent[0], 16 * TG * GROUPS)
            sp.wait_ge(s_sent[1], 16 * TG * GROUPS)
            sp.wait_ge(s_list, 3)

            def load_slots(j, i, q):
                if later(j, 8):
                    sp.wait_ge(s_gT, j - 7)
                    sp.wait_ge(s_back[q % 4], i * 64 + (q // 4 - 1) * 32)
                row = sp.value_load(tile_row[0:1, bass.ds(j, 1)], min_val=0, max_val=IDLE_ROW)
                sp.dma_start(xg[:, q, :, :],
                             slots[bass.ds(row, ST), :].rearrange("(a p) w -> p a w", p=P)).then_inc(s_xg[q], 16)

            for q in range(8):
                load_slots(q, 0, q)
            with sp.Fori(1, TILES // 8) as i:
                for q in range(8):
                    load_slots(i * 8 + q, i, q)

            for q in range(4):
                sp.wait_ge(s_back[q], 32 * (TILES // 4))

            def load_pairs(j, q):
                sp.dma_start(yg[:, q, :, :], pairs[bass.ds(j * (2 * ST), 2 * ST), :].rearrange(
                    "(a p k) d -> p a (k d)", p=P, k=2)).then_inc(s_yg[q], 16)

            def store(j, q):
                sp.wait_ge(s_res, j + 1)
                sp.dma_start(out[bass.ds(j * 2, 2), :, :].rearrange("a p d -> p a d"),
                             res[:, q, :, :]).then_inc(s_out[q], 16)

            for q in range(YG):
                load_pairs(q, q)
            ROUNDS = (SHARED_TILES - YG) // YG
            with sp.Fori(0, ROUNDS) as i:
                for q in range(YG):
                    store(i * YG + q, q)
                    load_pairs(i * YG + (q + YG), q)
            for j in range(ROUNDS * YG, SHARED_TILES):
                store(j, j % 4)
                if j + YG < SHARED_TILES:
                    load_pairs(j + YG, j % YG)
            for q in range(4):
                sp.wait_ge(s_out[q], 16 * len(range(q, SHARED_TILES, 4)))

        @block.gpsimd
        def _(gp):
            nc.gpsimd.memset(ident[:, :], 0.0).then_inc(s_pool_c, 1)
            nc.gpsimd.memset(ones_h[:, :], 1.0).then_inc(s_pool_c, 1)
            nc.gpsimd.memset(tri[:, :, :], 1.0).then_inc(s_pool_c, 1)
            nc.gpsimd.memset(minus_half[:, :], -0.5).then_inc(s_pool_c, 1)
            nc.gpsimd.memset(v1[:, :, :, :, :], 1.0).then_inc(s_pool_c, 1)
            nc.gpsimd.memset(pad_rows[:, :, :], 0.0).then_inc(s_pool_c, 1)
            for k in range(8):
                nc.gpsimd.memset(powers[:, k:k + 1], float(8 ** k)).then_inc(s_pool_c, 1)
            nc.gpsimd.iota(rank_i[:, :], [[-1, E]], base=E, channel_multiplier=0).then_inc(s_pool_c, 1)
            nc.gpsimd.iota(j_i[:, :], [[1, J]], base=0, channel_multiplier=0).then_inc(s_pool_c, 1)
            nc.gpsimd.iota(base_i[:, :], [[REGION, E]], base=0, channel_multiplier=0).then_inc(s_pool_c, 1)
            nc.gpsimd.iota(ids[:, :], [[2 * P, B]], base=0, channel_multiplier=2).then_inc(s_pool_c, 1)
            gp.wait_ge(s_pool_c, 18)
            nc.gpsimd.affine_select(out=ident[:, :], in_=ident[:, :], compare_op=ALU.not_equal, fill=1.0,
                                    base=0, pattern=[[-1, P]], channel_multiplier=1).then_inc(s_pool_c, 1)
            nc.gpsimd.affine_select(out=before[:, :], in_=ones_h[:, :], compare_op=ALU.is_gt, fill=0.0,
                                    base=0, pattern=[[1, P]], channel_multiplier=-1).then_inc(s_pool_c, 1)
            nc.gpsimd.affine_select(out=tri[:, :, :], in_=tri[:, :, :], compare_op=ALU.is_ge, fill=0.0,
                                    base=0, pattern=[[1, E], [-1, E]], channel_multiplier=0).then_inc(s_pool_c, 1)
            nc.gpsimd.iota(pad_rows[:, :, :].bitcast(U32)[:, :, P:P + 1], [[0, 2], [0, 1]], base=NOWHERE,
                           channel_multiplier=0).then_inc(s_pool_c, 1)

            ORDER = ((1, 3), (2, 3), (0, -2))

            def inv_std(n, s, g, to):
                gp.wait_ge(s_var[n], g + 1)
                apart(gp)
                nc.gpsimd.tensor_scalar(var_eps[:, n, :], meanvar[:, n, :, 1], EPS, None, ALU.add).then_inc(s_pl, 1)
                if n == 0 and later(g, 1):
                    gp.wait_ge(s_xn, g)
                if n == 1 and later(g, 1):
                    gp.wait_ge(s_x1res, g * TG)
                if n == 2 and later(g, 2):
                    gp.wait_ge(s_x2n, g - 1)
                gp.wait_ge(s_pl, norms_before(s, ORDER, n) + 1)
                nc.gpsimd.tensor_tensor(rstd[:, to, :], var_eps[:, n, :], minus_half[:, :],
                                        ALU.pow).then_inc(s_rstd[n], 1)

            def add_beta(g):
                if isinstance(g, int) and g == 0:
                    gp.wait_ge(s_c2, 7 * 16)
                gp.wait_ge(s_xn, g + 1)
                nc.gpsimd.tensor_tensor(x_all[:, bass.ds(g * TG, TG), :], x_all[:, bass.ds(g * TG, TG), :],
                                        beta_row[:, None, :].broadcast_to([P, TG, P]), ALU.add).then_inc(s_xbeta, 1)

            def unit_low(u):
                src, high, low = unit_parts(u)
                gp.wait_ge(s_wh, u + 1)
                nc.gpsimd.tensor_tensor(low, src, high, ALU.subtract).then_inc(s_wl, 1)

            def send(par, choice, lo, hi):
                for t in range(lo, hi):
                    nc.gpsimd.indirect_dma_start(
                        out=slots[:, :], out_offset=bass.IndirectOffsetOnAxis(ap=slot[:, par, choice, t:t + 1], axis=0),
                        in_=rows[:, par, t, :], in_offset=None).then_inc(s_sent[choice], 16)

            def step(s, half, par):
                g, q = s - 6, par
                if active(s, 3):
                    inv_std(1, s, s - 3, 1)
                if active(s, 6):
                    nc.gpsimd.tensor_copy(row_ids[:, q, :, P], ids[:, bass.ds(g * TG, TG)]).then_inc(s_id, 1)
                    gp.wait_ge(s_slot, g + 1)
                    gp.wait_ge(s_rowl, g + 1)
                    gp.wait_ge(s_id, g * 2 + 1)
                    apart(gp)
                    send(q, 0, 0, TG)
                if active(s, -1):
                    add_beta(s + 1)
                if active(s, 3):
                    inv_std(2, s, s - 3, 3 - par)
                if active(s, 6):
                    gp.wait_ge(s_sent[0], (g + 1) * (16 * TG))
                    apart(gp)
                    nc.gpsimd.tensor_scalar(row_ids[:, q, :, P], row_ids[:, q, :, P], 1, None,
                                            ALU.add).then_inc(s_id, 1)
                    gp.wait_ge(s_id, g * 2 + 2)
                    apart(gp)
                    send(q, 1, 0, 1)
                if active(s, -2):
                    inv_std(0, s, s + 2, 0)
                if isinstance(s, int) and s == -2:
                    nc.gpsimd.memset(k_wide[:, :, :, :, :], 0.0).then_inc(s_pool_c, 1)
                if active(s, 6):
                    send(q, 1, 1, TG)
                if isinstance(s, int) and 0 <= s:
                    for u in range(UNITS_PER_STEP * s, UNITS_PER_STEP * (s + 1)):
                        if u < UNITS:
                            unit_low(u)

            steps(gp, step)

            def tile_step(n, i, q, kind=None):
                kind2 = kind_of(n - 2, kind)
                if kind2 == "expert":
                    gp.wait_ge(s_yc, n - 1)
                    apart(gp)
                    for a in range(2):
                        nc.gpsimd.indirect_dma_start(
                            out=pairs[:, :],
                            out_offset=bass.IndirectOffsetOnAxis(ap=xg_ids[:, (q - 2) % 8, a, P:P + 1], axis=0),
                            in_=y[:, (q - 2) % 4, a, :], in_offset=None, bounds_check=2 * TOKENS - 1,
                            oob_is_err=False).then_inc(s_back[(q - 2) % 4], 16)
                if kind_of(n, kind) == "shared":
                    for b in range(2):
                        half_ = slice(2 * b, 2 * b + 2)
                        gp.wait_ge(s_hs, n * 2 + (b + 1 - 2 * TILES))
                        if b == 0:
                            if isinstance(n, int) and n == L_FROM:
                                gp.wait_ge(s_hl[0], n)
                                gp.wait_ge(s_hl[1], n)
                            gp.wait_ge(s_y, n - 3)
                        nc.gpsimd.tensor_tensor(hid_l[:, q % 4, half_, :], hid[:, q % 2, half_, :],
                                                hid_h[:, q % 4, half_, :], ALU.subtract).then_inc(s_hl[b], 1)

            tiles(gp, tile_step)

        @block.scalar
        def _(act):
            def copy(out, in_, **kw):
                return nc.scalar.activation(out, in_, ACT.Identity, **kw)

            act.wait_ge(s_pe_c, 1)
            copy(bias_cols[:, :], ps_m[:, 0:NB + 3]).then_inc(s_act_c, 1)
            act.wait_ge(s_act_c, 1)
            nc.scalar.mul(bq_scaled[:, :], bias_cols[:, NB:NB + 1], SCALE).then_inc(s_act_c, 1)
            act.wait_ge(s_act_c, 2)

            def tile_of(n):
                return x_all[:, bass.ds(n, 1), :].rearrange("p a d -> p (a d)")

            def x_normed(g):
                act.wait_ge(s_shift[0], g + 1)
                if later(g, 1):
                    act.wait_ge(s_xT, g)
                for t in range(TG):
                    last = copy(xn[:, t * P:(t + 1) * P], tile_of(g * TG + t), bias=shift[:, 0, t:t + 1],
                                scale=rstd[:, 0, t:t + 1])
                last.then_inc(s_xn, 1)

            def x1_normed(g, par):
                norm = 2 + par
                act.wait_ge(s_shift[2], g + 1)
                if later(g, 2):
                    act.wait_ge(s_rowl, g - 1)
                for t in range(TG):
                    last = copy(x2n[:, par, t, :], tile_of(g * TG + t), bias=shift[:, 2, t:t + 1],
                                scale=rstd[:, norm, t:t + 1])
                last.then_inc(s_x2n, 1)

            def unit_high(u):
                src, high, low = unit_parts(u)
                act.wait_ge(s_w[u % 4], (u // 4 + 1) * 16)
                copy(high, src).then_inc(s_wh, 1)

            def copy_xT(g):
                act.wait_ge(s_xT, g + 1)
                copy(xnT[:, :], ps_m[:, :]).then_inc(s_xTc, 1)

            def copy_q(g, par):
                act.wait_ge(s_q, g + 1)
                copy(qT[:, par, :], ps_n[:, :], bias=bq_scaled[:, 0:1], scale=SCALE).then_inc(s_qc, 1)

            def copy_k(g, half, par):
                act.wait_ge(s_k, g + 1)
                if later(g, 2):
                    act.wait_ge(s_kz[par], half * 64)
                copy(kT[:, par, :], ps_m[:, :], bias=bias_cols[:, NB + 1:NB + 2]).then_inc(s_kc, 1)

            def copy_v(g, par):
                act.wait_ge(s_v, g + 1)
                copy(v1[:, par, :, :, 0:HD],
                     ps_n[:, :].rearrange("p (t h d) -> p t h d", t=TG, h=HEADS)).then_inc(s_vc, 1)

            def exponentials(k, q):
                act.wait_ge(s_max, k + 1)
                for h in range(HEADS):
                    last = nc.scalar.activation(probs[:, q, h, :], ps_s[:, q, h, :], ACT.Exp,
                                                bias=neg_max[:, q, h:h + 1])
                last.then_inc(s_exp, 1)

            def copy_probsT(k, q):
                act.wait_ge(s_pT, k + 1)
                copy(probsT[:, q, :], ps_pT[:, :]).then_inc(s_pTc, 1)

            def copy_attnT(g):
                act.wait_ge(s_oT, g + 1)
                copy(attnT[:, :], ps_m[:, :]).then_inc(s_oTc, 1)

            def row_high(g, par):
                if later(g, 2):
                    act.wait_ge(s_sent[1], (g - 1) * (16 * TG))
                copy(rows[:, par, :, 0:P], x2n[:, par, :, :]).then_inc(s_rowh, 1)

            def copy_x2T(g):
                act.wait_ge(s_x2T, g + 1)
                if later(g, 1):
                    act.wait_ge(s_xl, g)
                    act.wait_ge(s_logit, g)
                copy(x2T[:, :], ps_m[:, :]).then_inc(s_x2Tc, 1)
                copy(xh_all[:, bass.ds(g * W, W)], ps_m[:, :]).then_inc(s_xh, 1)

            def step(s, half, par):
                for t in range(TG):
                    if graph(s, t) is not None:
                        copy_probsT(graph(s, t), t % 2)
                    if t == 0 and active(s, 0):
                        copy_k(s, half(0), par)
                    if t == 1 and active(s, -1):
                        x_normed(s + 1)
                    if t == 2 and active(s, 4):
                        x1_normed(s - 4, par)
                    if t == 3 and active(s, 5):
                        row_high(s - 5, 1 - par)
                    if graph(s, t, 2) is not None:
                        exponentials(graph(s, t, 2), t % 2)
                    if t == 0 and active(s, 0):
                        copy_q(s, par)
                    if t == 1:
                        if active(s, 0):
                            copy_v(s, par)
                        if active(s, 2):
                            copy_attnT(s - 2)
                    if t == 2 and active(s, -1):
                        copy_xT(s + 1)
                    if t == 3 and active(s, 4):
                        copy_x2T(s - 4)
                    if t and isinstance(s, int) and 0 <= s * UNITS_PER_STEP + (t - 1) < UNITS:
                        unit_high(s * UNITS_PER_STEP + (t - 1))
                    for n in tiles_in(s, t):
                        tile_step(n, n // 8, n % 8)

            def tile_step(n, i, q, kind=None):
                kind0, kind1 = kind_of(n, kind), kind_of(n + 1, kind)
                par = q % 2
                if kind0 == "expert":
                    if q == 0:
                        rounds.read(i - X_FROM // 8, "this")
                    e = rounds.expert("this", q)
                if isinstance(n, int) and n == X_FROM:
                    act.wait_ge(s_gT, 1)
                    copy(xgT[:, 0, :, :], ps_xT[0]).then_inc(s_gTc, 1)
                if kind1 == "expert" and later(n, X_FROM):
                    j = n - (X_FROM - 1)
                    act.wait_ge(s_gT, j + 1)
                    if later(j, 2):
                        act.wait_ge(s_h, n * 2 - 2)
                    copy(xgT[:, 1 - par, :, :], ps_xT[1 - par]).then_inc(s_gTc, 1)
                if kind0 is None:
                    return
                for c in range(FC):
                    if c % 2 == 0:
                        act.wait_ge(s_h, n * 2 + (c // 2 + 1))
                        if later(n, 2):
                            act.wait_ge(s_hl[c // 2], n - 1)
                    col = bass.ds(e * FC + c, 1) if kind0 == "expert" else slice(E * FC + c, E * FC + c + 1)
                    nc.scalar.activation(hid[:, par, c, :], ps_h[:, par, c, :], ACT.Gelu,
                                         bias=bias_cols[:, col]).then_inc(s_hid, 1)
                if kind0 in ("early", "shared"):
                    for b in range(2):
                        act.wait_ge(s_hid, n * 4 + (2 * b + 2))
                        if b == 0 and later(n, 4):
                            act.wait_ge(s_y, n - 3)
                        copy(hid_h[:, q % 4, 2 * b:2 * b + 2, :], hid[:, par, 2 * b:2 * b + 2, :]).then_inc(s_hs, 1)

            rounds = ExpertsOfRounds(act)
            steps(act, step)
            act.wait_ge(s_list, 3)
            nc.scalar.activation(weight2[:, :], delta[:, :], ACT.Exp).then_inc(s_soft, 1)
            tiles(act, tile_step)

        @block.vector
        def _(dve):
            def constants_1():
                dve.wait_ge(s_c1, 9 * 16)
                dve.wait_ge(s_pool_c, 22)
                nc.vector.tensor_copy(ident_h[:, :], ident[:, :]).then_inc(s_cast_c, 1)
                nc.vector.tensor_scalar(mask_h[:, :], adj_i[:, :], 0, MASKED, ALU.is_equal,
                                        ALU.mult).then_inc(s_cast_c, 1)
                nc.vector.tensor_copy(rank[:, :], rank_i[:, :]).then_inc(s_cast_c, 1)
                nc.vector.tensor_copy(region_start[:, :], base_i[:, :]).then_inc(s_cast_c, 1)
                nc.vector.tensor_copy(base[:, 0, :], base_i[:, :]).then_inc(s_cast_c, 1)
                nc.vector.tensor_copy(j_f[:, :], j_i[:, :]).then_inc(s_cast_c, 1)
                dve.wait_ge(s_act_c, 1)
                nc.vector.tensor_copy(bv_wide[:, :],
                                      bias_cols[:, NB + 2:NB + 3].broadcast_to([P, P])).then_inc(s_cast_c, 1)

            def constants_2():
                dve.wait_ge(s_c2, 7 * 16)
                nc.vector.tensor_tensor(b2_rows[:, :, :], b2_rows[:, :, :],
                                        b2s_row[:, None, :].broadcast_to([P, E, P]), ALU.add).then_inc(s_cast_c, 1)
                dve.wait_ge(s_pe_c, 2)
                nc.vector.tensor_tensor(c_row[:, :], ps_n[:, 0:P], bo_row[:, :], ALU.add).then_inc(s_crow, 1)
                dve.wait_ge(s_cast_c, 8)
                dve.wait_ge(s_crow, 1)

            ORDER = ((2, 3), (0, -2), (1, 2))

            def statistics(n, s, g, src):
                if later(g, 1):
                    dve.wait_ge(s_rstd[n], g)
                apart(dve)
                for t in range(TG):
                    nc.vector.bn_stats(stats[:, n, t, :], src(t)).then_inc(s_ln, 1)
                dve.wait_ge(s_ln, (norms_before(s, ORDER, n) + 1) * TG)
                apart(dve)
                for t in range(TG):
                    last = nc.vector.bn_aggr(meanvar[:, n, t, :], stats[:, n, t, :])
                last.then_inc(s_var[n], 1)

            def make_shift(n, g, at):
                dve.wait_ge(s_rstd[n], g + 1)
                if n == 2 and later(g, 1):
                    dve.wait_ge(s_x2n, g)
                nc.vector.scalar_tensor_tensor(shift[:, n, :], meanvar[:, n, :, 0], -1.0, rstd[:, at, :],
                                               ALU.mult, ALU.mult).then_inc(s_shift[n], 1)

            def normalise_and_max(k, par, t, m, q):
                if k is not None:
                    dve.wait_ge(s_av, k + 1)
                    nc.vector.reciprocal(inv_sum[:, t % 2, :], ps_av[:, t % 2, :, HD]).then_inc(s_inv, 1)
                if m is not None:
                    dve.wait_ge(s_score, m + 1)
                    if later(m, 2):
                        dve.wait_ge(s_exp, m - 1)
                    nc.vector.tensor_reduce(neg_max[:, q, :], ps_s[:, q, :, :], AX_X, ALU.max,
                                            negate=True).then_inc(s_max, 1)
                if k is not None:
                    dve.wait_ge(s_inv, k + 1)
                    nc.vector.tensor_tensor(attn[:, par, t, :].rearrange("p (h d) -> p h d", h=HEADS),
                                            ps_av[:, t % 2, :, 0:HD],
                                            inv_sum[:, t % 2, :].unsqueeze(2).broadcast_to([P, HEADS, HD]),
                                            ALU.mult).then_inc(s_attn, 1)

            def link(ins, g, n, meanwhile, piece):
                ins.then_inc(s_route, 1)
                meanwhile(piece)
                dve.wait_ge(s_route, g * 11 + n)

            def route_top1(g, meanwhile):
                rk = rank[:, None, :].broadcast_to([P, TG, E])
                dve.wait_ge(s_logit, g + 1)
                link(nc.vector.tensor_copy(logits[:, :, :], ps_logit), g, 1, meanwhile, 0)
                link(nc.vector.tensor_reduce(top1[:, :], logits[:, :, :], AX_X, ALU.max), g, 2, meanwhile, 1)
                link(nc.vector.tensor_tensor(hit[:, 0, :, :], logits[:, :, :],
                                             top1[:, :].unsqueeze(2).broadcast_to([P, TG, E]), ALU.is_equal),
                     g, 3, meanwhile, 2)
                link(nc.vector.tensor_tensor(hit[:, 1, :, :], hit[:, 0, :, :], rk, ALU.mult), g, 4, meanwhile, 3)
                link(nc.vector.tensor_reduce(first[:, 0, :], hit[:, 1, :, :], AX_X, ALU.max), g, 5, meanwhile, 4)
                link(nc.vector.tensor_tensor(hot1[:, :, :], rk, first[:, 0, :].unsqueeze(2).broadcast_to([P, TG, E]),
                                             ALU.is_equal), g, 6, meanwhile, 5)

            def route_top2(g, meanwhile):
                rk = rank[:, None, :].broadcast_to([P, TG, E])
                link(nc.vector.scalar_tensor_tensor(rest[:, :, :], hot1[:, :, :], MASKED, logits[:, :, :],
                                                    ALU.mult, ALU.add), g, 7, meanwhile, 0)
                link(nc.vector.tensor_reduce(top2[:, :], rest[:, :, :], AX_X, ALU.max), g, 8, meanwhile, 1)
                nc.vector.tensor_tensor(delta[:, bass.ds(g * TG, TG)], top2[:, :], top1[:, :], ALU.subtract)
                link(nc.vector.tensor_tensor(hit[:, 0, :, :], rest[:, :, :],
                                             top2[:, :].unsqueeze(2).broadcast_to([P, TG, E]), ALU.is_equal),
                     g, 9, meanwhile, 2)
                link(nc.vector.tensor_tensor(hit[:, 1, :, :], hit[:, 0, :, :], rk, ALU.mult), g, 10, meanwhile, 3)
                link(nc.vector.tensor_reduce(first[:, 1, :], hit[:, 1, :, :], AX_X, ALU.max), g, 11, meanwhile, 4)
                nc.vector.tensor_tensor(hot2[:, :, :], rk, first[:, 1, :].unsqueeze(2).broadcast_to([P, TG, E]),
                                        ALU.is_equal).then_inc(s_chosen, 1)
                meanwhile(5)
                dve.wait_ge(s_chosen, g * 2 + 1)
                nc.vector.tensor_tensor(chosen[:, :, :], hot1[:, :, :], hot2[:, :, :], ALU.add).then_inc(s_chosen, 1)

            def route_slots(g, par):
                o = g * 5
                dve.wait_ge(s_before, g + 1)
                nc.vector.tensor_tensor(place[:, :, :], ps_before, base[:, par, None, :].broadcast_to([P, TG, E]),
                                        ALU.add).then_inc(s_place, 1)
                nc.vector.tensor_tensor(base[:, 1 - par, :], ps_total, base[:, par, :], ALU.add).then_inc(s_place, 1)
                dve.wait_ge(s_place, o + 2)
                nc.vector.tensor_tensor(placed[:, 0, :, :], place[:, :, :], hot1[:, :, :], ALU.mult).then_inc(s_place, 1)
                nc.vector.tensor_tensor(placed[:, 1, :, :], place[:, :, :], hot2[:, :, :], ALU.mult).then_inc(s_place, 1)
                dve.wait_ge(s_place, o + 4)
                nc.vector.tensor_reduce(slot_f[:, :, :], placed[:, :, :, :], AX_X, ALU.add).then_inc(s_place, 1)
                dve.wait_ge(s_place, o + 5)
                if later(g, 2):
                    dve.wait_ge(s_sent[1], (g - 1) * (16 * TG))
                nc.vector.tensor_copy(slot[:, par, :, :], slot_f[:, :, :]).then_inc(s_slot, 1)

            def tile_of(n):
                return x_all[:, bass.ds(n, 1), :].rearrange("p a d -> p (a d)")

            def x_statistics(s, g):
                piece = max(n for n in range(len(X_PIECES) - 1) if not isinstance(g, int) or X_PIECES[n] <= g)
                dve.wait_ge(s_x, 16 * (piece + 1))
                statistics(0, s, g, lambda t: tile_of(g * TG + t))

            def projection(s, g):
                dve.wait_ge(s_proj, g + 1)
                if later(g, 1):
                    dve.wait_ge(s_scaled, g * TG)
                nc.vector.tensor_tensor(proj[:, :, :], ps_n[:, :].rearrange("p (t d) -> p t d", t=TG),
                                        c_row[:, None, :].broadcast_to([P, TG, P]), ALU.add).then_inc(s_projc, 1)
                dve.wait_ge(s_projc, g + 1)
                statistics(1, s, g, lambda t: proj[:, t, :])

            def scale(g, t):
                if t >= TG:
                    return
                if t == 0:
                    dve.wait_ge(s_var[1], g + 1)
                    if later(g, 1):
                        dve.wait_ge(s_x1res, g * TG)
                nc.vector.scalar_tensor_tensor(scaled[:, t, :], proj[:, t, :], meanvar[:, 1, t, 0:1],
                                               gamma_row[:, :], ALU.subtract, ALU.mult).then_inc(s_scaled, 1)

            def residual(g, t):
                if t >= TG:
                    return
                if t == 0:
                    dve.wait_ge(s_rstd[1], g + 1)
                    dve.wait_ge(s_xbeta, g + 1)
                dve.wait_ge(s_scaled, g * TG + (t + 1))
                nc.vector.scalar_tensor_tensor(tile_of(g * TG + t), scaled[:, t, :], rstd[:, 1, t:t + 1],
                                               tile_of(g * TG + t), ALU.mult, ALU.add).then_inc(s_x1res, 1)

            def x1_statistics(s, g):
                dve.wait_ge(s_x1res, g * TG + TG)
                statistics(2, s, g, lambda t: tile_of(g * TG + t))

            def low_part(g):
                dve.wait_ge(s_xh, g + 1)
                nc.vector.tensor_tensor(xl_all[:, bass.ds(g * W, W)], x2T[:, :], xh_all[:, bass.ds(g * W, W)],
                                        ALU.subtract).then_inc(s_xl, 1)

            def row_low(g, par):
                dve.wait_ge(s_rowh, g + 1)
                nc.vector.tensor_tensor(rows[:, par, :, P:2 * P], x2n[:, par, :, :], rows[:, par, :, 0:P],
                                        ALU.subtract).then_inc(s_rowl, 1)

            k = [0]

            def own(ins):
                k[0] += 1
                ins.then_inc(s_wt, 1)
                dve.wait_ge(s_wt, k[0])

            end = base[:, GROUPS % 2, :]

            def list_tiles():
                own(nc.vector.tensor_tensor(count[:, :], end, region_start[:, :], ALU.subtract))
                own(nc.vector.tensor_scalar(ntile_i[:, :], count[:, :], ST / 2 - 0.5, 1.0 / ST, ALU.add, ALU.mult))
                own(nc.vector.tensor_copy(ntile[:, :], ntile_i[:, :]))
                own(nc.vector.tensor_tensor(tmp88[:, :, :], tri[:, :, :], ntile[:, None, :].broadcast_to([P, E, E]),
                                            ALU.mult))
                own(nc.vector.tensor_reduce(upto[:, :], tmp88[:, :, :], AX_X, ALU.add))
                own(nc.vector.tensor_scalar(jump[:, :], ntile[:, :], -float(ST), float(REGION), ALU.mult, ALU.add))
                own(nc.vector.tensor_tensor(past[:, :, :], j_f[:, :].unsqueeze(2).broadcast_to([P, J, E]),
                                            upto[:, None, :].broadcast_to([P, J, E]), ALU.is_ge))
                own(nc.vector.tensor_tensor(jumps[:, :, :], past[:, :, :], jump[:, None, :].broadcast_to([P, J, E]),
                                            ALU.mult))
                own(nc.vector.tensor_reduce(e_f[:, :], past[:, :, :], AX_X, ALU.add))
                own(nc.vector.tensor_reduce(r_f[:, :], jumps[:, :, :], AX_X, ALU.add))
                own(nc.vector.scalar_tensor_tensor(r_g[:, :], j_f[:, :], float(ST), r_f[:, :], ALU.mult, ALU.add))
                own(nc.vector.tensor_scalar(e_c[:, :], e_f[:, :], float(E - 1), None, ALU.min))
                own(nc.vector.tensor_tensor(e_c[:, :].rearrange("p (r k) -> p r k", k=8),
                                            e_c[:, :].rearrange("p (r k) -> p r k", k=8),
                                            powers[:, None, :].broadcast_to([P, J // 8, 8]), ALU.mult))
                own(nc.vector.tensor_reduce(e_sum[:, :], e_c[:, :].rearrange("p (r k) -> p r k", k=8), AX_X, ALU.add))
                nc.vector.tensor_copy(experts[:, :], e_sum[:, :]).then_inc(s_list, 1)
                nc.vector.tensor_scalar(tile_row[:, :], r_g[:, :], float(IDLE_ROW), None, ALU.min).then_inc(s_list, 1)

            def step(s, half, par):
                def scale_piece(n):
                    if active(s, 3):
                        scale(s - 3, n)

                def residual_piece(n):
                    if active(s, 3):
                        residual(s - 3, n)

                for t in range(TG):
                    normalise_and_max(graph(s, t, -1), par if t == 0 else 1 - par, (t - 1) % TG,
                                      graph(s, t, 2), t % 2)
                    if t == 0:
                        if active(s, 5):
                            route_top1(s - 5, scale_piece)
                        else:
                            for n in range(TG):
                                scale_piece(n)
                    if t == 1:
                        if active(s, 5):
                            route_top2(s - 5, residual_piece)
                        else:
                            for n in range(TG):
                                residual_piece(n)
                        if active(s, 3):
                            x1_statistics(s, s - 3)
                    if t == 2:
                        if active(s, 5):
                            low_part(s - 5)
                        if active(s, -2):
                            x_statistics(s, s + 2)
                    if t == 3:
                        if active(s, 5):
                            route_slots(s - 5, 1 - par)
                            row_low(s - 5, 1 - par)
                        if active(s, 2):
                            projection(s, s - 2)
                        if active(s, 3):
                            make_shift(2, s - 3, 3 - par)
                        if active(s, -2):
                            make_shift(0, s + 2, 0)
                        if isinstance(s, int) and s == STEPS - 2:
                            nc.vector.tensor_copy(end_i[:, :], end).then_inc(s_list, 1)
                    for n in tiles_in(s, t):
                        tile_step(n, n // 8, n % 8)
                        if n == IN_STEPS + AHEAD_OF_LIST - 1:
                            list_tiles()
                if isinstance(s, int) and s == -2:
                    constants_1()
                if isinstance(s, int) and s == 1:
                    constants_2()

            def tile_step(n, i, q, kind=None):
                kind0, kind2 = kind_of(n, kind), kind_of(n - 2, kind)
                par = q % 2
                if kind2 == "expert":
                    if q == 0:
                        rounds.read(i - (X_FROM // 8 + 1), "last")
                    if q == 2:
                        rounds.read(i - X_FROM // 8, "this")
                    e = rounds.expert("this", q - 2) if q > 1 else rounds.expert("last", q + 6)
                for b in range(2):
                    half_ = slice(2 * b, 2 * b + 2)
                    if kind0 in ("early", "expert"):
                        if kind0 == "expert":
                            dve.wait_ge(s_hid, n * 4 + (2 * b + 2))
                        if b == 0 and later(n, 4):
                            dve.wait_ge(s_y, n - 3)
                        if kind0 == "expert":
                            nc.vector.tensor_copy(hid_h[:, q % 4, half_, :], hid[:, par, half_, :]).then_inc(s_hh, 1)
                            dve.wait_ge(s_hh, n * 2 + (b + 1 - 2 * X_FROM))
                        else:
                            dve.wait_ge(s_hs, n * 2 + (b + 1))
                        nc.vector.tensor_tensor(hid_l[:, q % 4, half_, :], hid[:, par, half_, :],
                                                hid_h[:, q % 4, half_, :],
                                                ALU.subtract).then_inc(s_hl[b], 1)
                if kind2 == "expert":
                    j = n - (2 + X_FROM)
                    dve.wait_ge(s_y, n - 1)
                    if later(j, 4):
                        dve.wait_ge(s_back[(q - 2) % 4], i * 64 + ((q - 2 - X_FROM) // 4) * 32)
                    nc.vector.tensor_tensor(y[:, (q - 2) % 4, :, :], ps_y[:, par, :, :],
                                            b2_rows[:, bass.ds(e, 1), :].broadcast_to([P, 2, P]),
                                            ALU.add).then_inc(s_yc, 1)
                elif kind2:
                    tile = n - 2 if kind2 == "early" else n - (2 + TILES)
                    dve.wait_ge(s_y, n - 1)
                    nc.vector.tensor_tensor(x_all[:, bass.ds(tile * 2, 2), :],
                                            ps_y[:, 0 if kind2 == "early" and n - 2 < IN_STEPS else par, :, :],
                                            x_all[:, bass.ds(tile * 2, 2), :], ALU.add).then_inc(s_yc, 1)
                if isinstance(n, int):
                    ready = {L_FROM + 3: (0, 3), T_END - 4: (19, 21), T_END - 3: (21, 23), T_END - 2: (23, 25),
                             T_END - 1: (25, 27), T_END: (27, 30), T_END + 1: (30, 32)}
                    for j in range(*ready.get(n, (0, 0))):
                        finish(j, j // YG, j % YG)
                elif kind == "shared":
                    first_i = (L_FROM + 4) // 4
                    for u in (2 * q + 3, 2 * q + 4):
                        finish(i * 8 + (u - 8 * first_i), i * 2 + (u // 4 - 2 * first_i), u % 4)

            def finish(j, r, q):
                dve.wait_ge(s_yg[q], r * 16 + 16)
                dve.wait_ge(s_yc, j + 1 if isinstance(j, int) and j < EARLY else j + (TILES + 1))
                for a in range(2):
                    nc.vector.scalar_tensor_tensor(part[:, q, a, :], yg[:, q, a, 0:P],
                                                   weight1[:, bass.ds(j * 2 + a, 1)], tile_of(j * 2 + a),
                                                   ALU.mult, ALU.add).then_inc(s_part, 1)
                if later(r, 1):
                    dve.wait_ge(s_out[q], r * 16)
                for a in range(2):
                    dve.wait_ge(s_part, j * 2 + (a + 1))
                    last = nc.vector.scalar_tensor_tensor(res[:, q, a, :], yg[:, q, a, P:2 * P],
                                                          weight2[:, bass.ds(j * 2 + a, 1)], part[:, q, a, :],
                                                          ALU.mult, ALU.add)
                last.then_inc(s_res, 1)

            rounds = ExpertsOfRounds(dve)
            steps(dve, step)

            dve.wait_ge(s_soft, 1)
            own(nc.vector.tensor_scalar(weight1[:, :], weight2[:, :], 1.0, None, ALU.add))
            own(nc.vector.reciprocal(weight1[:, :], weight1[:, :]))
            own(nc.vector.tensor_tensor(weight2[:, :], weight2[:, :], weight1[:, :], ALU.mult))
            dve.wait_ge(s_list, 3)
            tiles(dve, tile_step)

        @block.tensor
        def _(pe):
            pe.wait_ge(s_c1, 9 * 16)
            pe.wait_ge(s_pool_c, 22)
            nc.tensor.transpose(ps_m[:, 0:NB + 3], bias_rows[:, :], ident[0:NB + 3, 0:NB + 3]).then_inc(s_pe_c, 1)
            pe.wait_ge(s_act_c, 1)

            M_USERS = [(s_kc, 0), (s_oTc, 2), (s_xTc, -1), (s_xh, 4)]
            N_USERS = [(s_qc, 0), (s_vc, 0), (s_projc, 2)]

            def wait_free(users, s, at):
                for back in range(len(users)):
                    at -= 1
                    earlier = 1 if at < 0 else 0
                    sem_, lag = users[at]
                    if not isinstance(s, int):
                        pe.wait_ge(sem_, s - (lag + earlier - 1))
                        return
                    if active(s - earlier, lag):
                        pe.wait_ge(sem_, s - (lag + earlier - 1))
                        return

            def transpose_x(s):
                g = s + 1
                pe.wait_ge(s_xn, g + 1)
                wait_free(M_USERS, s, 2)
                for t in range(TG):
                    last = nc.tensor.transpose(ps_m[:, t * P:(t + 1) * P], xn[:, t * P:(t + 1) * P], ident[:, :])
                last.then_inc(s_xT, 1)

            def project_kq(s):
                pe.wait_ge(s_xTc, s + 1)
                wait_free(M_USERS, s, 0)
                nc.tensor.matmul(ps_m[:, :], w_k[:, :], xnT[:, :], start=True, stop=True).then_inc(s_k, 1)
                if isinstance(s, int) and s == 2:
                    pe.wait_ge(s_crow, 1)
                wait_free(N_USERS, s, 0)
                nc.tensor.matmul(ps_n[:, :], w_q[:, :], xnT[:, :], start=True, stop=True).then_inc(s_q, 1)

            def project_v(s):
                wait_free(N_USERS, s, 1)
                for t in range(TG):
                    last = nc.tensor.matmul(ps_n[:, t * P:(t + 1) * P], xnT[:, t * P:(t + 1) * P], w_v[:, :],
                                            start=True, stop=True)
                last.then_inc(s_v, 1)

            def scores(k, half, par, t, q):
                if t == 0:
                    pe.wait_ge(s_kz[par], half * 64 + 64)
                if later(k, 2):
                    pe.wait_ge(s_exp, k - 1)
                nc.tensor.matmul(ps_s[:, q, :, :], ident_h[:, :], mask_h[:, None, :].broadcast_to([P, HEADS, P]),
                                 start=True, stop=False)
                nc.tensor.matmul(ps_s[:, q, :, :], qT[:, par, t * P:(t + 1) * P], k_wide[:, par, t, :, :],
                                 start=False, stop=True).then_inc(s_score, 1)

            def transpose_probs(k, q):
                pe.wait_ge(s_exp, k + 1)
                if later(k, 1):
                    pe.wait_ge(s_pTc, k)
                for h in range(HEADS):
                    last = nc.tensor.transpose(ps_pT[:, h * P:(h + 1) * P], probs[:, q, h, :], ident[:, :])
                last.then_inc(s_pT, 1)

            def attend(k, g, par, t):
                pe.wait_ge(s_pTc, k + 1)
                if t == 0:
                    pe.wait_ge(s_vc, g + 1)
                if later(k, 2):
                    pe.wait_ge(s_attn, k - 1)
                for h in range(HEADS):
                    last = nc.tensor.matmul(ps_av[:, t % 2, h, :], probsT[:, t % 2, h * P:(h + 1) * P],
                                            v1[:, par, t, h, :], start=True, stop=True)
                last.then_inc(s_av, 1)

            def transpose_attn(s, par):
                pe.wait_ge(s_attn, s * TG - TG)
                wait_free(M_USERS, s, 1)
                for t in range(TG):
                    last = nc.tensor.transpose(ps_m[:, t * P:(t + 1) * P], attn[:, par, t, :], ident[:, :])
                last.then_inc(s_oT, 1)

            def project_out(s):
                pe.wait_ge(s_oTc, s - 1)
                wait_free(N_USERS, s, 2)
                for t in range(TG):
                    last = nc.tensor.matmul(ps_n[:, t * P:(t + 1) * P], attnT[:, t * P:(t + 1) * P], w_o[:, :],
                                            start=True, stop=True)
                last.then_inc(s_proj, 1)

            def count_before(g):
                pe.wait_ge(s_chosen, g * 2 + 2)
                for t in range(TG):
                    nc.tensor.matmul(ps_before[:, t, :], before[:, :], chosen[:, t, :], start=True, stop=t == 0)
                    for u in range(t):
                        nc.tensor.matmul(ps_before[:, t, :], ones_h[:, :], chosen[:, u, :], start=False,
                                         stop=u == t - 1)
                for t in range(TG):
                    last = nc.tensor.matmul(ps_total, ones_h[:, :], chosen[:, t, :], start=t == 0, stop=t == TG - 1)
                last.then_inc(s_before, 1)

            def transpose_x1(s, par):
                pe.wait_ge(s_x2n, s - 3)
                wait_free(M_USERS, s, 3)
                for t in range(TG):
                    last = nc.tensor.transpose(ps_m[:, t * P:(t + 1) * P], x2n[:, par, t, :], ident[:, :])
                last.then_inc(s_x2T, 1)

            def router(g):
                pe.wait_ge(s_x2Tc, g + 1)
                if later(g, 1):
                    pe.wait_ge(s_place, g * 5)
                for t in range(TG):
                    last = nc.tensor.matmul(ps_logit[:, t, :], x2T[:, t * P:(t + 1) * P], w_r[:, :],
                                            start=True, stop=True)
                last.then_inc(s_logit, 1)

            def step(s, half, par):
                for t in range(TG):
                    k = graph(s, t)
                    if k is not None:
                        transpose_probs(k, t % 2)
                    if graph(s, t, 2) is not None:
                        if t < 2:
                            scores(graph(s, t, 2), None, 1 - par, t + 2, t % 2)
                        else:
                            if isinstance(s, int) and s == 0:
                                pe.wait_ge(s_cast_c, 2)
                            scores(graph(s, t, 2), half(0), par, t - 2, t % 2)
                    if t == 0:
                        if active(s, 5):
                            router(s - 5)
                        if active(s, 0):
                            project_kq(s)
                    if t == 1:
                        if active(s, 0):
                            project_v(s)
                        if active(s, 2):
                            transpose_attn(s, par)
                    if t == 2:
                        if active(s, 5):
                            count_before(s - 5)
                        if active(s, 2):
                            project_out(s)
                        if active(s, -1):
                            transpose_x(s)
                    if t == 3 and active(s, 4):
                        transpose_x1(s, par)
                    if k is not None:
                        attend(k, s - 1, 1 - par, t)
                    for n in tiles_in(s, t):
                        tile_step(n, n // 8, n % 8)
                if isinstance(s, int) and s == 1:
                    pe.wait_ge(s_c2, 7 * 16)
                    pe.wait_ge(s_cast_c, 7)
                    pe.wait_ge(s_vc, 2)
                    nc.tensor.matmul(ps_n[:, 0:P], bv_wide[:, :], w_o[:, :], start=True, stop=True).then_inc(s_pe_c, 1)

            def slots_T(j, landed, q):
                pe.wait_ge(s_xg[q], landed)
                if later(j, 2):
                    pe.wait_ge(s_gTc, j - 1)
                for hl in range(2):
                    for a in range(2):
                        last = nc.tensor.transpose(ps_xT[q % 2][:, hl, a * P:(a + 1) * P],
                                                   xg[:, q, a, hl * P:(hl + 1) * P], ident_h[:, :])
                last.then_inc(s_gT, 1)

            def shared_w(w, k):
                return w[:, E * FC * 2 + k, :]

            rounds = ExpertsOfRounds(pe)

            def expert_weights(e):
                def w_at(w, k):
                    by_expert = w[:, :, :].rearrange("p (e k) d -> p e k d", k=2 * FC)
                    return by_expert[:, bass.ds(e, 1), k, :].rearrange("p a d -> p (a d)")
                return w_at

            def first_layer(n, par, w_at, hi, lo, then):
                for c in range(FC):
                    if c % 2 == 0 and later(n, 2):
                        pe.wait_ge(s_hid, n * FC + (c + 2 - 2 * FC))
                    dst = ps_h[:, par, c, :]
                    nc.tensor.matmul(dst, w_at(w1, 2 * c), hi, start=True, stop=False)
                    nc.tensor.matmul(dst, w_at(w1, 2 * c), lo, start=False, stop=False)
                    last = nc.tensor.matmul(dst, w_at(w1, 2 * c + 1), hi, start=False, stop=True)
                    if c % 2:
                        last.then_inc(s_h, 1)
                    if c == 2:
                        then()

            def second_layer(m, q, w_at):
                in_steps = isinstance(m, int) and m < IN_STEPS
                if isinstance(m, int) and 1 <= m <= IN_STEPS:
                    pe.wait_ge(s_yc, m)
                elif later(m, IN_STEPS + 1):
                    pe.wait_ge(s_yc, m - 1)
                if isinstance(m, int) and m == IN_STEPS + 1:
                    pe.wait_ge(s_place, GROUPS * 5)
                pe.wait_ge(s_hl[0], m + 1)
                weights = [(w_at(w2, 2 * c), w_at(w2, 2 * c + 1)) for c in range(FC)]
                for a in range(2):
                    cols = slice(a * P, (a + 1) * P)
                    for c, (high, low) in enumerate(weights):
                        if a == 0 and c == 2:
                            pe.wait_ge(s_hl[1], m + 1)
                        dst = ps_y[:, 0 if in_steps else q % 2, a, :]
                        nc.tensor.matmul(dst, hid_h[:, q, c, cols], high, start=c == 0, stop=False)
                        nc.tensor.matmul(dst, hid_l[:, q, c, cols], high, start=False, stop=False)
                        last = nc.tensor.matmul(dst, hid_h[:, q, c, cols], low, start=False, stop=c == FC - 1)
                last.then_inc(s_y, 1)

            def tile_step(n, i, q, kind=None):
                kind0, kind1, kind2 = kind_of(n, kind), kind_of(n + 1, kind), kind_of(n - 2, kind)
                if kind0 == "expert" and isinstance(n, int) and n == X_FROM:
                    pe.wait_ge(s_list, 3)
                in_loop = not isinstance(n, int)
                if q == 0 and kind0 == "expert" and not in_loop:
                    rounds.read(i - X_FROM // 8, "this")
                if kind2 == "expert" and q > 1:
                    e2 = rounds.expert("this", q - 2)
                elif kind2 == "expert" and (in_loop or q == 1):
                    e2 = rounds.expert("last", q + 6)

                def read_registers():
                    if in_loop and kind == "expert" and q == 6:
                        rounds.read_into("last", i - X_FROM // 8)
                    if in_loop and kind == "expert" and q == 7:
                        rounds.read_into("this", i - (X_FROM // 8 - 1))
                    if not in_loop and q == 0 and kind2 == "expert":
                        rounds.read(i - (X_FROM // 8 + 1), "last")

                if isinstance(n, int) and n == 0:
                    pe.wait_ge(s_exp, B)
                    pe.wait_ge(s_pTc, B)
                    pe.wait_ge(s_attn, B)
                    pe.wait_ge(s_wl, UNITS)
                if isinstance(n, int) and n == X_FROM:
                    pe.wait_ge(s_xh, GROUPS)
                    pe.wait_ge(s_projc, GROUPS)
                    slots_T(0, 16, 0)
                if kind1 == "expert" and later(n, X_FROM):
                    slots_T(n - (X_FROM - 1), i * 16 + ((q + 1) // 8 - X_FROM // 8 + 1) * 16, (q + 1) % 8)
                if kind0 == "expert":
                    w_at = expert_weights(rounds.expert("this", q))
                    pe.wait_ge(s_gTc, n - (X_FROM - 1))
                    first_layer(n, q % 2, w_at, xgT[:, q % 2, 0, :], xgT[:, q % 2, 1, :], read_registers)
                elif kind0:
                    if kind0 == "early" and n % 2 == 0:
                        pe.wait_ge(s_xl, n // 2 + 1)
                    if isinstance(n, int) and n == L_FROM:
                        pe.wait_ge(s_xl, GROUPS)
                    tile = n if kind0 == "early" else n - TILES
                    cols = bass.ds(tile * ST, ST)
                    first_layer(n, q % 2, shared_w, xh_all[:, cols], xl_all[:, cols], read_registers)
                if kind2 == "expert":
                    if q == 0 and not in_loop:
                        e2 = rounds.expert("last", 6)
                    second_layer(n - 2, (q - 2) % 4, expert_weights(e2))
                elif kind2:
                    second_layer(n - 2, (q - 2) % 4, shared_w)

            steps(pe, step)
            def before_loop(i):
                rounds.hold("last", i - (X_FROM // 8 + 1))
                rounds.hold("this", i - X_FROM // 8)

            tiles(pe, tile_step, before_loop)


NAMES = ["x", "adj", "L0_gnn_Wq", "L0_gnn_bq", "L0_gnn_Wk", "L0_gnn_bk", "L0_gnn_Wv", "L0_gnn_bv", "L0_gnn_Wo",
         "L0_gnn_bo", "L0_gnn_gamma", "L0_gnn_beta", "L0_ffn_Wr", "L0_ffn_W1s", "L0_ffn_b1s", "L0_ffn_W2s",
         "L0_ffn_b2s", "L0_ffn_W1p", "L0_ffn_b1p", "L0_ffn_W2p", "L0_ffn_b2p"]


def kernel(**inputs):
    import numpy as np
    import concourse.bacc as bacc
    from concourse.bass_utils import run_bass_kernel_spmd

    nc = bacc.Bacc("TRN2", target_bir_lowering=False, num_devices=1)
    arrays, args = {}, []
    for name in NAMES:
        a = np.ascontiguousarray(inputs[name])
        arrays["in_" + name] = a
        args.append(nc.dram_tensor("in_" + name, a.shape, mybir.dt.from_np(a.dtype), kind="ExternalInput").ap())
    result = nc.dram_tensor("result", arrays["in_x"].shape, F32, kind="ExternalOutput").ap()
    build_program(nc, *args, result)
    return run_bass_kernel_spmd(nc, [arrays], core_ids=[0]).results[0]["result"]
```
